# Optimizing a Trainium2 kernel written in Bass

```python
import numpy as np
import jax
import jax.numpy as jnp

def _softmax(x, axis=-1):
    return jax.nn.softmax(x, axis=axis)

def _gelu(x):
    return jax.nn.gelu(x, approximate=True)

def _silu(x):
    return jax.nn.silu(x)

def _sigmoid(x):
    return jax.nn.sigmoid(x)

def _layernorm(x, axis=-1, eps=1e-05):
    m = jnp.mean(x, axis=axis, keepdims=True)
    v = jnp.var(x, axis=axis, keepdims=True)
    return (x - m) / jnp.sqrt(v + eps)

def _scatter_add(tgt, idx, src, axis=0):
    return tgt.at[idx].add(src)

def _segment_sum(src, seg, n):
    return jax.ops.segment_sum(src, seg, n)
kernel_name = 'mk_decoder_postln_d1_seqx_r4_f4fd8a'

def setup_inputs(seed: int=0):
    np.random.seed(seed)
    _w = jnp.asarray

    def _rec_inputs():
        import jax
        import jax.numpy as jnp
        _rk = jax.random.key(seed)
        x = -0.000125 + 0.9999 * jax.random.normal(jax.random.fold_in(_rk, 1), (4, 512, 512), jnp.float32)
        _lenS = 512 - jax.random.randint(jax.random.fold_in(_rk, 7), (4,), 0, max(1, 512 // 4) + 1, jnp.int32)
        _lenS2 = 512 - jax.random.randint(jax.random.fold_in(_rk, 8), (4,), 0, max(1, 512 // 4) + 1, jnp.int32)
        fside_BxS2xS2_0 = -3.05549e-07 + 0.0199987 * jax.random.normal(jax.random.fold_in(_rk, 11), (4, 512, 512), jnp.float32)
        _ctx_1024P = jax.random.normal(jax.random.fold_in(_rk, 12), (4, 16, 256), jnp.float32)
        _ctx_1024c = jax.random.dirichlet(jax.random.fold_in(_rk, 512), 0.3 * jnp.ones((16,), jnp.float32), (4, 512))
        _ctx_1024t = jnp.einsum('bsk,bkd->bsd', _ctx_1024c, _ctx_1024P)
        _ctx_1024t = _ctx_1024t * jax.lax.rsqrt(jnp.mean(jnp.square(_ctx_1024t)) + 1e-12) * 0.953939
        ctx_1024 = 6.82029e-06 + 0.0200006 * (_ctx_1024t + 0.3 * jax.random.normal(jax.random.fold_in(_rk, 612), (4, 512, 256), jnp.float32))
        return (x, fside_BxS2xS2_0, ctx_1024)
    x, fside_BxS2xS2_0, ctx_1024 = _rec_inputs()

    def _L0_attn_setup():
        import jax, jax.numpy as jnp
        import numpy as np
        import math
        HIDDEN = 512
        NUM_HEADS = 16
        HEAD_SIZE = HIDDEN // NUM_HEADS
        BATCH = 2
        SEQ = 512
        key = jax.random.key(seed)
        k_x, k_wq, k_bq, k_wo, k_bo = jax.random.split(key, 5)
        scale_in = 1.0 / math.sqrt(HIDDEN)
        return {'x': jax.random.normal(k_x, (BATCH, SEQ, HIDDEN), dtype=jnp.float32), 'Wqkv': jax.random.normal(k_wq, (HIDDEN, 3 * HIDDEN), dtype=jnp.float32) * scale_in, 'bqkv': jax.random.normal(k_bq, (3 * HIDDEN,), dtype=jnp.float32) * 0.01, 'Wo': jax.random.normal(k_wo, (HIDDEN, HIDDEN), dtype=jnp.float32) * scale_in, 'bo': jax.random.normal(k_bo, (HIDDEN,), dtype=jnp.float32) * 0.01}
    _L0_attn_all = _L0_attn_setup()
    _L0_attn_in = {k: v for k, v in _L0_attn_all.items() if k in ('Wqkv', 'bqkv', 'Wo', 'bo')}
    del _L0_attn_all

    def _L0_xattn_setup():
        import jax, jax.numpy as jnp
        import numpy as np
        EPS = 1e-06
        QMAX = 127.0

        def _smooth_quant_linear(x, w):
            amax_x = jnp.max(jnp.abs(x), axis=0)
            amax_w = jnp.max(jnp.abs(w), axis=0)
            s = jnp.sqrt(jnp.maximum(amax_x, EPS) / jnp.maximum(amax_w, EPS))
            s = jnp.maximum(s, EPS)
            xs = x / s
            ws = w * s
            x_scale = jnp.maximum(jnp.max(jnp.abs(xs), axis=-1, keepdims=True), EPS) / QMAX
            w_scale = jnp.maximum(jnp.max(jnp.abs(ws), axis=-1, keepdims=True), EPS) / QMAX
            x_q = jnp.clip(jnp.round(xs / x_scale), -QMAX, QMAX)
            w_q = jnp.clip(jnp.round(ws / w_scale), -QMAX, QMAX)
            return x_q @ w_q.T * x_scale * w_scale.T

        def _expert_forward(xe, guw, dw):
            h = _smooth_quant_linear(xe, guw)
            gate, up = jnp.split(h, 2, axis=-1)
            a = jax.nn.silu(gate) * up
            return _smooth_quant_linear(a, dw)
        key = jax.random.key(seed)
        k1, k2, k3 = jax.random.split(key, 3)
        E, T, D, I = (8, 512, 512, 256)
        x = jax.random.normal(k1, (E, T, D), dtype=jnp.float32)
        gate_up_weight = jax.random.normal(k2, (E, 2 * I, D), dtype=jnp.float32) * 0.02
        down_weight = jax.random.normal(k3, (E, D, I), dtype=jnp.float32) * 0.02
        return {'x': x, 'gate_up_weight': gate_up_weight, 'down_weight': down_weight}
    _L0_xattn_all = _L0_xattn_setup()
    _L0_xattn_in = {k: v for k, v in _L0_xattn_all.items() if k in ()}
    del _L0_xattn_all

    def _L0_ffn_setup():
        import jax, jax.numpy as jnp
        import numpy as np
        DIM = 512
        INTER = 352
        E = 16
        TOPK = 4
        G = 4
        TOPK_G = 2
        N_SHARED = 2
        ROUTE_SCALE = 1.0
        INIT_STD = 0.02
        B, S = (1, 512)
        key = jax.random.key(seed)
        ks = jax.random.split(key, 9)
        std = INIT_STD
        x = jax.random.normal(ks[0], (B, S, DIM), jnp.float32)
        gate_w = jax.random.normal(ks[1], (E, DIM), jnp.float32) * std
        expert_bias = jnp.zeros((E,), jnp.float32)
        w1 = jax.random.normal(ks[2], (E, DIM, INTER), jnp.float32) * std
        w3 = jax.random.normal(ks[3], (E, DIM, INTER), jnp.float32) * std
        w2 = jax.random.normal(ks[4], (E, INTER, DIM), jnp.float32) * std
        sh = N_SHARED * INTER
        sw1 = jax.random.normal(ks[5], (DIM, sh), jnp.float32) * std
        sw3 = jax.random.normal(ks[6], (DIM, sh), jnp.float32) * std
        sw2 = jax.random.normal(ks[7], (sh, DIM), jnp.float32) * std
        return {'x': x, 'gate_w': gate_w, 'expert_bias': expert_bias, 'w1': w1, 'w2': w2, 'w3': w3, 'sw1': sw1, 'sw2': sw2, 'sw3': sw3}
    _L0_ffn_all = _L0_ffn_setup()
    _L0_ffn_in = {k: v for k, v in _L0_ffn_all.items() if k in ('gate_w', 'expert_bias', 'w1', 'w2', 'w3', 'sw1', 'sw2', 'sw3')}
    del _L0_ffn_all
    return {'x': x, 'fside_BxS2xS2_0': fside_BxS2xS2_0, 'ctx_1024': ctx_1024, 'L0_attn_Wqkv': _L0_attn_in['Wqkv'], 'L0_attn_bqkv': _L0_attn_in['bqkv'], 'L0_attn_Wo': _L0_attn_in['Wo'], 'L0_attn_bo': _L0_attn_in['bo'], 'L0_ffn_gate_w': _L0_ffn_in['gate_w'], 'L0_ffn_expert_bias': _L0_ffn_in['expert_bias'], 'L0_ffn_w1': _L0_ffn_in['w1'], 'L0_ffn_w2': _L0_ffn_in['w2'], 'L0_ffn_w3': _L0_ffn_in['w3'], 'L0_ffn_sw1': _L0_ffn_in['sw1'], 'L0_ffn_sw2': _L0_ffn_in['sw2'], 'L0_ffn_sw3': _L0_ffn_in['sw3']}

def reference(x, fside_BxS2xS2_0, ctx_1024, L0_attn_Wqkv, L0_attn_bqkv, L0_attn_Wo, L0_attn_bo, L0_ffn_gate_w, L0_ffn_expert_bias, L0_ffn_w1, L0_ffn_w2, L0_ffn_w3, L0_ffn_sw1, L0_ffn_sw2, L0_ffn_sw3):
    import jax
    import jax.numpy as jnp

    def _L0_attn_ref(x, Wqkv, bqkv, Wo, bo):
        import jax, jax.numpy as jnp
        import numpy as np
        import math
        HIDDEN = 512
        NUM_HEADS = 16
        HEAD_SIZE = HIDDEN // NUM_HEADS
        BATCH = 2
        SEQ = 512
        b, s, _ = x.shape
        kqv = x @ Wqkv + bqkv
        kqv = kqv.reshape(b, s, 3, NUM_HEADS, HEAD_SIZE)
        q = kqv[:, :, 0]
        k = kqv[:, :, 1]
        v = kqv[:, :, 2]
        scores = jnp.einsum('bsnh,btnh->bnst', k, q) / math.sqrt(HEAD_SIZE)
        ones = jnp.ones_like(scores)
        scores = jnp.triu(scores) + -10000.0 * jnp.tril(ones, k=-1)
        attn = jax.nn.softmax(scores, axis=2)
        out = jnp.einsum('bnkq,bknh->bqnh', attn, v)
        out = out.reshape(b, s, NUM_HEADS * HEAD_SIZE)
        return out @ Wo + bo

    def _L0_xattn_ref(x, gate_up_weight, down_weight):
        import jax, jax.numpy as jnp
        import numpy as np
        EPS = 1e-06
        QMAX = 127.0

        def _smooth_quant_linear(x, w):
            amax_x = jnp.max(jnp.abs(x), axis=0)
            amax_w = jnp.max(jnp.abs(w), axis=0)
            s = jnp.sqrt(jnp.maximum(amax_x, EPS) / jnp.maximum(amax_w, EPS))
            s = jnp.maximum(s, EPS)
            xs = x / s
            ws = w * s
            x_scale = jnp.maximum(jnp.max(jnp.abs(xs), axis=-1, keepdims=True), EPS) / QMAX
            w_scale = jnp.maximum(jnp.max(jnp.abs(ws), axis=-1, keepdims=True), EPS) / QMAX
            x_q = jnp.clip(jnp.round(xs / x_scale), -QMAX, QMAX)
            w_q = jnp.clip(jnp.round(ws / w_scale), -QMAX, QMAX)
            return x_q @ w_q.T * x_scale * w_scale.T

        def _expert_forward(xe, guw, dw):
            h = _smooth_quant_linear(xe, guw)
            gate, up = jnp.split(h, 2, axis=-1)
            a = jax.nn.silu(gate) * up
            return _smooth_quant_linear(a, dw)
        return jax.vmap(_expert_forward)(x, gate_up_weight, down_weight)

    def _L0_ffn_ref(x, gate_w, expert_bias, w1, w2, w3, sw1, sw2, sw3):
        import jax, jax.numpy as jnp
        import numpy as np
        DIM = 512
        INTER = 352
        E = 16
        TOPK = 4
        G = 4
        TOPK_G = 2
        N_SHARED = 2
        ROUTE_SCALE = 1.0
        INIT_STD = 0.02
        B, S = (1, 512)
        b, s, d = x.shape
        T = b * s
        xf = x.reshape(T, d)
        scores = jax.nn.sigmoid(xf @ gate_w.T)
        original_scores = scores
        scores = scores + expert_bias
        sg = scores.reshape(T, G, E // G)
        group_scores = sg.max(axis=-1)
        _, gidx = jax.lax.top_k(group_scores, TOPK_G)
        gmask = jnp.zeros((T, G), bool).at[jnp.arange(T)[:, None], gidx].set(True)
        masked = jnp.where(gmask[:, :, None], sg, -jnp.inf).reshape(T, E)
        _, idx = jax.lax.top_k(masked, TOPK)
        w = jnp.take_along_axis(original_scores, idx, axis=1)
        w = w / jnp.sum(w, axis=-1, keepdims=True)
        w = w * ROUTE_SCALE
        cw = jnp.zeros((T, E), x.dtype).at[jnp.arange(T)[:, None], idx].add(w)
        h = jax.nn.silu(jnp.einsum('td,edh->teh', xf, w1)) * jnp.einsum('td,edh->teh', xf, w3)
        y = jnp.einsum('teh,ehd,te->td', h, w2, cw)
        z = jax.nn.silu(xf @ sw1) * (xf @ sw3) @ sw2
        return (y + z).reshape(b, s, d)
    x = _layernorm(x + _L0_attn_ref(x, L0_attn_Wqkv, L0_attn_bqkv, L0_attn_Wo, L0_attn_bo), axis=-1)
    x = _layernorm(x + _L0_xattn_ref(x, fside_BxS2xS2_0, ctx_1024), axis=-1)
    x = _layernorm(x + _L0_ffn_ref(x, L0_ffn_gate_w, L0_ffn_expert_bias, L0_ffn_w1, L0_ffn_w2, L0_ffn_w3, L0_ffn_sw1, L0_ffn_sw2, L0_ffn_sw3), axis=-1)
    return x

_drawn_inputs = setup_inputs


def setup_inputs(seed=0):
    import zlib

    import numpy as np

    out = dict(_drawn_inputs(seed))
    spreads = {'L0_ffn_expert_bias': (0.0, 0.412)}
    factors = {'L0_attn_bqkv': 5.641,
     'L0_attn_bo': 5.748,
     'L0_ffn_gate_w': 3.819,
     'L0_ffn_w1': 2.806,
     'L0_ffn_w2': 2.749,
     'L0_ffn_w3': 2.748}
    for name, (base, spread) in spreads.items():
        noise = np.random.default_rng([zlib.crc32(name.encode()), seed]).standard_normal(out[name].shape)
        drawn = base * np.exp(spread * noise) if base else spread * noise
        out[name] = jnp.asarray(drawn.astype(out[name].dtype))
    for name, factor in factors.items():
        out[name] = (out[name] * factor).astype(out[name].dtype)
    return out
```

```python
from contextlib import ExitStack

import concourse.bass as bass
from concourse import mybir

F32 = mybir.dt.float32
F32R = mybir.dt.float32r
BF16 = mybir.dt.bfloat16
I32 = mybir.dt.int32
U32 = mybir.dt.uint32
ALU = mybir.AluOpType
ACT = mybir.ActivationFunctionType
AX = mybir.AxisListType

P = 128
HEADS = 16
HD = 32
LN_EPS = 1e-5
Q_EPS = 1e-6
QMAX = 127.0
ROUND = 12582912.0
NEG = -1e30
BIG = 1e30
NR = 2
TOPK = 4


def decoder_layer(nc, x, fside, ctxw, Wqkv, bqkv, Wo, bo, gate_w, ebias, w1, w2, w3, sw1, sw2, sw3, out, dbg=None):
    B, S, D = x.shape
    C = D // P
    ST = S // P
    I2 = ctxw.shape[2]
    C2 = I2 // P
    E, _, F = w1.shape
    NT = B * ST
    T = B * S
    KF = [(k * P, min(P, F - k * P)) for k in range((F + P - 1) // P)]
    SH = sw1.shape[1] // F
    SCALE = float(HD) ** -0.5
    PW = ST * S - P * ST * (ST - 1) // 2
    RT = (TOPK * T + (P - 1) * E) // P
    RT += RT % 2
    JT = RT + SH * NT
    assert D == 512 and S == 512 and HEADS * HD == D and I2 == 256 and sw1.shape[1] == SH * F

    x2_d = nc.dram_tensor("x2_d", [T, D], F32).ap()
    slot_d = nc.dram_tensor("slot_d", [RT * P, 1], F32).ap()
    YPAD = TOPK * T
    YSH = YPAD + RT * P
    y_d = nc.dram_tensor("y_d", [YSH + SH * T, D], F32).ap()

    with ExitStack() as ctx:
        def sb(name, shape, dt=F32, stack=ctx):
            return stack.enter_context(nc.sbuf_tensor(name, shape, dt))

        def sem(name):
            return ctx.enter_context(nc.semaphore(name))

        ident = sb("ident", [P, P])
        identb = sb("identb", [P, P], BF16)
        ones = sb("ones", [P, P])
        mask_qk = sb("mask_qk", [P, P], BF16)
        mask_kq = sb("mask_kq", [P, P], BF16)
        onehot = sb("onehot", [P, HEADS, 32])
        sel = sb("sel", [HEADS, D])
        tri16 = sb("tri16", [P, E, E])
        tri4 = sb("tri4", [P, 4, 4])
        upper = sb("upper", [P, P])
        k128 = sb("k128", [P, E, NT])
        jrow = sb("jrow", [P, RT, E])
        krow = sb("krow", [P, TOPK, E])
        halfp = sb("halfp", [P, 8])
        halfn = sb("halfn", [P, 8])
        tokf = sb("tokf", [P, NT, TOPK])
        padf = sb("padf", [RT, P])
        logits = sb("logits", [P, NT * E])
        ebias_bc = sb("ebias_bc", [P, E])

        psA = ctx.enter_context(ExitStack())
        psST = psA.enter_context(nc.psum_tensor("psST", [P, 3 * 512], F32))
        psR = [psA.enter_context(nc.psum_tensor(f"psR{i}", [P, 512], F32)) for i in range(NR)]
        psOT = psA.enter_context(nc.psum_tensor("psOT", [P, 512], F32))
        psDEN = psA.enter_context(nc.psum_tensor("psDEN", [P, 512], F32))
        psX = psA.enter_context(nc.psum_tensor("psX", [P, 512], F32))

        s_const = sem("s_const")
        s_pool_fill = sem("s_pool_fill")
        s_wload = sem("s_wload")
        s_x = sem("s_x")
        s_xr = sem("s_xr")
        s_bw = sem("s_bw")
        s_rfull = sem("s_rfull")
        s_rfree = sem("s_rfree")
        s_dve = sem("s_dve")
        s_apart = sem("s_apart")
        s_gw = sem("s_gw")
        s_gwT = sem("s_gwT")
        s_rden = sem("s_rden")
        s_qin = sem("s_qin")
        s_diag = sem("s_diag")
        s_quant = sem("s_quant")
        s_qkhi = sem("s_qkhi")
        s_stk = [sem(f"s_stk{g}") for g in range(C)]
        s_mrow = [sem(f"s_mrow{g}") for g in range(C)]
        s_st = sem("s_st")
        s_exp = sem("s_exp")
        s_pv = sem("s_pv")
        s_ot = sem("s_ot")
        s_xrb = sem("s_xrb")
        s_powin = sem("s_powin")
        s_pow = sem("s_pow")
        s_silu = sem("s_silu")
        s_x2 = sem("s_x2")
        s_x2st = sem("s_x2st")

        NTICK = 4 + 8 + 4 + 64 + 4 + 4 + 4 + (C + C + 2 + C + C + 1 + ST) + (C2 + C2 + 2 + C2 + C2 + 1 + ST) + C + 2
        assert NTICK % NR == 0
        TICK_H1 = NTICK - (C2 + C2 + 2 + C2 + C2 + 1 + ST) - C - 2
        NSTEP = 4 + 2 * 11 + 2 * 23 + 2 * C + 2 * C2 + 1

        ATTN = []
        for h in range(8):
            ATTN += [("max", h)] + [("rows", 0)] * (h == 4)
        for h in range(HEADS):
            ATTN += [("max", h + 8)] * (h + 8 < HEADS)
            ATTN += [("rows", h // 4 + 1)] * (h % 4 == 0 and h // 4 + 1 < C)
            ATTN += [("scores", h)] + [("weigh", h - 1)] * (h > 0)
        ATTN += [("weigh", HEADS - 1)]
        ROWS_TICK, at = {}, C + 2 * C + ST
        for what, h in ATTN:
            if what == "rows":
                ROWS_TICK[h] = at
            at += {"max": ST, "rows": 1}.get(what, 0)

        stA = ctx.enter_context(ExitStack())

        def sa(name, shape, dt=F32):
            return sb(name, shape, dt, stA)

        xq_shape = [P, ST, D]
        wqkv = sa("wqkv", [P, C, 3 * D])
        wo_s = sa("wo_s", [P, C, D])
        bqk = sa("bqk", [P, 2 * C])
        bv_bc = sa("bv_bc", [P, D])
        bo_bc = sa("bo_bc", [P, D])
        gw = sa("gw", [E, D])
        gwT = sa("gwT", [P, C, E])
        xt = sa("xt", [P, ST, D])
        xr = sa("xr", [P, ST, D])
        xT = sa("xT", [P, C, S])
        v_s = sa("v_s", [P, ST, D])
        x1 = sa("x1", [P, ST, D])
        small = sa("small", [P, 64])
        amw, amx, ram, sm, rsm, wsc, rws, xsc, rxs = (sa(n, [P, 4]) for n in
                                                      ("amw", "amx", "ram", "sm", "rsm", "wsc", "rws", "xsc", "rxs"))
        bn = sa("bn", [P, ST, 6])
        mv = sa("mv", [P, ST, 2])
        otu = xT
        with ExitStack() as st1:
            qh = sb("qh", [P, 2 * C, S], F32R, st1)
            ql = sb("ql", [P, 2 * C, S], F32R, st1)
            qst = sb("qst", [P, HEADS, S], F32R, st1)
            pT = sb("pT", [P, 2, PW], F32, st1)
            kst = sb("kst", [P, HEADS, S], F32R, st1)
            nm = sb("nm", [P, HEADS, ST], F32, st1)
            nmh = sb("nmh", [4 * ST, C, P], F32R, st1)
            nml = sb("nml", [4 * ST, C, P], F32R, st1)
            rden = sb("rden", [HEADS, S], F32, st1)
        with ExitStack() as st2:
            wf = sb("wf", [P, ST, D], F32, st2)
            wc = sb("wc", [P, ST, I2], F32, st2)
            dg = sb("dg", [P, 2, D], F32, st2)
            xs = sb("xs", [P, ST, D], F32, st2)
            ws = sb("ws", [P, ST, D], F32, st2)
            xq = sb("xq", xq_shape, BF16, st2)
            wq = sb("wq", xq_shape, BF16, st2)
            xqT = sb("xqT", [P, C, S], BF16, st2)
            wqT = sb("wqT", [P, C, S], BF16, st2)
            wsc_bc = sb("wsc_bc", [P, D], F32, st2)
            h1 = sb("h1", [P, ST, D], F32, st2)
            sil = sb("sil", [P, ST, I2], F32, st2)
            a2 = sb("a2", [P, ST, I2], F32, st2)
            lgT = sb("lgT", [E, S], F32, st2)

        x_v = x.rearrange("b (i p) d -> p b i d", p=P)
        f_v = fside.rearrange("b (i p) d -> p b i d", p=P)
        c_v = ctxw.rearrange("b (i p) d -> p b i d", p=P)
        x2_v = x2_d.rearrange("(b i p) d -> p b i d", p=P, i=ST)
        wqkv_v = Wqkv.rearrange("(c p) n -> p c n", p=P)
        KOFF = [0, S, 2 * S, 2 * S - P]

        def bias_row(b, lo):
            return b[lo:lo + D].rearrange("(a n) -> a n", a=1).to_broadcast([P, D])

        def apart(eng):
            eng.sem_inc(s_apart, 1)

        blk = ExitStack()
        block = blk.enter_context(nc.Block())

        @block.sync
        def _(sp):
            sp.dma_start(wqkv[:, :, 0:D], wqkv_v[:, :, 0:D]).then_inc(s_wload, 16)
            sp.dma_start(wqkv[:, :, D:2 * D], wqkv_v[:, :, D:2 * D]).then_inc(s_wload, 16)
            sp.dma_start(wqkv[:, :, 2 * D:3 * D], wqkv_v[:, :, 2 * D:3 * D]).then_inc(s_wload, 16)
            with nc.allow_non_contiguous_dma(reason="a bias by rows, once"):
                sp.dma_start(bqk[:, :], bqkv[0:2 * D].rearrange("(c p) -> p c", p=P)).then_inc(s_wload, 16)
            sp.dma_start(bv_bc[:, :], bias_row(bqkv, 2 * D)).then_inc(s_wload, 16)
            sp.dma_start(bo_bc[:, :], bias_row(bo, 0)).then_inc(s_wload, 16)
            sp.dma_start(wo_s[:, :, :], Wo.rearrange("(c p) n -> p c n", p=P)).then_inc(s_wload, 16)
            sp.dma_start(gw[:, :], gate_w).then_inc(s_wload, 16)
            sp.dma_start(ebias_bc[:, :], ebias.rearrange("(a n) -> a n", a=1).to_broadcast([P, E])).then_inc(s_wload, 16)
            with sp.Fori(0, B) as b:
                sp.dma_start(xt[:, :, :], x_v[:, bass.ds(b, 1)]).then_inc(s_x, 16)
                sp.dma_start(xr[:, :, :], x_v[:, bass.ds(b, 1)]).then_inc(s_xr, 16)
                for g in range(C):
                    for m, stack, parts in ((g, qst, "hlh"), (C + g, kst, "hhl")):
                        n = 2 * g + (m >= C)
                        sp.wait_ge(s_rfree, NR + b * NTICK + C + n + 1)
                        for k, part in enumerate(parts):
                            src = qh if part == "h" else ql
                            for j in range(4):
                                sp.dma_start(stack[HD * k:HD * (k + 1), 4 * g + j, :].bitcast(F32),
                                             src[HD * j:HD * (j + 1), m, :].bitcast(F32)).then_inc(s_stk[g], 16)
                for g in range(C):
                    sp.wait_ge(s_rfree, NR + b * NTICK + ROWS_TICK[g] + 1)
                    sp.dma_start(qst[96:97, 4 * g:4 * g + 4, :].bitcast(F32), nmh[:, g, :].bitcast(F32)).then_inc(s_mrow[g], 16)
                    sp.dma_start(qst[97:98, 4 * g:4 * g + 4, :].bitcast(F32), nml[:, g, :].bitcast(F32)).then_inc(s_mrow[g], 16)
                sp.wait_ge(s_pv, b * HEADS + HEADS)
                sp.dma_start(wf[:, :, :], f_v[:, bass.ds(b, 1)]).then_inc(s_bw, 16)
                sp.dma_start(wc[:, :, :], c_v[:, bass.ds(b, 1)]).then_inc(s_bw, 16)
                sp.wait_ge(s_x2, b + 1)
                sp.dma_start(x2_v[:, bass.ds(b, 1)], x1[:, :, :]).then_inc(s_x2st, 16)
                sp.wait_ge(s_x2st, 16 * b + 16)
                apart(sp)

        @block.gpsimd
        def _(pool):
            n = [0]

            def fill(t, v):
                pool.memset(t, v).then_inc(s_pool_fill, 1)
                n[0] += 1

            def cut(t, pattern, base, mult, op, v):
                pool.affine_select(out=t, in_=t, compare_op=op, fill=v, base=base, pattern=pattern,
                                   channel_multiplier=mult).then_inc(s_const, 1)
            fill(ident[:, :], 0.0)
            fill(identb[:, :], 0.0)
            fill(ones[:, :], 1.0)
            fill(mask_qk[:, :], 0.0)
            fill(mask_kq[:, :], 0.0)
            fill(onehot[:, :, :], 0.0)
            fill(sel[:, :], 0.0)
            fill(tri16[:, :, :], 1.0)
            fill(tri4[:, :, :], 1.0)
            fill(upper[:, :], 1.0)
            fill(halfp[:, :], 0.5)
            fill(halfn[:, :], -0.5)
            pool.wait_ge(s_pool_fill, n[0])
            cut(ident[:, :], [[-1, P]], 0, 1, ALU.not_equal, 1.0)
            cut(identb[:, :], [[-1, P]], 0, 1, ALU.not_equal, 1.0)
            cut(mask_qk[:, :], [[-1, P]], 0, 1, ALU.is_ge, NEG)
            cut(mask_kq[:, :], [[1, P]], 0, -1, ALU.is_ge, NEG)
            cut(onehot[:, :, :], [[1, HEADS], [-1, 32]], 0, 0, ALU.not_equal, 1.0)
            cut(sel[:, :].rearrange("h (g r) -> h g r", r=HD), [[1, HEADS], [0, HD]], 0, -1, ALU.not_equal, 1.0)
            cut(tri16[:, :, :], [[1, E], [-1, E]], -1, 0, ALU.is_ge, 0.0)
            cut(tri4[:, :, :], [[1, 4], [-1, 4]], -1, 0, ALU.is_ge, 0.0)
            cut(upper[:, :], [[1, P]], -1, -1, ALU.is_ge, 0.0)
            for t, pat, base, mult in ((k128, [[0, E], [P, NT]], 0, 0), (jrow, [[1, RT], [0, E]], 0, 0),
                                       (krow, [[1, TOPK], [0, E]], 0, 0), (tokf, [[P, NT], [T, TOPK]], 0, 1)):
                pool.iota(t[:, :, :], pat, base=base, channel_multiplier=mult,
                          allow_small_or_imprecise_dtypes=True).then_inc(s_const, 1)
            pool.iota(padf[:, :], [[1, P]], base=TOPK * T, channel_multiplier=P,
                      allow_small_or_imprecise_dtypes=True).then_inc(s_const, 1)
            pool.wait_ge(s_wload, 16 * 9)
            with pool.Fori(0, B) as b:
                pool.wait_ge(s_xr, 16 * (b + 1))
                for i in range(ST):
                    pool.tensor_tensor(xr[:, i, :], xr[:, i, :], bo_bc[:, :], ALU.add).then_inc(s_xrb, 1)
                for k, (width, half) in enumerate(((ST, halfn), (C, halfp), (C2, halfp), (ST, halfn))):
                    pool.wait_ge(s_powin, 4 * b + k + 1)
                    pool.tensor_tensor(small[:, 8:8 + width], small[:, 0:width], half[:, 0:width],
                                       ALU.pow).then_inc(s_pow, 1)

        @block.scalar
        def _(act):
            act.wait_ge(s_wload, 16 * 9)
            with act.Fori(0, B) as b:
                for n in range(2 * C):
                    m = n // 2 + C * (n % 2)
                    act.wait_ge(s_rfull, b * NTICK + 4 + n + 1)
                    act.activation(qh[:, m, :], psR[n % NR][:, :], ACT.Identity,
                                   bias=bqk[:, m:m + 1]).then_inc(s_qkhi, 1)
                for h in range(HEADS):
                    act.wait_ge(s_st, b * HEADS + h + 1)
                    if h >= 2:
                        act.wait_ge(s_pv, b * HEADS + h - 1)
                    act.activation(pT[:, h % 2, :], psST[:, 0:PW], ACT.Exp, scale=SCALE).then_inc(s_exp, 1)
                    if h % 4 == 0 and h:
                        act.wait_ge(s_pv, b * HEADS + h)
                        act.copy(otu[:, h // 4 - 1, :], psOT[:, :]).then_inc(s_ot, 1)
                act.wait_ge(s_pv, b * HEADS + HEADS)
                act.copy(otu[:, C - 1, :], psOT[:, :]).then_inc(s_ot, 1)
                act.wait_ge(s_rfree, NR + b * NTICK + TICK_H1)
                act.activation(sil[:, :, :], h1[:, :, 0:I2], ACT.Silu).then_inc(s_silu, 1)

        @block.tensor
        def _(pe):
            tick = [0]
            MAXED = {}

            def bank(b):
                pe.wait_ge(s_rfree, b * NTICK + tick[0] + 1)
                t = psR[tick[0] % NR]
                tick[0] += 1
                return t

            def transposes(b, src, c, bf=False):
                t = bank(b)
                t = t[:, :].bitcast(BF16)[:, 0:ST * P] if bf else t[:, :]
                for i in range(ST):
                    mm = pe.transpose(t[:, i * P:(i + 1) * P], src[:, i, c * P:(c + 1) * P],
                                      (identb if bf else ident)[:, :])
                mm.then_inc(s_rfull, 1)

            def product(out_, pairs, then=True):
                for n, (l, r) in enumerate(pairs):
                    mm = pe.matmul(out_, l, r, start=(n == 0), stop=(n == len(pairs) - 1))
                if then:
                    mm.then_inc(s_rfull, 1)
                return mm

            pe.wait_ge(s_const, 14)
            pe.wait_ge(s_wload, 16 * 9)
            for c in range(C):
                mm = pe.transpose(psX[:, c * E:(c + 1) * E], gw[:, c * P:(c + 1) * P], ident[0:E, 0:E])
            mm.then_inc(s_gw, 1)
            pe.wait_ge(s_gwT, 2)
            with pe.Fori(0, B) as b:
                tick[0] = 0
                pe.wait_ge(s_x, 16 * (b + 1))
                for c in range(C):
                    transposes(b, xt, c)
                pe.wait_ge(s_rfree, NR + b * NTICK + tick[0])
                for n in range(2 * C):
                    m = n // 2 + C * (n % 2)
                    product(bank(b)[:, :], [(wqkv[:, c, m * P:(m + 1) * P], xT[:, c, :]) for c in range(C)])
                for i in range(ST):
                    product(bank(b)[:, :], [(xT[:, c, i * P:(i + 1) * P], wqkv[:, c, 2 * D:3 * D]) for c in range(C)])

                def row_max(h):
                    if h % 4 == 0:
                        pe.wait_ge(s_stk[h // 4], (b + 1) * (16 * 24))
                    for q in range(ST):
                        t = bank(b)
                        MAXED[h // 4] = NR + tick[0]
                        w = max(2, q + 1) * P
                        pe.matmul(t[:, 0:w], qst[0:96, h, q * P:(q + 1) * P], kst[0:96, h, 0:w], start=True, stop=False)
                        pe.matmul(t[:, q * P:(q + 1) * P], identb[:, :], mask_qk[:, :], start=False,
                                  stop=True).then_inc(s_rfull, 1)

                def max_rows(g):
                    t = bank(b)
                    pe.wait_ge(s_rfree, b * NTICK + MAXED[g])
                    pe.transpose(t[0:4 * ST, 0:P], nm[:, 4 * g:4 * g + 4, :].rearrange("p h q -> p (h q)"), ident[:, :]).then_inc(s_rfull, 1)

                def scores(h):
                    if h % 4 == 0:
                        pe.wait_ge(s_mrow[h // 4], 32 * (b + 1))
                    if h:
                        pe.wait_ge(s_exp, b * HEADS + h)
                    for kb in (0, 3, 1, 2):
                        o, w = (KOFF[kb], S - kb * P) if kb < 3 else (KOFF[3] - P, 2 * P)
                        lo = S - w
                        pe.matmul(psST[:, o:o + w], kst[0:98, h, kb * P:(kb + 1) * P], qst[0:98, h, lo:S],
                                  start=True, stop=False)
                        mm = pe.matmul(psST[:, KOFF[kb]:KOFF[kb] + P], identb[:, :], mask_kq[:, :], start=False, stop=True)
                    mm.then_inc(s_st, 1)

                def weigh(h):
                    g, j = divmod(h, 4)
                    pe.wait_ge(s_exp, b * HEADS + h + 1)
                    if j == 0 and g:
                        pe.wait_ge(s_ot, b * C + g)
                    for kb in range(ST):
                        p = pT[:, h % 2, KOFF[kb]:KOFF[kb] + S - kb * P]
                        pe.matmul(psOT[HD * j:HD * (j + 1), kb * P:S], v_s[:, kb, h * HD:(h + 1) * HD], p,
                                  start=(kb == 0), stop=(kb == ST - 1), skip_group_check=True)
                        mm = pe.matmul(psDEN[0:32, kb * P:S], onehot[:, h, :], p, start=(h == 0 and kb == 0),
                                       stop=(h == HEADS - 1 and kb == ST - 1), skip_group_check=True)
                    mm.then_inc(s_pv, 1)

                for what, h in ATTN:
                    {"max": row_max, "rows": max_rows, "scores": scores, "weigh": weigh}[what](h)
                pe.wait_ge(s_rden, b + 1)
                for g in range(C):
                    product(bank(b)[:, :], [(sel[:, g * P:(g + 1) * P], rden[:, :])])
                pe.wait_ge(s_rfree, NR + b * NTICK + tick[0])
                for i in range(ST):
                    product(bank(b)[:, :], [(otu[:, c, i * P:(i + 1) * P], wo_s[:, c, :]) for c in range(C)])

                def quant_linear(n, xin, win, cn, first):
                    for c in range(cn):
                        transposes(b, win, c)
                    pe.wait_ge(s_qin, 2 * b + n + 1)
                    for c in range(cn):
                        transposes(b, xin, c)
                    pe.wait_ge(s_diag, 4 * b + 2 * n + 1)
                    for k in range(2):
                        product(bank(b)[:, 0:cn * P], [(ones[:, :], dg[:, k, 0:cn * P])])
                    pe.wait_ge(s_diag, 4 * b + 2 * n + 2)
                    product(bank(b)[:, :], [(ones[:, :], dg[:, 0, :])])
                    pe.wait_ge(s_quant, 2 * b + n + 1)
                    for c in range(cn):
                        transposes(b, wq, c, True)
                        transposes(b, xq, c, True)
                    pe.wait_ge(s_rfree, NR + b * NTICK + tick[0])
                    for i in range(ST):
                        product(bank(b)[:, :], [(xqT[:, c, i * P:(i + 1) * P], wqT[:, c, :]) for c in range(cn)])

                pe.wait_ge(s_bw, 32 * b + 32)
                quant_linear(0, x1, wf, C, True)
                quant_linear(1, a2, wc, C2, False)
                pe.wait_ge(s_x2, b + 1)
                for c in range(C):
                    transposes(b, x1, c)
                pe.wait_ge(s_rfree, NR + b * NTICK + tick[0])
                product(bank(b)[0:E, :], [(gwT[:, c, :], xT[:, c, :]) for c in range(C)])
                pe.wait_ge(s_rfree, NR + b * NTICK + tick[0])
                apart(pe)
                t = bank(b)
                apart(pe)
                for i in range(ST):
                    mm = pe.transpose(t[:, i * E:(i + 1) * E], lgT[:, i * P:(i + 1) * P], ident[0:E, 0:E])
                mm.then_inc(s_rfull, 1)
                assert tick[0] == NTICK, (tick[0], NTICK)

        @block.vector
        def _(dve):
            tick = [0]

            def full(b):
                dve.wait_ge(s_rfull, b * NTICK + tick[0] + 1)
                t = psR[tick[0] % NR]
                tick[0] += 1
                return t

            def done(ins):
                ins.then_inc(s_rfree, 1)

            step = [0]

            def after(b):
                dve.wait_ge(s_dve, b * NSTEP + step[0])

            def made(ins):
                ins.then_inc(s_dve, 1)
                step[0] += 1

            for i in range(NR):
                done(dve.memset(amw[:, i:i + 1], 0.0))
            dve.memset(kst[96:98, :, :].bitcast(F32), 1.0).then_inc(s_gwT, 1)
            dve.wait_ge(s_wload, 16 * 9)
            dve.wait_ge(s_const, 14)
            dve.wait_ge(s_gw, 1)
            dve.tensor_copy(gwT[:, :, :], psX[:, 0:C * E].rearrange("p (c e) -> p c e", c=C)).then_inc(s_gwT, 1)

            def normalise(b, n, r):
                for i in range(ST):
                    made(dve.bn_stats(bn[:, i, :], r[:, i, :]))
                after(b)
                apart(dve)
                for i in range(ST):
                    made(dve.bn_aggr(mv[:, i, :], bn[:, i, :]))
                after(b)
                dve.tensor_scalar(small[:, 0:ST], mv[:, :, 1], LN_EPS, None, ALU.add).then_inc(s_powin, 1)
                dve.wait_ge(s_pow, 4 * b + n + 1)
                for i in range(ST):
                    ins = dve.tensor_scalar(x1[:, i, :], r[:, i, :], mv[:, i, 0:1], small[:, 8 + i:9 + i],
                                            ALU.subtract, ALU.mult)
                    if i < ST - 1:
                        made(ins)
                return ins

            def quant_linear(b, n, xin, win, cn):
                w = cn * P
                for am in (amw, amx):
                    for c in range(cn):
                        t = full(b)
                        done(dve.tensor_reduce(am[:, c:c + 1], t[:, :], AX.X, ALU.max, apply_absolute_value=True))
                dve.wait_ge(s_rfree, NR + b * NTICK + tick[0])
                made(dve.tensor_scalar(amw[:, 0:cn], amw[:, 0:cn], Q_EPS, None, ALU.max))
                after(b)
                made(dve.reciprocal(ram[:, 0:cn], amw[:, 0:cn]))
                after(b)
                dve.scalar_tensor_tensor(out=small[:, 0:cn], in0=amx[:, 0:cn], scalar=Q_EPS, in1=ram[:, 0:cn],
                                         op0=ALU.max, op1=ALU.mult).then_inc(s_powin, 1)
                dve.wait_ge(s_pow, 4 * b + n + 2)
                made(dve.tensor_scalar(sm[:, 0:cn], small[:, 8:8 + cn], Q_EPS, None, ALU.max))
                after(b)
                made(dve.reciprocal(rsm[:, 0:cn], sm[:, 0:cn]))
                after(b)
                for k, f in enumerate((sm, rsm)):
                    for c in range(cn):
                        ins = dve.tensor_scalar(dg[:, k, c * P:(c + 1) * P], ident[:, :], f[:, c:c + 1], None, ALU.mult)
                        if k == 0 or c < cn - 1:
                            made(ins)
                ins.then_inc(s_diag, 1)
                for dst, src, m, sc, rc in ((ws, win, amw, wsc, rws), (xs, xin, amx, xsc, rxs)):
                    t = full(b)
                    done(dve.tensor_tensor(dst[:, :, 0:w], src[:, :, :],
                                           t[:, 0:w].rearrange("p (a n) -> p a n", a=1).to_broadcast([P, ST, w]), ALU.mult))
                    dve.wait_ge(s_rfree, NR + b * NTICK + tick[0])
                    made(dve.tensor_reduce(m[:, :], dst[:, :, 0:w], AX.X, ALU.max, apply_absolute_value=True))
                    after(b)
                    made(dve.tensor_scalar(sc[:, :], m[:, :], Q_EPS, 1.0 / QMAX, ALU.max, ALU.mult))
                    after(b)
                    made(dve.reciprocal(rc[:, :], sc[:, :]))
                    after(b)
                for i in range(ST):
                    ins = dve.tensor_scalar(dg[:, 0, i * P:(i + 1) * P], ident[:, :], wsc[:, i:i + 1], None, ALU.mult)
                    if i < ST - 1:
                        made(ins)
                ins.then_inc(s_diag, 1)
                for dst, q, rc in ((ws, wq, rws), (xs, xq, rxs)):
                    for i in range(ST):
                        made(dve.tensor_scalar(dst[:, i, 0:w], dst[:, i, 0:w], rc[:, i:i + 1], QMAX, ALU.mult, ALU.min))
                    after(b)
                    made(dve.tensor_scalar(dst[:, :, 0:w], dst[:, :, 0:w], -QMAX, ROUND, ALU.max, ALU.add))
                    after(b)
                    ins = dve.tensor_scalar(q[:, :, 0:w], dst[:, :, 0:w], -ROUND, None, ALU.add)
                    if q is wq:
                        made(ins)
                ins.then_inc(s_quant, 1)
                t = full(b)
                done(dve.tensor_copy(wsc_bc[:, :], t[:, :]))
                for c in range(cn):
                    for dst in (wqT, xqT):
                        t = full(b)
                        done(dve.tensor_copy(dst[:, c, :], t[:, :].bitcast(BF16)[:, 0:S]))
                for i in range(ST):
                    t = full(b)
                    done(dve.scalar_tensor_tensor(out=h1[:, i, :], in0=t[:, :], scalar=xsc[:, i:i + 1], in1=wsc_bc[:, :],
                                                  op0=ALU.mult, op1=ALU.mult))
                dve.wait_ge(s_rfree, NR + b * NTICK + tick[0])

            with dve.Fori(0, B) as b:
                tick[0] = 0
                step[0] = 0
                for c in range(C):
                    t = full(b)
                    done(dve.tensor_copy(xT[:, c, :], t[:, :]))
                for n in range(2 * C):
                    m = n // 2 + C * (n % 2)
                    t = full(b)
                    dve.wait_ge(s_qkhi, b * 2 * C + n + 1)
                    done(dve.scalar_tensor_tensor(out=ql[:, m, :], in0=t[:, :], scalar=bqk[:, m:m + 1],
                                                  in1=qh[:, m, :].bitcast(F32), op0=ALU.add, op1=ALU.subtract))
                for i in range(ST):
                    t = full(b)
                    done(dve.tensor_tensor(v_s[:, i, :], t[:, :], bv_bc[:, :], ALU.add))

                def row_max(h):
                    for q in range(ST):
                        t = full(b)
                        done(dve.tensor_reduce(nm[:, h, q:q + 1], t[:, 0:(q + 1) * P], AX.X, ALU.max, negate=True))

                def max_rows(g):
                    t = full(b)
                    made(dve.tensor_copy(nmh[:, g, :], t[0:4 * ST, 0:P]))
                    after(b)
                    done(dve.tensor_tensor(nml[:, g, :], t[0:4 * ST, 0:P], nmh[:, g, :].bitcast(F32), ALU.subtract))

                for what, h in ATTN:
                    if what == "max":
                        row_max(h)
                    elif what == "rows":
                        max_rows(h)
                dve.wait_ge(s_pv, b * HEADS + HEADS)
                dve.reciprocal(rden[:, :], psDEN[0:HEADS, :]).then_inc(s_rden, 1)
                dve.wait_ge(s_ot, b * C + C)
                for g in range(C):
                    t = full(b)
                    done(dve.tensor_tensor(otu[:, g, :], otu[:, g, :], t[:, :], ALU.mult))
                dve.wait_ge(s_xrb, ST * (b + 1))
                for i in range(ST):
                    t = full(b)
                    done(dve.tensor_tensor(xr[:, i, :], xr[:, i, :], t[:, :], ALU.add))
                dve.wait_ge(s_rfree, NR + b * NTICK + tick[0])
                normalise(b, 0, xr).then_inc(s_qin, 1)
                dve.wait_ge(s_bw, 32 * b + 32)
                dve.wait_ge(s_qin, 2 * b + 1)
                quant_linear(b, 0, x1, wf, C)
                dve.wait_ge(s_silu, b + 1)
                dve.tensor_tensor(a2[:, :, :], sil[:, :, :], h1[:, :, I2:D], ALU.mult).then_inc(s_qin, 1)
                dve.wait_ge(s_qin, 2 * b + 2)
                quant_linear(b, 1, a2, wc, C2)
                made(dve.tensor_tensor(h1[:, :, :], h1[:, :, :], x1[:, :, :], ALU.add))
                after(b)
                normalise(b, 3, h1).then_inc(s_x2, 1)
                for c in range(C):
                    t = full(b)
                    done(dve.tensor_copy(xT[:, c, :], t[:, :]))
                t = full(b)
                done(dve.tensor_copy(lgT[:, :], t[0:E, :]))
                t = full(b)
                done(dve.tensor_copy(logits[:, bass.ds(b * (ST * E), ST * E)], t[:, 0:ST * E]))
                assert step[0] == NSTEP, (step[0], NSTEP)
        blk.close()

        stA.close()
        psA.close()
        stR = ctx.enter_context(ExitStack())

        def se(name, shape, dt=F32):
            return sb(name, shape, dt, stR)

        NE = NT * E
        NK = NT * TOPK
        w1_s = se("w1_s", [P, 2, C, F])
        w3_s = se("w3_s", [P, 2, C, F])
        w2_s = se("w2_s", [P, 2, len(KF), D])
        xg = se("xg", [P, 2, D])
        xgT = se("xgT", [P, 2, D])
        silg = se("silg", [P, F])
        hg = se("hg", [P, F])
        hgT = se("hgT", [P, len(KF), P])
        yg = se("yg", [P, 2, D])
        slot_T = se("slot_T", [RT, P])
        src_i = se("src_i", [P, JT], I32)
        dst_i = se("dst_i", [P, JT], I32)
        six = se("six", [P, 2, 1], I32)
        dix = se("dix", [P, 2, 1], I32)
        need_i = se("need_i", [1, JT], I32)
        buf_i = se("buf_i", [1, JT], I32)
        free_i = se("free_i", [1, E], I32)
        cwk = se("cwk", [P, NT, TOPK])
        cb = se("cb", [P, 2, TOPK + SH + 1, D])
        ob = se("ob", [P, 2, D])
        bn2 = se("bn2", [P, 2, 6])
        mv2 = se("mv2", [P, 2, 2])
        rs2 = se("rs2", [P, 2, 2])
        score = se("score", [P, NT, E])
        biased = se("biased", [P, NT, E])
        gmax = se("gmax", [P, NT, 4])
        gpair = se("gpair", [P, NT * 16])
        gpair2 = se("gpair2", [P, NT * 16])
        grank = se("grank", [P, NT, 4])
        pair = se("pair", [P, NT * E * E])
        pair2 = se("pair2", [P, NT * E * E])
        rank = se("rank", [P, NT, E])
        chosen = se("chosen", [P, NT, E])
        wsum = se("wsum", [P, NT])
        cwt = se("cwt", [P, NT, E])
        pos = se("pos", [P, NT, E])
        offs = se("offs", [P, NT + 1, E])
        ntile = se("ntile", [P, E])
        base = se("base", [P, E])
        tend = se("tend", [P, E])
        posk = se("posk", [P, NT, TOPK])
        posk_i = se("posk_i", [P, NT, TOPK], I32)
        need_f = se("need_f", [P, JT])
        free_f = se("free_f", [P, E])
        slotf = se("slotf", [P, RT])

        psE = ctx.enter_context(ExitStack())
        psTX, psUA, psUB, psTH, psY0, psY1, psP, psQ = (
            psE.enter_context(nc.psum_tensor(n, [P, 512], F32))
            for n in ("psTX", "psUA", "psUB", "psTH", "psY0", "psY1", "psP", "psQ"))
        psY = [psY0, psY1]

        s_sig = sem("s_sig")
        s_rt = sem("s_rt")
        s_cnt = sem("s_cnt")
        s_padin = sem("s_padin")
        s_slots = sem("s_slots")
        s_slotld = sem("s_slotld")
        s_slotT = sem("s_slotT")
        s_tab = sem("s_tab")
        s_w = sem("s_w")
        s_gat = [sem("s_gat0"), sem("s_gat1")]
        s_six = sem("s_six")
        s_dix = sem("s_dix")
        s_cc = sem("s_cc")
        NRT = 64
        NCC = 2 * (SH + TOPK + 2)
        s_tx = sem("s_tx")
        s_xe = sem("s_xe")
        s_up = sem("s_up")
        s_sil = sem("s_sil")
        s_hm = sem("s_hm")
        s_th = sem("s_th")
        s_ht = sem("s_ht")
        s_dn = sem("s_dn")
        s_ye = sem("s_ye")
        s_sca = [sem("s_sca0"), sem("s_sca1")]
        s_cin = [sem("s_cin0"), sem("s_cin1")]
        s_cv = sem("s_cv")
        s_cp = sem("s_cp")
        s_cy = sem("s_cy")
        s_out = [sem("s_out0"), sem("s_out1")]
        w1_v = w1.rearrange("e (c p) f -> p e c f", p=P)
        w3_v = w3.rearrange("e (c p) f -> p e c f", p=P)
        sw1_v = sw1.rearrange("(c p) (s f) -> p s c f", p=P, f=F)
        sw3_v = sw3.rearrange("(c p) (s f) -> p s c f", p=P, f=F)
        y_v = y_d[0:TOPK * T, :].rearrange("(k n p) d -> p n k d", p=P, n=NT)
        ys_v = y_d[YSH:YSH + SH * T, :].rearrange("(k n p) d -> p n k d", p=P, n=NT)
        xn_v = x2_d.rearrange("(n p) d -> p n d", p=P)
        o_v = out.rearrange("b (i p) d -> p (b i) d", p=P)

        def tiles(eng, body):
            for j in range(3):
                body(j, j % 2)
            with eng.Fori(0, (JT - 6) // 2) as i:
                body(2 * i + 3, 1)
                body(2 * i + 4, 0)
            for j in range(JT - 3, JT):
                body(j, j % 2)

        def is_first(j):
            return isinstance(j, int) and j == 0

        def is_last(j):
            return isinstance(j, int) and j == JT - 1

        def halves(j, par):
            return 8 * (j - par) + 16

        block2 = ctx.enter_context(nc.Block())

        @block2.sync
        def _(sp):
            sp.wait_ge(s_rfree, NR + B * NTICK)

            def weights(buf, parts):
                for dst, src_ in parts:
                    sp.dma_start(dst, src_).then_inc(s_w, 16)

            def w2_parts(buf, rows):
                k0 = (len(KF) - 1) * P
                return [(w2_s[:, buf, 0:len(KF) - 1, :], rows[0:k0, :].rearrange("(k p) d -> p k d", p=P)),
                        (w2_s[0:F - k0, buf, len(KF) - 1, :], rows[k0:F, :])]
            for s in range(SH):
                if s:
                    sp.wait_ge(s_w, 64 * s)
                weights(s, [(w1_s[:, s], sw1_v[:, s]), (w3_s[:, s], sw3_v[:, s])] + w2_parts(s, sw2[s * F:(s + 1) * F, :]))
            sp.dma_start(slot_d.rearrange("(t p) a -> t (p a)", p=P), padf[:, :]).then_inc(s_slotld, 16)
            sp.wait_ge(s_slots, 16 * NK)
            sp.dma_start(slot_T[:, :], slot_d.rearrange("(t p) a -> t (p a)", p=P)).then_inc(s_slotld, 16)
            sp.wait_ge(s_tab, 1)
            with sp.Fori(0, E // 2) as e2:
                for par in range(2):
                    e = 2 * e2 + par
                    sp.wait_ge(s_dn, sp.value_load(free_i[0:1, bass.ds(e, 1)], min_val=1, max_val=JT))
                    sp.wait_ge(s_w, 64 * (e + SH))
                    k0 = (len(KF) - 1) * P
                    weights(par, [(w1_s[:, par], w1_v[:, bass.ds(e, 1)]), (w3_s[:, par], w3_v[:, bass.ds(e, 1)]),
                                  (w2_s[:, par, 0:len(KF) - 1, :],
                                   w2[bass.ds(e, 1), 0:k0, :].rearrange("e (k p) d -> p (e k) d", p=P)),
                                  (w2_s[0:F - k0, par, len(KF) - 1, :],
                                   w2[bass.ds(e, 1), k0:F, :].rearrange("e p d -> p (e d)"))])
            sp.wait_ge(s_sca[0], 8 * JT)
            sp.wait_ge(s_sca[1], 8 * JT)

            def load(n, par):
                sp.dma_start(cb[:, par, 0:TOPK, :], y_v[:, bass.ds(n, 1)]).then_inc(s_cin[par], 16)
                sp.dma_start(cb[:, par, TOPK:TOPK + SH, :], ys_v[:, bass.ds(n, 1)]).then_inc(s_cin[par], 16)
                sp.dma_start(cb[:, par, TOPK + SH, :], xn_v[:, bass.ds(n, 1)]).then_inc(s_cin[par], 16)

            load(0, 0)
            load(1, 1)
            with sp.Fori(0, NT // 2 - 1) as i:
                n = 2 * i
                for par in range(2):
                    sp.wait_ge(s_cy, n + par + 1)
                    load(n + par + 2, par)
                    sp.dma_start(o_v[:, bass.ds(n + par, 1)], ob[:, par, :]).then_inc(s_out[par], 16)
            for par in range(2):
                sp.wait_ge(s_cy, NT - 2 + par + 1)
                sp.dma_start(o_v[:, NT - 2 + par], ob[:, par, :]).then_inc(s_out[par], 16)
            for par in range(2):
                sp.wait_ge(s_out[par], 8 * NT)

        @block2.gpsimd
        def _(pool):
            for s in range(SH):
                pool.iota(dst_i[:, s * NT:(s + 1) * NT], [[P, NT]], base=YSH + s * T,
                          channel_multiplier=1).then_inc(s_padin, 1)
                pool.iota(src_i[:, s * NT:(s + 1) * NT], [[P, NT]], base=0, channel_multiplier=1).then_inc(s_padin, 1)
            pool.wait_ge(s_slotld, 16)
            pool.wait_ge(s_rt, NRT)
            for n in range(NT):
                for k in range(TOPK):
                    pool.indirect_dma_start(slot_d, bass.IndirectOffsetOnAxis(ap=posk_i[:, n, k:k + 1], axis=0),
                                            tokf[:, n, k:k + 1], None).then_inc(s_slots, 16)
            pool.wait_ge(s_tab, 1)

            def gather(j, par):
                pool.tensor_copy(six[:, par, :], src_i[:, bass.ds(j, 1)]).then_inc(s_six, 1)
                pool.wait_ge(s_six, j + 1)
                apart(pool)
                pool.indirect_dma_start(xg[:, par, :], None, x2_d,
                                        bass.IndirectOffsetOnAxis(ap=six[:, par, :], axis=0)).then_inc(s_gat[par], 16)

            def scatter(j, par):
                pool.wait_ge(s_ye, j + 1)
                pool.tensor_copy(dix[:, par, :], dst_i[:, bass.ds(j, 1)]).then_inc(s_dix, 1)
                pool.wait_ge(s_dix, j + 1)
                apart(pool)
                pool.indirect_dma_start(y_d, bass.IndirectOffsetOnAxis(ap=dix[:, par, :], axis=0),
                                        yg[:, par, :], None).then_inc(s_sca[par], 16)

            def one(j, par):
                if not isinstance(j, int) or j + 2 < JT:
                    pool.wait_ge(s_tx, j + 1)
                    gather(j + 2, par)
                if not is_first(j):
                    scatter(j - 1, 1 - par)

            gather(0, 0)
            gather(1, 1)
            tiles(pool, one)
            scatter(JT - 1, (JT - 1) % 2)
            with pool.Fori(0, NT // 2) as i:
                n = 2 * i
                for par in range(2):
                    pool.wait_ge(s_cv, n + par + 1)
                    pool.tensor_tensor(rs2[:, par, 1:2], rs2[:, par, 0:1], halfn[:, 0:1], ALU.pow).then_inc(s_cp, 1)

        @block2.scalar
        def _(act):
            act.wait_ge(s_rfree, NR + B * NTICK)
            act.activation(score[:, :, :].rearrange("p n e -> p (n e)"), logits[:, :], ACT.Sigmoid).then_inc(s_sig, 1)

            def one(j, par):
                act.wait_ge(s_up, j + 1)
                act.activation(silg[:, :], psUA[:, 0:F], ACT.Silu).then_inc(s_sil, 1)
                if not is_last(j):
                    act.wait_ge(s_tx, j + 2)
                    act.copy(xgT[:, 1 - par, :], psTX[:, :]).then_inc(s_xe, 1)
                if not is_first(j):
                    evacuate(j - 1, 1 - par)

            def evacuate(j, par):
                act.wait_ge(s_dn, j + 1)
                if not isinstance(j, int) or j >= 2:
                    act.wait_ge(s_sca[par], 8 * (j - par))
                act.copy(yg[:, par, :], psY[par][:, :]).then_inc(s_ye, 1)

            act.wait_ge(s_tx, 1)
            act.copy(xgT[:, 0, :], psTX[:, :]).then_inc(s_xe, 1)
            tiles(act, one)
            evacuate(JT - 1, (JT - 1) % 2)

        @block2.tensor
        def _(pe):
            pe.wait_ge(s_cnt, 1)
            pe.matmul(psP[:, 0:NE], upper[:, :], chosen[:, :, :].rearrange("p n e -> p (n e)"), start=True, stop=True)
            pe.matmul(psQ[:, 0:NE], ones[:, :], chosen[:, :, :].rearrange("p n e -> p (n e)"), start=True,
                      stop=True).then_inc(s_slotT, 1)
            pe.wait_ge(s_slotld, 32)
            pe.wait_ge(s_rt, NRT)
            pe.transpose(psP[:, 0:RT], slot_T[:, :], ident[0:RT, 0:RT]).then_inc(s_slotT, 1)
            pe.wait_ge(s_tab, 1)

            def gathered(j, par):
                pe.wait_ge(s_gat[par], 8 * (j - par) + 16)
                for c in range(C):
                    mm = pe.transpose(psTX[:, c * P:(c + 1) * P], xg[:, par, c * P:(c + 1) * P], ident[:, :])
                mm.then_inc(s_tx, 1)

            def down(j, par):
                pe.wait_ge(s_ht, j + 1)
                if not isinstance(j, int) or j >= 2:
                    pe.wait_ge(s_ye, j - 1)
                apart(pe)
                buf = pe.value_load(buf_i[0:1, bass.ds(j, 1)], min_val=0, max_val=1)
                for k, (k0, kn) in enumerate(KF):
                    mm = pe.matmul(psY[par][:, :], hgT[0:kn, k, :], w2_s[0:kn, bass.ds(buf, 1), k, :],
                                   start=(k == 0), stop=(k == len(KF) - 1))
                mm.then_inc(s_dn, 1)

            def one(j, par):
                need = pe.value_load(need_i[0:1, bass.ds(j, 1)], min_val=1, max_val=E + SH)
                pe.wait_ge(s_w, need * 64)
                pe.wait_ge(s_xe, j + 1)
                apart(pe)
                buf = pe.value_load(buf_i[0:1, bass.ds(j, 1)], min_val=0, max_val=1)
                for t, w in ((psUA, w1_s), (psUB, w3_s)):
                    for c in range(C):
                        mm = pe.matmul(t[:, 0:F], xgT[:, par, c * P:(c + 1) * P], w[:, bass.ds(buf, 1), c, :],
                                       start=(c == 0), stop=(c == C - 1))
                mm.then_inc(s_up, 1)
                if not is_last(j):
                    gathered(j + 1, 1 - par)
                if not is_first(j):
                    down(j - 1, 1 - par)
                pe.wait_ge(s_hm, j + 1)
                for k, (k0, kn) in enumerate(KF):
                    mm = pe.transpose(psTH[0:kn, k * P:(k + 1) * P], hg[:, k0:k0 + kn], ident[:, :])
                mm.then_inc(s_th, 1)

            gathered(0, 0)
            tiles(pe, one)
            down(JT - 1, (JT - 1) % 2)

        @block2.vector
        def _(dve):
            step = [0]

            def link(ins):
                ins.then_inc(s_rt, 1)
                step[0] += 1
                dve.wait_ge(s_rt, step[0])

            def mid(t, k):
                return t.rearrange("p a (o b) -> p a o b", o=1).to_broadcast([P, t.shape[1], k, t.shape[2]])

            def last(t, k):
                return t.rearrange("p a (b o) -> p a b o", o=1).to_broadcast([P, t.shape[1], t.shape[2], k])

            def front(t, n):
                return t.rearrange("p (o a) b -> p o a b", o=1).to_broadcast([P, n, t.shape[1], t.shape[2]])

            def as4(t, n, a, b):
                return t[:, 0:n * a * b].rearrange("p (n a b) -> p n a b", a=a, b=b)

            def ranks(out_, val, tri, n, m, t1, t2):
                link(dve.tensor_tensor(as4(t1, n, m, m), mid(val, m), last(val, m), ALU.is_equal))
                link(dve.tensor_tensor(as4(t1, n, m, m), as4(t1, n, m, m), front(tri, n), ALU.mult))
                link(dve.tensor_tensor(as4(t2, n, m, m), mid(val, m), last(val, m), ALU.is_gt))
                link(dve.tensor_tensor(as4(t1, n, m, m), as4(t1, n, m, m), as4(t2, n, m, m), ALU.add))
                link(dve.tensor_reduce(out_, as4(t1, n, m, m), AX.X, ALU.add))

            dve.wait_ge(s_sig, 1)
            link(dve.tensor_tensor(biased[:, :, :], score[:, :, :],
                                   ebias_bc[:, :].rearrange("p (o e) -> p o e", o=1).to_broadcast([P, NT, E]), ALU.add))
            grouped = biased[:, :, :].rearrange("p n (g r) -> p (n g) r", g=4)
            link(dve.tensor_reduce(gmax[:, :, :].rearrange("p n g -> p (n g)"), grouped, AX.X, ALU.max))
            ranks(grank[:, :, :], gmax[:, :, :], tri4[:, :, :], NT, 4, gpair, gpair2)
            link(dve.tensor_scalar(grank[:, :, :], grank[:, :, :], 2.0, None, ALU.is_lt))
            spread = grank[:, :, :].rearrange("p n (g o) -> p (n g) o", o=1).to_broadcast([P, NT * 4, 4])
            link(dve.tensor_tensor(grouped, grouped, spread, ALU.mult))
            link(dve.tensor_scalar(grank[:, :, :], grank[:, :, :], BIG, -BIG, ALU.mult, ALU.add))
            link(dve.tensor_tensor(grouped, grouped, spread, ALU.add))
            ranks(rank[:, :, :], biased[:, :, :], tri16[:, :, :], NT, E, pair, pair2)
            link(dve.tensor_scalar(chosen[:, :, :], rank[:, :, :], float(TOPK), None, ALU.is_lt))
            link(dve.tensor_tensor(cwt[:, :, :], chosen[:, :, :], score[:, :, :], ALU.mult))
            dve.tensor_scalar(offs[:, 0, :], chosen[:, 0, :], 0.0, None, ALU.mult).then_inc(s_cnt, 1)
            link(dve.tensor_reduce(wsum[:, :], cwt[:, :, :], AX.X, ALU.add))
            link(dve.reciprocal(wsum[:, :], wsum[:, :]))
            link(dve.tensor_tensor(cwt[:, :, :], cwt[:, :, :],
                                   wsum[:, :].rearrange("p (n o) -> p n o", o=1).to_broadcast([P, NT, E]), ALU.mult))
            dve.wait_ge(s_slotT, 1)
            dve.wait_ge(s_cnt, 1)
            tot = psQ[:, 0:NE].rearrange("p (n e) -> p n e", e=E)
            for n in range(NT):
                link(dve.tensor_tensor(offs[:, n + 1, :], offs[:, n, :], tot[:, n, :], ALU.add))
            cnt = offs[:, NT, :].rearrange("p (e o) -> p e o", o=1)
            pv = pair[:, 0:E * NT].rearrange("p (e k) -> p e k", e=E)
            link(dve.tensor_tensor(pv, cnt.to_broadcast([P, E, NT]), k128[:, :, :], ALU.is_gt))
            link(dve.tensor_reduce(ntile[:, :], pv, AX.X, ALU.add))
            link(dve.tensor_scalar(ntile[:, :], ntile[:, :], 1.0, None, ALU.max))
            pe2 = pair[:, 0:E * E].rearrange("p (e k) -> p e k", e=E)
            link(dve.tensor_tensor(pe2, ntile[:, :].rearrange("p (o e) -> p o e", o=1).to_broadcast([P, E, E]),
                                   tri16[:, :, :], ALU.mult))
            link(dve.tensor_reduce(base[:, :], pe2, AX.X, ALU.add))
            link(dve.tensor_tensor(tend[:, :], base[:, :], ntile[:, :], ALU.add))
            link(dve.tensor_tensor(pos[:, :, :], psP[:, 0:NE].rearrange("p (n e) -> p n e", e=E), offs[:, 0:NT, :], ALU.add))
            link(dve.scalar_tensor_tensor(out=pos[:, :, :], in0=base[:, :].rearrange("p (o e) -> p o e", o=1).to_broadcast([P, NT, E]),
                                          scalar=float(P), in1=pos[:, :, :], op0=ALU.mult, op1=ALU.add))
            isk = as4(pair, NT, TOPK, E)
            tmp = as4(pair2, NT, TOPK, E)
            link(dve.tensor_tensor(isk, mid(rank[:, :, :], TOPK), front(krow[:, :, :], NT), ALU.is_equal))
            link(dve.tensor_tensor(tmp, isk, mid(pos[:, :, :], TOPK), ALU.mult))
            link(dve.tensor_reduce(posk[:, :, :], tmp, AX.X, ALU.add))
            link(dve.tensor_copy(posk_i[:, :, :], posk[:, :, :]))
            link(dve.tensor_tensor(tmp, isk, mid(cwt[:, :, :], TOPK), ALU.mult))
            link(dve.tensor_reduce(cwk[:, :, :], tmp, AX.X, ALU.add))
            pj = pair[:, 0:RT * E].rearrange("p (j e) -> p j e", e=E)
            link(dve.tensor_tensor(pj, tend[:, :].rearrange("p (o e) -> p o e", o=1).to_broadcast([P, RT, E]),
                                   jrow[:, :, :], ALU.is_le))
            link(dve.tensor_reduce(need_f[:, SH * NT:JT], pj, AX.X, ALU.add))
            link(dve.tensor_scalar(need_f[:, SH * NT:JT], need_f[:, SH * NT:JT], float(E - 1), float(SH + 1), ALU.min, ALU.add))
            for s in range(SH):
                link(dve.memset(need_f[:, s * NT:(s + 1) * NT], float(s + 1)))
                link(dve.memset(free_f[:, s:s + 1], float((s + 1) * NT)))
            link(dve.tensor_scalar(free_f[:, SH:E], base[:, 1:E - 1], float(SH * NT), None, ALU.add))
            link(dve.tensor_copy(need_i[:, :], need_f[0:1, :]))
            link(dve.tensor_copy(free_i[:, :], free_f[0:1, :]))
            link(dve.tensor_scalar(need_f[:, :], need_f[:, :], -1.0, None, ALU.add))
            link(dve.tensor_copy(buf_i[:, :], need_f[0:1, :]))
            link(dve.tensor_scalar(buf_i[:, :], buf_i[:, :], 1, None, ALU.bitwise_and))
            assert step[0] == NRT, step[0]
            dve.wait_ge(s_slotT, 2)
            link(dve.tensor_copy(dst_i[:, SH * NT:JT], psP[:, 0:RT]))
            dve.wait_ge(s_padin, 2 * SH)
            link(dve.tensor_scalar(src_i[:, SH * NT:JT], dst_i[:, SH * NT:JT], T - 1, None, ALU.bitwise_and))
            dve.tensor_scalar(wsum[:, 0:1], wsum[:, 0:1], 1.0, None, ALU.mult).then_inc(s_tab, 1)

            def one(j, par):
                dve.wait_ge(s_sil, j + 1)
                dve.tensor_tensor(hg[:, :], silg[:, :], psUB[:, 0:F], ALU.mult).then_inc(s_hm, 1)
                dve.wait_ge(s_th, j + 1)
                k0 = len(KF) - 1
                dve.tensor_copy(hgT[:, 0:k0, :], psTH[:, 0:k0 * P].rearrange("p (k n) -> p k n", n=P))
                dve.tensor_copy(hgT[0:KF[k0][1], k0, :], psTH[0:KF[k0][1], k0 * P:(k0 + 1) * P]).then_inc(s_ht, 1)

            tiles(dve, one)
            ch = [0]

            def made(ins, n):
                ins.then_inc(s_cc, 1)
                ch[0] += 1
                dve.wait_ge(s_cc, n * (NCC // 2) + ch[0])

            def combine(n, first):
                ch[0] = 0
                for par in range(2):
                    dve.wait_ge(s_cin[par], n * 24 + 48)
                    acc = cb[:, par, TOPK + SH, :]
                    for k in range(SH):
                        made(dve.tensor_tensor(acc, acc, cb[:, par, TOPK + k, :], ALU.add), n)
                    for k in range(TOPK):
                        w = cwk[:, bass.ds(n + par, 1), k:k + 1].rearrange("p a b -> p (a b)")
                        made(dve.scalar_tensor_tensor(out=acc, in0=cb[:, par, k, :], scalar=w, in1=acc,
                                                      op0=ALU.mult, op1=ALU.add), n)
                    made(dve.bn_stats(bn2[:, par, :], acc), n)
                    apart(dve)
                    made(dve.bn_aggr(mv2[:, par, :], bn2[:, par, :]), n)
                    dve.tensor_scalar(rs2[:, par, 0:1], mv2[:, par, 1:2], LN_EPS, None, ALU.add).then_inc(s_cv, 1)
                    dve.wait_ge(s_cp, n + par + 1)
                    if not first:
                        dve.wait_ge(s_out[par], 8 * n)
                    dve.tensor_scalar(ob[:, par, :], acc, mv2[:, par, 0:1], rs2[:, par, 1:2],
                                      ALU.subtract, ALU.mult).then_inc(s_cy, 1)
                    dve.wait_ge(s_cy, n + par + 1)
                assert ch[0] == NCC, ch[0]

            combine(0, True)
            with dve.Fori(1, NT // 2) as i:
                combine(2 * i, False)


_INS = ["x", "fside_BxS2xS2_0", "ctx_1024", "L0_attn_Wqkv", "L0_attn_bqkv", "L0_attn_Wo", "L0_attn_bo", "L0_ffn_gate_w",
        "L0_ffn_expert_bias", "L0_ffn_w1", "L0_ffn_w2", "L0_ffn_w3", "L0_ffn_sw1", "L0_ffn_sw2", "L0_ffn_sw3"]
_OUTS = [((4, 512, 512), "float32")]


def kernel(**inputs):
    import numpy as _np
    import concourse.bacc as _bacc
    from concourse import mybir as _mybir
    from concourse.bass_utils import run_bass_kernel_spmd as _run

    nc = _bacc.Bacc("TRN2", target_bir_lowering=False, num_devices=1)
    arrays, args = {}, []
    for name in _INS:
        a = _np.ascontiguousarray(inputs[name])
        arrays[f"in_{name}_dram"] = a
        args.append(nc.dram_tensor(f"in_{name}_dram", a.shape, _mybir.dt.from_np(a.dtype), kind="ExternalInput").ap())
    for i, (shape, dtype) in enumerate(_OUTS):
        dt = _mybir.dt.from_np(_np.dtype(dtype))
        args.append(nc.dram_tensor(f"out_{i}_dram", shape, dt, kind="ExternalOutput").ap())
    decoder_layer(nc, *args)
    r = _run(nc, [arrays], core_ids=[0])
    got = tuple(r.results[0][f"out_{i}_dram"] for i in range(len(_OUTS)))
    return got[0]
```

```python
from contextlib import ExitStack

import concourse.bass as bass
from concourse import mybir

F32 = mybir.dt.float32
F32R = mybir.dt.float32r
BF16 = mybir.dt.bfloat16
I32 = mybir.dt.int32
U32 = mybir.dt.uint32
ALU = mybir.AluOpType
ACT = mybir.ActivationFunctionType
AX = mybir.AxisListType

P = 128
HEADS = 16
HD = 32
LN_EPS = 1e-5
Q_EPS = 1e-6
QMAX = 127.0
ROUND = 12582912.0
NEG = -1e30
BIG = 1e30
NR = 3
TOPK = 4


def decoder_layer(nc, x, fside, ctxw, Wqkv, bqkv, Wo, bo, gate_w, ebias, w1, w2, w3, sw1, sw2, sw3, out, dbg=None):
    B, S, D = x.shape
    C = D // P
    ST = S // P
    I2 = ctxw.shape[2]
    C2 = I2 // P
    E, _, F = w1.shape
    NT = B * ST
    T = B * S
    KF = [(k * P, min(P, F - k * P)) for k in range((F + P - 1) // P)]
    SH = sw1.shape[1] // F
    SCALE = float(HD) ** -0.5
    PW = ST * S - P * ST * (ST - 1) // 2
    RT = (TOPK * T + (P - 1) * E) // P
    RT += RT % 2
    JT = RT + SH * NT
    assert D == 512 and S == 512 and HEADS * HD == D and I2 == 256 and sw1.shape[1] == SH * F

    x2_d = nc.dram_tensor("x2_d", [T, D], F32).ap()
    slot_d = nc.dram_tensor("slot_d", [RT * P, 1], F32).ap()
    YPAD = TOPK * T
    y_d = nc.dram_tensor("y_d", [YPAD + RT * P, D], F32).ap()
    sx_d = nc.dram_tensor("sx_d", [T, D], F32).ap()

    with ExitStack() as ctx:
        def sb(name, shape, dt=F32, stack=ctx):
            return stack.enter_context(nc.sbuf_tensor(name, shape, dt))

        def sem(name):
            return ctx.enter_context(nc.semaphore(name))

        ident = sb("ident", [P, P])
        identb = sb("identb", [P, P], BF16)
        ones = sb("ones", [P, P])
        mask_qk = sb("mask_qk", [P, P], BF16)
        mask_kq = sb("mask_kq", [P, P], BF16)
        onehot = sb("onehot", [P, HEADS, 32])
        sel = sb("sel", [HEADS, D])
        tri16 = sb("tri16", [P, E, E])
        tri4 = sb("tri4", [P, 4, 4])
        upper = sb("upper", [P, P])
        k128 = sb("k128", [P, E, NT])
        jrow = sb("jrow", [P, RT, 1])
        krow = sb("krow", [P, TOPK, E])
        halfp = sb("halfp", [P, 8])
        halfn = sb("halfn", [P, 8])
        tokf = sb("tokf", [P, NT, TOPK])
        padf = sb("padf", [RT, P])
        score = sb("score", [P, NT, E])
        rank = sb("rank", [P, NT, E])
        chosen = sb("chosen", [P, NT, E])
        cwk = sb("cwk", [P, NT, TOPK])
        UPN, DNN = C * F, len(KF) * D
        room = sb("room", [P, max(2 * (2 * UPN + DNN), 4 * C * D + D)])
        w1_r = room[:, 0:2 * UPN].rearrange("p (a c n) -> p a c n", a=2, c=C)
        w3_r = room[:, 2 * UPN:4 * UPN].rearrange("p (a c n) -> p a c n", a=2, c=C)
        w2_r = room[:, 4 * UPN:4 * UPN + 2 * DNN].rearrange("p (a c n) -> p a c n", a=2, c=len(KF))
        ebias_bc = sb("ebias_bc", [P, E])

        psA = ctx.enter_context(ExitStack())
        psST = psA.enter_context(nc.psum_tensor("psST", [P, 3 * 512], F32))
        psR = [psA.enter_context(nc.psum_tensor(f"psR{i}", [P, 512], F32)) for i in range(NR)]
        psOT = psA.enter_context(nc.psum_tensor("psOT", [P, 512], F32))
        psDEN = psA.enter_context(nc.psum_tensor("psDEN", [P, 512], F32))

        s_const = sem("s_const")
        s_apart = sem("s_apart")
        s_pool_fill = sem("s_pool_fill")
        s_wload = sem("s_wload")
        s_gw = sem("s_gw")
        s_gwT = sem("s_gwT")
        s_x = sem("s_x")
        s_xr = sem("s_xr")
        s_bw = sem("s_bw")
        s_rfull = sem("s_rfull")
        s_dfree = sem("s_dfree")
        s_afree = sem("s_afree")
        s_dve = sem("s_dve")
        s_qkhi = sem("s_qkhi")
        s_scr = sem("s_scr")
        s_stk = [sem(f"s_stk{i}") for i in range(2)]
        s_mrow = [sem(f"s_mrow{i}") for i in range(2)]
        s_st = sem("s_st")
        s_exp = sem("s_exp")
        s_pv = sem("s_pv")
        s_ot = sem("s_ot")
        s_rden = sem("s_rden")
        s_xrb = sem("s_xrb")
        s_qin = sem("s_qin")
        s_diag = sem("s_diag")
        s_quant = sem("s_quant")
        s_powin = sem("s_powin")
        s_pow = sem("s_pow")
        s_silu = sem("s_silu")
        s_x2 = sem("s_x2")
        s_x2st = sem("s_x2st")

        def quant_steps(n, cn):
            return ([("wtr", n, c) for c in range(cn)] + [("xtr", n, c) for c in range(cn)] + [("s", n)]
                    + [("ws", n), ("wq", n), ("wb", n)] + [("wqt", n, c) for c in range(cn)]
                    + [("xs", n), ("xq", n)] + [("xqt", n, c) for c in range(cn)] + [("h", n, i) for i in range(ST)])

        def merge(*lists):
            return [x for items in lists for x in items]

        b_steps = [("ln1",)] + quant_steps(0, C) + [("a2",)] + quant_steps(1, C2) + [("ln2",)] + [
            ("x2t", c) for c in range(C)] + [("lg",), ("lgt",), ("route",)]
        B_KINDS = {x[0] for x in b_steps}
        rest = list(b_steps)

        def take(n):
            out_ = rest[:n]
            del rest[:n]
            return out_

        def until(*x):
            return take(rest.index(x) + 1)

        def heads(*hs):
            return merge(*([("scores", h)] + [("weigh", h - 1)] * (h > 0) for h in hs))

        def each(kind, *ns):
            return [(kind, n) for n in ns]

        SEQ = merge(
            until("ln1"), each("xt", *range(C)), each("qk", 0, 1), until("wtr", 0, C - 1), each("qk", 2, 3),
            until("s", 0), each("v", 0, 1), until("ws", 0), each("v", 2, 3), until("wb", 0),
            each("max", 0, 1, 2, 3), each("rows", 0), until("xq", 0), heads(0, 1, 2), until("xqt", 0, C - 1),
            each("max", 4, 5, 6, 7), each("rows", 1), heads(3), until("a2"), heads(4), each("qk", 4, 5), until("s", 1),
            heads(5, 6), until("ws", 1), heads(7), until("wb", 1), each("qk", 6, 7), each("max", 8, 9, 10, 11),
            each("rows", 2), until("xq", 1), heads(8, 9), until("h", 1, ST - 1), heads(10), until("ln2"), heads(11),
            each("max", 12, 13, 14, 15), each("rows", 3), heads(12), until("lgt"), heads(13), until("route"),
            heads(14, 15), each("weigh", 15), each("bc", *range(C)), each("wo", *range(ST)))
        assert not rest
        ONE = {"xt", "qk", "v", "rows", "bc", "wo", "wtr", "xtr", "ws", "wb", "wqt", "xs", "xqt", "h", "x2t", "lg", "lgt"}
        TICKS = {"max": ST, **dict.fromkeys(ONE, 1)}
        CHAIN = {"rows": 1, "ln1": 11, "ln2": 12, "s": None, "ws": ST + 2, "wq": ST + 1, "xs": 3, "xq": ST + 1,
                 "route": 24}

        BY_ACT = {"xt", "wqt", "xqt", "x2t", "lg", "lgt"}

        def chain(x):
            return {0: 3 + 2 * C, 1: 3 + 2 * C2}[x[1]] if x[0] == "s" else CHAIN.get(x[0], 0)

        def apart(eng):
            eng.sem_inc(s_apart, 1)

        class Pass:

            def __init__(self, steps, start):
                self.steps, self.start, self.where, self.holder = steps, start, {}, []
                n = [0, 0, 0, 0]
                for x in steps:
                    self.where[x] = tuple(n)
                    used = TICKS.get(x[0], 0)
                    self.holder += [(x, m) for m in range(used)]
                    n[0] += used
                    n[2 if x[0] in BY_ACT else 1] += used
                    n[3] += chain(x)
                self.count = tuple(n)

            def end(self, turns=1):
                return tuple(s_ + turns * c_ for s_, c_ in zip(self.start, self.count))

        class At:

            def __init__(self, p, turn):
                self.p, self.turn = p, turn

            def value(self, which, local):
                p = self.p
                if self.turn is None:
                    return p.start[which] + local
                return self.turn * p.count[which] + (p.start[which] + local)

            def ticket(self, x):
                return self.value(0, self.p.where[x][0])

            def freed(self, x):
                return self.value(1, self.p.where[x][1])

            def ordered(self, x):
                return self.value(3, self.p.where[x][3])

            def let_go(self, eng, x, more=0):
                if x[0] in BY_ACT:
                    eng.wait_ge(s_afree, self.value(2, self.p.where[x][2] + more + 1))
                else:
                    eng.wait_ge(s_dfree, self.value(1, self.p.where[x][1] + more + 1))

            def bank(self, x, more=0):
                return psR[(self.p.where[x][0] + more) % NR][:, :]

            def take_bank(self, pe, x, more=0):
                n = self.p.where[x][0] + more
                if n >= NR:
                    self.let_go(pe, *self.p.holder[n - NR])
                elif n == 0 and self.p.start[0]:
                    pe.wait_ge(s_dfree, self.value(1, 0))
                    apart(pe)
                    pe.wait_ge(s_afree, self.value(2, 0))
                return self.bank(x, more)

        A_ONLY = [x for x in SEQ if x[0] not in B_KINDS]
        first_pass = Pass(A_ONLY, (0, 0, 0, 0))
        both_pass = Pass(SEQ, first_pass.end())
        last_pass = Pass(b_steps, both_pass.end(B - 1))
        ALL_D, ALL_A = last_pass.end()[1:3]

        def passes(eng, walk):
            walk(first_pass.steps, 0, None, At(first_pass, None))
            with eng.Fori(1, B) as i:
                walk(both_pass.steps, i, i - 1, At(both_pass, i - 1))
            walk(last_pass.steps, None, B - 1, At(last_pass, None))

        stA = ctx.enter_context(ExitStack())

        def sa(name, shape, dt=F32):
            return sb(name, shape, dt, stA)

        wqkv = room[:, 0:3 * C * D].rearrange("p (c n) -> p c n", c=C)
        wo_s = room[:, 3 * C * D:4 * C * D].rearrange("p (c n) -> p c n", c=C)
        bqk = sa("bqk", [P, 2 * C])
        bv_bc = room[:, 4 * C * D:4 * C * D + D]
        bo_bc = sa("bo_bc", [P, D])
        gwT = sa("gwT", [P, C, E])
        xt = sa("xt", [P, ST, D])
        xr = sa("xr", [P, ST, D])
        xT = sa("xT", [P, C, S])
        v_s = sa("v_s", [P, ST, D])
        qhl = sa("qhl", [P, 4, 2, S], F32R)
        qst = sa("qst", [P, 2, 4, S], F32R)
        kst = sa("kst", [P, 2, 4, S], F32R)
        pT = sa("pT", [P, 2, PW])
        nm = sa("nm", [P, HEADS, ST])
        nmh = sa("nmh", [4 * ST, 2, P], F32R)
        nml = sa("nml", [4 * ST, 2, P], F32R)
        rden = sa("rden", [HEADS, S])
        otu = sa("otu", [P, C, S])
        x1 = sa("x1", [P, ST, D])
        wf = sa("wf", [P, ST, D])
        wc = sa("wc", [P, ST, I2])
        dg = sa("dg", [P, 2, D])
        xs = sa("xs", [P, ST, D])
        xq = sa("xq", [P, ST, D], BF16)
        xqT = sa("xqT", [P, C, S], BF16)
        wqT = sa("wqT", [P, C, S], BF16)
        wsc_bc = sa("wsc_bc", [P, D])
        h1 = sa("h1", [P, ST, D])
        x2T = xs
        small = sa("small", [P, 16])
        biased = sa("biased", [P, ST, E])
        gmax = sa("gmax", [P, ST, 4])
        gpair = sa("gpair", [P, ST * 16])
        gpair2 = sa("gpair2", [P, ST * 16])
        grank = sa("grank", [P, ST, 4])
        cwt = sa("cwt", [P, ST, E])
        wsum = sa("wsum", [P, ST])
        epair = xs[:, 0:2, :].rearrange("p a n -> p (a n)")
        epair2 = xs[:, 2:4, :].rearrange("p a n -> p (a n)")
        amw, amx, ram, sm, rsm, wsc, rws, xsc, rxs = (sa(n, [P, 4]) for n in
                                                      ("amw", "amx", "ram", "sm", "rsm", "wsc", "rws", "xsc", "rxs"))
        bn = sa("bn", [P, ST, 6])
        mv = sa("mv", [P, ST, 2])
        gate_half = h1[:, :, 0:I2]
        gw = h1[0:E, 0, :]
        lgT = h1[0:E, 1, :]

        scr_d = nc.dram_tensor("scr_d", [2 * C, 2, P, S], F32).ap()
        x_v = x.rearrange("b (i p) d -> p b i d", p=P)
        f_v = fside.rearrange("b (i p) d -> p b i d", p=P)
        c_v = ctxw.rearrange("b (i p) d -> p b i d", p=P)
        x2_v = x2_d.rearrange("(b i p) d -> p b i d", p=P, i=ST)
        wqkv_v = Wqkv.rearrange("(c p) n -> p c n", p=P)
        KOFF = [0, S, 2 * S, 2 * S - P]

        def mid(t, k):
            return t.rearrange("p a (o b) -> p a o b", o=1).to_broadcast([P, t.shape[1], k, t.shape[2]])

        def last(t, k):
            return t.rearrange("p a (b o) -> p a b o", o=1).to_broadcast([P, t.shape[1], t.shape[2], k])

        def front(t, n):
            return t.rearrange("p (o a) b -> p o a b", o=1).to_broadcast([P, n, t.shape[1], t.shape[2]])

        def as4(t, n, a, b):
            return t[:, 0:n * a * b].rearrange("p (n a b) -> p n a b", a=a, b=b)

        def bias_row(b, lo):
            return b[lo:lo + D].rearrange("(a n) -> a n", a=1).to_broadcast([P, D])

        s_w = sem("s_w")
        s_slotld = sem("s_slotld")
        sw1_v = sw1.rearrange("(c p) (s f) -> p s c f", p=P, f=F)
        sw3_v = sw3.rearrange("(c p) (s f) -> p s c f", p=P, f=F)
        W2K = (len(KF) - 1) * P

        def weights(sp, parts_):
            for dst, src_ in parts_:
                sp.dma_start(dst, src_).then_inc(s_w, 16)

        blk = ExitStack()
        block = blk.enter_context(nc.Block())

        @block.sync
        def _(sp):
            sp.dma_start(xt[:, :, :], x_v[:, 0]).then_inc(s_x, 16)
            sp.dma_start(wqkv[:, :, 0:D], wqkv_v[:, :, 0:D]).then_inc(s_wload, 16)
            sp.dma_start(wqkv[:, :, D:2 * D], wqkv_v[:, :, D:2 * D]).then_inc(s_wload, 16)
            sp.dma_start(wqkv[:, :, 2 * D:3 * D], wqkv_v[:, :, 2 * D:3 * D]).then_inc(s_wload, 16)
            with nc.allow_non_contiguous_dma(reason="a bias by rows, once"):
                sp.dma_start(bqk[:, :], bqkv[0:2 * D].rearrange("(c p) -> p c", p=P)).then_inc(s_wload, 16)
            sp.dma_start(bv_bc[:, :], bias_row(bqkv, 2 * D)).then_inc(s_wload, 16)
            sp.dma_start(bo_bc[:, :], bias_row(bo, 0)).then_inc(s_wload, 16)
            sp.dma_start(wo_s[:, :, :], Wo.rearrange("(c p) n -> p c n", p=P)).then_inc(s_wload, 16)
            sp.dma_start(gw[:, :], gate_w).then_inc(s_wload, 16)
            sp.dma_start(ebias_bc[:, :], ebias.rearrange("(a n) -> a n", a=1).to_broadcast([P, E])).then_inc(s_wload, 16)

            def walk(steps, a, b, at):
                if b is not None:
                    sp.dma_start(wf[:, :, :], f_v[:, bass.ds(b, 1)]).then_inc(s_bw, 16)
                    sp.dma_start(wc[:, :, :], c_v[:, bass.ds(b, 1)]).then_inc(s_bw, 16)
                if a is not None:
                    if b is not None:
                        sp.wait_ge(s_qin, 2 * b + 1)
                        apart(sp)
                    sp.dma_start(xr[:, :, :], x_v[:, bass.ds(a, 1)]).then_inc(s_xr, 16)
                if a is None:
                    sp.wait_ge(s_const, 14)
                    sp.dma_start(slot_d.rearrange("(t p) a -> t (p a)", p=P), padf[:, :]).then_inc(s_slotld, 16)
                    sp.wait_ge(s_dfree, last_pass.start[1])
                    for s in range(SH):
                        if s:
                            sp.wait_ge(s_w, 64 * s)
                        rows = sw2[s * F:(s + 1) * F, :]
                        weights(sp, [(w1_r[:, s], sw1_v[:, s]), (w3_r[:, s], sw3_v[:, s]),
                                     (w2_r[:, s, 0:len(KF) - 1, :], rows[0:W2K, :].rearrange("(k p) d -> p k d", p=P)),
                                     (w2_r[0:F - W2K, s, len(KF) - 1, :], rows[W2K:F, :])])
                for x in steps:
                    if x == ("xt", C - 1):
                        at.let_go(sp, x)
                        apart(sp)
                        nxt = (a + 1) % B
                        sp.dma_start(xt[:, :, :], x_v[:, bass.ds(nxt, 1)]).then_inc(s_x, 16)
                    elif x[0] == "qk" and x[1] % 2:
                        g = x[1] // 2
                        i = g % 2
                        at.let_go(sp, x)
                        for t in (2 * g, 2 * g + 1):
                            sp.dma_start(scr_d[t].rearrange("v p s -> p v s"), qhl[:, t % 4].bitcast(F32)).then_inc(s_scr, 16)
                        sp.wait_ge(s_scr, a * (32 * C) + 32 * (g + 1))
                        apart(sp)
                        if g >= 2:
                            sp.wait_ge(s_st, a * HEADS + 4 * (g - 1))
                            apart(sp)
                        for t, stack, first, second in ((2 * g, qst, (0, 1), 0), (2 * g + 1, kst, (0, 0), 1)):
                            src = scr_d[t].rearrange("v (j r) s -> v r j s", r=HD)
                            for k, v in enumerate((*first, second)):
                                sp.dma_start(stack[HD * k:HD * (k + 1), i].bitcast(F32), src[v]).then_inc(s_stk[i], 16)
                    elif x[0] == "rows":
                        i = x[1] % 2
                        at.let_go(sp, x)
                        sp.dma_start(qst[96:97, i].bitcast(F32), nmh[:, i, :].bitcast(F32)).then_inc(s_mrow[i], 16)
                        sp.dma_start(qst[97:98, i].bitcast(F32), nml[:, i, :].bitcast(F32)).then_inc(s_mrow[i], 16)
                    elif x[0] == "ln2":
                        sp.wait_ge(s_x2, b + 1)
                        apart(sp)
                        sp.dma_start(x2_v[:, bass.ds(b, 1)], x1[:, :, :]).then_inc(s_x2st, 16)
            passes(sp, walk)
            sp.wait_ge(s_x, 16 * (B + 1))
            sp.wait_ge(s_x2st, 16 * B)

        @block.gpsimd
        def _(pool):
            n = [0]

            def fill(t, v):
                pool.memset(t, v).then_inc(s_pool_fill, 1)
                n[0] += 1

            def cut(t, pattern, base, mult, op, v):
                pool.affine_select(out=t, in_=t, compare_op=op, fill=v, base=base, pattern=pattern,
                                   channel_multiplier=mult).then_inc(s_const, 1)
            fill(ident[:, :], 0.0)
            fill(identb[:, :], 0.0)
            fill(ones[:, :], 1.0)
            fill(mask_qk[:, :], 0.0)
            fill(mask_kq[:, :], 0.0)
            fill(onehot[:, :, :], 0.0)
            fill(sel[:, :], 0.0)
            fill(tri16[:, :, :], 1.0)
            fill(tri4[:, :, :], 1.0)
            fill(upper[:, :], 1.0)
            fill(halfp[:, :], 0.5)
            fill(halfn[:, :], -0.5)
            pool.wait_ge(s_pool_fill, n[0])
            cut(ident[:, :], [[-1, P]], 0, 1, ALU.not_equal, 1.0)
            cut(identb[:, :], [[-1, P]], 0, 1, ALU.not_equal, 1.0)
            cut(mask_qk[:, :], [[-1, P]], 0, 1, ALU.is_ge, NEG)
            cut(mask_kq[:, :], [[1, P]], 0, -1, ALU.is_ge, NEG)
            cut(onehot[:, :, :], [[1, HEADS], [-1, 32]], 0, 0, ALU.not_equal, 1.0)
            cut(sel[:, :].rearrange("h (g r) -> h g r", r=HD), [[1, HEADS], [0, HD]], 0, -1, ALU.not_equal, 1.0)
            cut(tri16[:, :, :], [[1, E], [-1, E]], -1, 0, ALU.is_ge, 0.0)
            cut(tri4[:, :, :], [[1, 4], [-1, 4]], -1, 0, ALU.is_ge, 0.0)
            cut(upper[:, :], [[1, P]], -1, -1, ALU.is_ge, 0.0)
            for t, pat, base, mult in ((k128, [[0, E], [P, NT]], 0, 0), (jrow, [[1, RT], [0, 1]], 0, 0),
                                       (krow, [[1, TOPK], [0, E]], 0, 0), (tokf, [[P, NT], [T, TOPK]], 0, 1)):
                pool.iota(t[:, :, :], pat, base=base, channel_multiplier=mult,
                          allow_small_or_imprecise_dtypes=True).then_inc(s_const, 1)
            pool.iota(padf[:, :], [[1, P]], base=TOPK * T, channel_multiplier=P,
                      allow_small_or_imprecise_dtypes=True).then_inc(s_const, 1)
            pool.wait_ge(s_wload, 16 * 9)
            asked = [0]

            def power(b, width, half):
                pool.wait_ge(s_powin, 4 * b + asked[0] % 4 + 1)
                pool.tensor_tensor(small[:, 8:8 + width], small[:, 0:width], half[:, 0:width], ALU.pow).then_inc(s_pow, 1)
                asked[0] += 1

            def walk(steps, a, b, at):
                for x in steps:
                    if x[0] in ("ln1", "ln2"):
                        power(b, ST, halfn)
                    elif x[0] == "s":
                        power(b, C2 if x[1] else C, halfp)
                    elif x == ("rows", 1):
                        pool.wait_ge(s_xr, 16 * (a + 1))
                        for i in range(ST):
                            pool.tensor_tensor(xr[:, i, :], xr[:, i, :], bo_bc[:, :], ALU.add).then_inc(s_xrb, 1)
            passes(pool, walk)

        @block.scalar
        def _(act):
            act.wait_ge(s_wload, 16 * 9)

            def walk(steps, a, b, at):
                for x in steps:
                    if x[0] in BY_ACT:
                        act.wait_ge(s_rfull, at.ticket(x) + 1)
                        t, c = at.bank(x), x[-1]
                        if x[0] == "xt":
                            act.copy(xT[:, c, :], t).then_inc(s_afree, 1)
                        elif x[0] in ("wqt", "xqt"):
                            act.copy((wqT if x[0] == "wqt" else xqT)[:, c, :], t.bitcast(BF16)[:, 0:S]).then_inc(s_afree, 1)
                        elif x[0] == "x2t":
                            act.copy(x2T[:, c, :], t).then_inc(s_afree, 1)
                        elif x[0] == "lg":
                            act.copy(lgT[:, :], t[0:E, :]).then_inc(s_afree, 1)
                        else:
                            act.activation(score[:, bass.ds(b * ST, ST), :].rearrange("p n e -> p (n e)"), t[:, 0:ST * E],
                                           ACT.Sigmoid).then_inc(s_afree, 1)
                    elif x[0] == "qk":
                        n = x[1]
                        m = n // 2 + C * (n % 2)
                        act.wait_ge(s_rfull, at.ticket(x) + 1)
                        if n >= 4:
                            act.wait_ge(s_scr, a * (32 * C) + 32 * (n // 2 - 1))
                        act.activation(qhl[:, n % 4, 0, :], at.bank(x), ACT.Identity,
                                       bias=bqk[:, m:m + 1]).then_inc(s_qkhi, 1)
                    elif x[0] == "scores":
                        h = x[1]
                        act.wait_ge(s_st, a * HEADS + h + 1)
                        if h >= 2:
                            act.wait_ge(s_pv, a * HEADS + h - 1)
                        act.activation(pT[:, h % 2, :], psST[:, 0:PW], ACT.Exp, scale=SCALE).then_inc(s_exp, 1)
                    elif x[0] == "weigh" and x[1] % 4 == 3:
                        act.wait_ge(s_pv, a * HEADS + x[1] + 1)
                        act.copy(otu[:, x[1] // 4, :], psOT[:, :]).then_inc(s_ot, 1)
                    elif x[0] == "a2":
                        at.let_go(act, ("h", 0, ST - 1))
                        act.activation(gate_half, gate_half, ACT.Silu).then_inc(s_silu, 1)
            passes(act, walk)

        @block.tensor
        def _(pe):
            def product(out_, pairs):
                for n, (l, r) in enumerate(pairs):
                    mm = pe.matmul(out_, l, r, start=(n == 0), stop=(n == len(pairs) - 1))
                return mm

            pe.wait_ge(s_const, 14)
            pe.wait_ge(s_wload, 16 * 9)
            for c in range(C):
                mm = pe.transpose(psOT[:, c * E:(c + 1) * E], gw[:, c * P:(c + 1) * P], ident[0:E, 0:E])
            mm.then_inc(s_gw, 1)
            pe.wait_ge(s_gwT, 3)

            def walk(steps, a, b, at):
                def transposes(t, src, c, idn=ident):
                    for i in range(ST):
                        mm = pe.transpose(t[:, i * P:(i + 1) * P], src[:, i, c * P:(c + 1) * P], idn[:, :])
                    return mm

                group = {}
                for x in steps:
                    kind, n = x[0], (x[1] if len(x) > 1 else None)
                    c = x[2] if len(x) > 2 else None
                    if x == ("xt", 0):
                        pe.wait_ge(s_x, 16 * (a + 1))
                    elif x in (("qk", 0), ("h", 0, 0), ("h", 1, 0), ("wo", 0), ("lg",), ("lgt",)):
                        at.let_go(pe, {"qk": ("xt", C - 1), "h": ("xqt", n, (C2 if n else C) - 1), "wo": ("bc", C - 1),
                                       "lg": ("x2t", C - 1), "lgt": ("lg",)}[kind])
                        apart(pe)
                    elif x == ("wtr", 0, 0):
                        pe.wait_ge(s_bw, 32 * b + 32)
                    elif kind == "xtr" and c == 0:
                        pe.wait_ge(s_qin, 2 * b + n + 1)
                    elif kind in ("ws", "wb"):
                        pe.wait_ge(s_diag, 4 * b + 2 * n + 1 + (kind == "wb"))
                    elif kind in ("wqt", "xqt") and c == 0:
                        pe.wait_ge(s_quant, 4 * b + 2 * n + 1 + (kind == "xqt"))
                    elif x == ("x2t", 0):
                        pe.wait_ge(s_x2, b + 1)
                    elif kind == "max" and n % 4 == 0:
                        pe.wait_ge(s_stk[n // 4 % 2], 96 * (2 * a + n // 8 + 1))
                    elif kind == "scores" and n % 4 == 0:
                        pe.wait_ge(s_mrow[n // 4 % 2], 32 * (2 * a + n // 8 + 1))
                    elif x == ("bc", 0):
                        pe.wait_ge(s_rden, a + 1)
                    elif kind == "rows":
                        at.let_go(pe, ("max", 4 * n + 3), ST - 1)
                        apart(pe)
                    if kind in ONE:
                        t = at.take_bank(pe, x)
                    if kind in ("rows", "lgt"):
                        apart(pe)
                    if kind == "xt":
                        mm = transposes(t, xt, n)
                    elif kind == "qk":
                        m = n // 2 + C * (n % 2)
                        mm = product(t, [(wqkv[:, k, m * P:(m + 1) * P], xT[:, k, :]) for k in range(C)])
                    elif kind == "v":
                        mm = product(t, [(xT[:, k, n * P:(n + 1) * P], wqkv[:, k, 2 * D:3 * D]) for k in range(C)])
                    elif kind == "max":
                        i, j = n // 4 % 2, n % 4
                        for q in range(ST):
                            t = at.take_bank(pe, x, q)
                            w = max(2, q + 1) * P
                            pe.matmul(t[:, 0:w], qst[0:96, i, j, q * P:(q + 1) * P], kst[0:96, i, j, 0:w],
                                      start=True, stop=False)
                            pe.matmul(t[:, q * P:(q + 1) * P], identb[:, :], mask_qk[:, :], start=False,
                                      stop=True).then_inc(s_rfull, 1)
                    elif kind == "rows":
                        mm = pe.transpose(t[0:4 * ST, 0:P], nm[:, 4 * n:4 * n + 4, :].rearrange("p h q -> p (h q)"),
                                          ident[:, :])
                    elif kind == "scores":
                        i, j = n // 4 % 2, n % 4
                        if n:
                            pe.wait_ge(s_exp, a * HEADS + n)
                        for kb in (0, 3, 1, 2):
                            o, w = (KOFF[kb], S - kb * P) if kb < 3 else (KOFF[3] - P, 2 * P)
                            pe.matmul(psST[:, o:o + w], kst[0:98, i, j, kb * P:(kb + 1) * P], qst[0:98, i, j, S - w:S],
                                      start=True, stop=False)
                            mm = pe.matmul(psST[:, KOFF[kb]:KOFF[kb] + P], identb[:, :], mask_kq[:, :], start=False,
                                           stop=True)
                        mm.then_inc(s_st, 1)
                    elif kind == "weigh":
                        g, j = divmod(n, 4)
                        pe.wait_ge(s_exp, a * HEADS + n + 1)
                        if j == 0 and g:
                            pe.wait_ge(s_ot, a * C + g)
                        if n == 0:
                            at.let_go(pe, ("v", ST - 1))
                        for kb in range(ST):
                            p = pT[:, n % 2, KOFF[kb]:KOFF[kb] + S - kb * P]
                            pe.matmul(psOT[HD * j:HD * (j + 1), kb * P:S], v_s[:, kb, n * HD:(n + 1) * HD], p,
                                      start=(kb == 0), stop=(kb == ST - 1), skip_group_check=True)
                            mm = pe.matmul(psDEN[0:32, kb * P:S], onehot[:, n, :], p, start=(n == 0 and kb == 0),
                                           stop=(n == HEADS - 1 and kb == ST - 1), skip_group_check=True)
                        mm.then_inc(s_pv, 1)
                    elif kind == "bc":
                        mm = product(t, [(sel[:, n * P:(n + 1) * P], rden[:, :])])
                    elif kind == "wo":
                        mm = product(t, [(otu[:, k, n * P:(n + 1) * P], wo_s[:, k, :]) for k in range(C)])
                    elif kind == "wtr":
                        mm = transposes(t, wc if n else wf, c)
                    elif kind == "xtr":
                        mm = transposes(t, h1 if n else x1, c)
                    elif kind in ("ws", "xs"):
                        w = I2 if n else D
                        mm = product(t[:, 0:w], [(ones[:, :], dg[:, int(kind == "xs"), 0:w])])
                    elif kind == "wb":
                        mm = product(t, [(ones[:, :], dg[:, 0, :])])
                    elif kind in ("wqt", "xqt"):
                        mm = transposes(t.bitcast(BF16)[:, 0:S], xq, c, identb)
                    elif kind == "h":
                        mm = product(t, [(xqT[:, k, c * P:(c + 1) * P], wqT[:, k, :]) for k in range(C2 if n else C)])
                    elif kind == "x2t":
                        mm = transposes(t, x1, n)
                    elif kind == "lg":
                        mm = product(t[0:E, :], [(gwT[:, k, :], x2T[:, k, :]) for k in range(C)])
                    elif kind == "lgt":
                        for i in range(ST):
                            mm = pe.transpose(t[:, i * E:(i + 1) * E], lgT[:, i * P:(i + 1) * P], ident[0:E, 0:E])
                    if kind in ONE:
                        mm.then_inc(s_rfull, 1)
            passes(pe, walk)

        @block.vector
        def _(dve):
            for i in range(2):
                dve.memset(kst[96:98, i].bitcast(F32), 1.0).then_inc(s_gwT, 1)
            dve.wait_ge(s_wload, 16 * 9)
            dve.wait_ge(s_const, 14)
            dve.wait_ge(s_gw, 1)
            dve.tensor_copy(gwT[:, :, :], psOT[:, 0:C * E].rearrange("p (c e) -> p c e", c=C)).then_inc(s_gwT, 1)

            def walk(steps, a, b, at):
                k = [0]
                asked = [0]
                x = None

                def made(ins):
                    ins.then_inc(s_dve, 1)
                    k[0] += 1

                def after():
                    dve.wait_ge(s_dve, at.ordered(x) + k[0])

                def done(ins):
                    ins.then_inc(s_dfree, 1)

                def power():
                    asked[0] += 1
                    dve.wait_ge(s_pow, 4 * b + asked[0])

                def normalise(r, signal):
                    for i in range(ST):
                        made(dve.bn_stats(bn[:, i, :], r[:, i, :]))
                    after()
                    apart(dve)
                    for i in range(ST):
                        made(dve.bn_aggr(mv[:, i, :], bn[:, i, :]))
                    after()
                    dve.tensor_scalar(small[:, 0:ST], mv[:, :, 1], LN_EPS, None, ALU.add).then_inc(s_powin, 1)
                    power()
                    for i in range(ST):
                        ins = dve.tensor_scalar(x1[:, i, :], r[:, i, :], mv[:, i, 0:1], small[:, 8 + i:9 + i],
                                                ALU.subtract, ALU.mult)
                        if i < ST - 1:
                            made(ins)
                    ins.then_inc(signal, 1)

                def scaled(dst, src, t, m, sc, rc):
                    w = dst.shape[2]
                    done(dve.tensor_tensor(dst, src, t[:, 0:w].rearrange("p (a n) -> p a n", a=1).to_broadcast([P, ST, w]),
                                           ALU.mult))
                    dve.wait_ge(s_dfree, at.freed(x) + 1)
                    made(dve.tensor_reduce(m[:, :], dst, AX.X, ALU.max, apply_absolute_value=True))
                    after()
                    made(dve.tensor_scalar(sc[:, :], m[:, :], Q_EPS, 1.0 / QMAX, ALU.max, ALU.mult))
                    after()
                    return dve.reciprocal(rc[:, :], sc[:, :])

                def quantised(v, q, rc):
                    for i in range(ST):
                        made(dve.tensor_scalar(v[:, i, :], v[:, i, :], rc[:, i:i + 1], QMAX, ALU.mult, ALU.min))
                    after()
                    made(dve.tensor_scalar(v, v, -QMAX, ROUND, ALU.max, ALU.add))
                    after()
                    dve.tensor_scalar(q, v, -ROUND, None, ALU.add).then_inc(s_quant, 1)

                def link(ins):
                    made(ins)
                    after()

                def ranks(out_, val, tri, m, t1, t2):
                    link(dve.tensor_tensor(as4(t1, ST, m, m), mid(val, m), last(val, m), ALU.is_equal))
                    link(dve.tensor_tensor(as4(t1, ST, m, m), as4(t1, ST, m, m), front(tri, ST), ALU.mult))
                    link(dve.tensor_tensor(as4(t2, ST, m, m), mid(val, m), last(val, m), ALU.is_gt))
                    link(dve.tensor_tensor(as4(t1, ST, m, m), as4(t1, ST, m, m), as4(t2, ST, m, m), ALU.add))
                    link(dve.tensor_reduce(out_, as4(t1, ST, m, m), AX.X, ALU.add))

                def route(score_, rank_, chosen_, cwk_):
                    link(dve.tensor_tensor(biased[:, :, :], score_,
                                           ebias_bc[:, :].rearrange("p (o e) -> p o e", o=1).to_broadcast([P, ST, E]), ALU.add))
                    grouped = biased[:, :, :].rearrange("p n (g r) -> p (n g) r", g=4)
                    link(dve.tensor_reduce(gmax[:, :, :].rearrange("p n g -> p (n g)"), grouped, AX.X, ALU.max))
                    ranks(grank[:, :, :], gmax[:, :, :], tri4[:, :, :], 4, gpair, gpair2)
                    link(dve.tensor_scalar(grank[:, :, :], grank[:, :, :], 2.0, None, ALU.is_lt))
                    spread = grank[:, :, :].rearrange("p n (g o) -> p (n g) o", o=1).to_broadcast([P, ST * 4, 4])
                    link(dve.tensor_tensor(grouped, grouped, spread, ALU.mult))
                    link(dve.tensor_scalar(grank[:, :, :], grank[:, :, :], BIG, -BIG, ALU.mult, ALU.add))
                    link(dve.tensor_tensor(grouped, grouped, spread, ALU.add))
                    ranks(rank_, biased[:, :, :], tri16[:, :, :], E, epair, epair2)
                    link(dve.tensor_scalar(chosen_, rank_, float(TOPK), None, ALU.is_lt))
                    link(dve.tensor_tensor(cwt[:, :, :], chosen_, score_, ALU.mult))
                    link(dve.tensor_reduce(wsum[:, :], cwt[:, :, :], AX.X, ALU.add))
                    link(dve.reciprocal(wsum[:, :], wsum[:, :]))
                    link(dve.tensor_tensor(cwt[:, :, :], cwt[:, :, :],
                                           wsum[:, :].rearrange("p (n o) -> p n o", o=1).to_broadcast([P, ST, E]), ALU.mult))
                    link(dve.tensor_tensor(as4(epair, ST, TOPK, E), mid(rank_, TOPK), front(krow[:, :, :], ST), ALU.is_equal))
                    link(dve.tensor_tensor(as4(epair, ST, TOPK, E), as4(epair, ST, TOPK, E), mid(cwt[:, :, :], TOPK), ALU.mult))
                    link(dve.tensor_reduce(cwk_, as4(epair, ST, TOPK, E), AX.X, ALU.add))

                for x in steps:
                    kind, n = x[0], (x[1] if len(x) > 1 else None)
                    c = x[2] if len(x) > 2 else None
                    k[0] = 0
                    w, cn = (I2, C2) if n else (D, C)
                    if kind in BY_ACT:
                        continue
                    if kind in ONE:
                        dve.wait_ge(s_rfull, at.ticket(x) + 1)
                        t = at.bank(x)
                    if kind == "qk":
                        m = n // 2 + C * (n % 2)
                        dve.wait_ge(s_qkhi, a * 2 * C + n + 1)
                        done(dve.scalar_tensor_tensor(out=qhl[:, n % 4, 1, :], in0=t, scalar=bqk[:, m:m + 1],
                                                      in1=qhl[:, n % 4, 0, :].bitcast(F32), op0=ALU.add, op1=ALU.subtract))
                    elif kind == "v":
                        done(dve.tensor_tensor(v_s[:, n, :], t, bv_bc[:, :], ALU.add))
                    elif kind == "max":
                        for q in range(ST):
                            dve.wait_ge(s_rfull, at.ticket(x) + (q + 1))
                            done(dve.tensor_reduce(nm[:, n, q:q + 1], at.bank(x, q)[:, 0:(q + 1) * P], AX.X, ALU.max,
                                                   negate=True))
                    elif kind == "rows":
                        made(dve.tensor_copy(nmh[:, n % 2, :], t[0:4 * ST, 0:P]))
                        after()
                        done(dve.tensor_tensor(nml[:, n % 2, :], t[0:4 * ST, 0:P], nmh[:, n % 2, :].bitcast(F32),
                                               ALU.subtract))
                    elif kind == "weigh" and n == HEADS - 1:
                        dve.wait_ge(s_pv, a * HEADS + HEADS)
                        dve.reciprocal(rden[:, :], psDEN[0:HEADS, :]).then_inc(s_rden, 1)
                    elif kind == "bc":
                        dve.wait_ge(s_ot, a * C + C)
                        done(dve.tensor_tensor(otu[:, n, :], otu[:, n, :], t, ALU.mult))
                    elif kind == "wo":
                        dve.wait_ge(s_xrb, ST * (a + 1))
                        done(dve.tensor_tensor(xr[:, n, :], xr[:, n, :], t, ALU.add))
                    elif kind == "ln1":
                        dve.wait_ge(s_dfree, at.freed(x))
                        normalise(xr, s_qin)
                    elif kind in ("wtr", "xtr"):
                        am = amw if kind == "wtr" else amx
                        done(dve.tensor_reduce(am[:, c:c + 1], t, AX.X, ALU.max, apply_absolute_value=True))
                    elif kind == "s":
                        dve.wait_ge(s_dfree, at.freed(x))
                        made(dve.tensor_scalar(amw[:, 0:cn], amw[:, 0:cn], Q_EPS, None, ALU.max))
                        after()
                        made(dve.reciprocal(ram[:, 0:cn], amw[:, 0:cn]))
                        after()
                        dve.scalar_tensor_tensor(out=small[:, 0:cn], in0=amx[:, 0:cn], scalar=Q_EPS, in1=ram[:, 0:cn],
                                                 op0=ALU.max, op1=ALU.mult).then_inc(s_powin, 1)
                        dve.wait_ge(s_pow, 4 * b + n + 2)
                        made(dve.tensor_scalar(sm[:, 0:cn], small[:, 8:8 + cn], Q_EPS, None, ALU.max))
                        after()
                        made(dve.reciprocal(rsm[:, 0:cn], sm[:, 0:cn]))
                        after()
                        for i, f in enumerate((sm, rsm)):
                            for m in range(cn):
                                ins = dve.tensor_scalar(dg[:, i, m * P:(m + 1) * P], ident[:, :], f[:, m:m + 1], None,
                                                        ALU.mult)
                                if i == 0 or m < cn - 1:
                                    made(ins)
                        ins.then_inc(s_diag, 1)
                    elif kind == "ws":
                        made(scaled(xs[:, :, 0:w], wc[:, :, :] if n else wf[:, :, :], t, amw, wsc, rws))
                        for i in range(ST):
                            ins = dve.tensor_scalar(dg[:, 0, i * P:(i + 1) * P], ident[:, :], wsc[:, i:i + 1], None,
                                                    ALU.mult)
                            if i < ST - 1:
                                made(ins)
                        ins.then_inc(s_diag, 1)
                    elif kind == "wq":
                        dve.wait_ge(s_dve, at.ordered(x))
                        quantised(xs[:, :, 0:w], xq[:, :, 0:w], rws)
                    elif kind == "wb":
                        done(dve.tensor_copy(wsc_bc[:, :], t))
                    elif kind == "xs":
                        made(scaled(xs[:, :, 0:w], gate_half if n else x1[:, :, :], t, amx, xsc, rxs))
                    elif kind == "xq":
                        dve.wait_ge(s_dve, at.ordered(x))
                        apart(dve)
                        dve.wait_ge(s_rfull, at.ticket(("wqt", n, cn - 1)) + 1)
                        apart(dve)
                        quantised(xs[:, :, 0:w], xq[:, :, 0:w], rxs)
                    elif kind == "h":
                        done(dve.scalar_tensor_tensor(out=h1[:, c, :], in0=t, scalar=xsc[:, c:c + 1], in1=wsc_bc[:, :],
                                                      op0=ALU.mult, op1=ALU.mult))
                    elif kind == "a2":
                        dve.wait_ge(s_silu, b + 1)
                        dve.tensor_tensor(gate_half, gate_half, h1[:, :, I2:D], ALU.mult).then_inc(s_qin, 1)
                        dve.wait_ge(s_qin, 2 * b + 2)
                    elif kind == "ln2":
                        dve.wait_ge(s_dfree, at.freed(x))
                        made(dve.tensor_tensor(h1[:, :, :], h1[:, :, :], x1[:, :, :], ALU.add))
                        after()
                        asked[0] = 3
                        normalise(h1, s_x2)
                    elif kind == "route":
                        at.let_go(dve, ("lgt",))
                        apart(dve)
                        dve.wait_ge(s_x2st, 16 * b + 16)
                        apart(dve)
                        rows = bass.ds(b * ST, ST)
                        route(score[:, rows, :], rank[:, rows, :], chosen[:, rows, :], cwk[:, rows, :])
                    want = chain(x)
                    assert k[0] == want, (x, k[0], want)
            passes(dve, walk)
        blk.close()

        stA.close()
        psA.close()
        stR = ctx.enter_context(ExitStack())

        def se(name, shape, dt=F32):
            return sb(name, shape, dt, stR)

        NE = NT * E
        NK = NT * TOPK
        NKF = len(KF)
        xg = se("xg", [P, 2, D])
        xgT = se("xgT", [P, 2, 2, D], F32R)
        silg = se("silg", [P, F])
        hg = se("hg", [P, F])
        hgT = se("hgT", [P, 2, NKF * P], F32R)
        yg = se("yg", [P, 2, D])
        slot_T = se("slot_T", [RT, P])
        src_i = se("src_i", [P, RT], I32)
        dst_i = se("dst_i", [P, RT], I32)
        six = se("six", [P, 2, 1], I32)
        dix = se("dix", [P, 2, 1], I32)
        need_i = se("need_i", [1, RT], I32)
        buf_i = se("buf_i", [1, RT], I32)
        first_i = se("first_i", [1, RT], I32)
        NCB = TOPK + 1
        work = se("work", [P, 2 * NCB * D])
        CBS = 8
        WK = NT * TOPK * E
        wa, wb_ = work[:, 0:WK], work[:, WK:2 * WK]
        assert 2 * WK <= 2 * NCB * D and RT * E <= 2 * WK
        bn2 = se("bn2", [P, CBS, 6])
        mv2 = se("mv2", [P, CBS, 2])
        ve, rs2, nb = (se(n, [P, CBS]) for n in ("ve", "rs2", "nb"))
        pos = se("pos", [P, NT, E])
        offs = se("offs", [P, NT + 1, E])
        ntile = se("ntile", [P, E])
        base = se("base", [P, E])
        tend = se("tend", [P, E])
        posk = se("posk", [P, NT, TOPK])
        posk_i = se("posk_i", [P, NT, TOPK], I32)
        need_f = se("need_f", [P, RT])
        first_f = se("first_f", [P, RT])

        stW = ctx.enter_context(ExitStack())
        w1_s, w3_s = (sb(n, [P, 2, 2, C, F], F32R, stW) for n in ("w1_s", "w3_s"))
        w2_s = sb("w2_s", [P, 2, 2, NKF, D], F32R, stW)
        stW.close()
        work2 = se("work2", [P, (CBS - 2) * NCB * D])
        cb = [t.rearrange("p (a k d) -> p a k d", a=n, k=NCB)[:, i] for t, n in ((work, 2), (work2, CBS - 2)) for i in range(n)]

        psE = ctx.enter_context(ExitStack())
        psTX, psUA, psUB, psTH, psY0, psY1, psP, psQ = (
            psE.enter_context(nc.psum_tensor(n, [P, 512], F32))
            for n in ("psTX", "psUA", "psUB", "psTH", "psY0", "psY1", "psP", "psQ"))
        psY = [psY0, psY1]

        s_rt = sem("s_rt")
        s_cnt = sem("s_cnt")
        s_slots = sem("s_slots")
        s_slotT = sem("s_slotT")
        s_slotrd = sem("s_slotrd")
        s_tab = sem("s_tab")
        s_xs = [sem("s_xs0"), sem("s_xs1")]
        s_ys = [sem("s_ys0"), sem("s_ys1")]
        s_gat = [sem("s_gat0"), sem("s_gat1")]
        s_six = sem("s_six")
        s_dix = sem("s_dix")
        s_cc = sem("s_cc")
        NPLACE, NTABLE = 29, 9
        NCC = 2 * (TOPK + 2)
        assert NT % CBS == 0
        s_tx = sem("s_tx")
        s_xhi = sem("s_xhi")
        s_xe = sem("s_xe")
        s_ye = sem("s_ye")
        s_up = sem("s_up")
        s_sil = sem("s_sil")
        s_hm = sem("s_hm")
        s_th = sem("s_th")
        s_hhi = sem("s_hhi")
        s_ht = sem("s_ht")
        s_dn = sem("s_dn")
        s_whi = sem("s_whi")
        s_wlo = sem("s_wlo")
        s_w2lo = sem("s_w2lo")
        s_zero = sem("s_zero")
        s_sca = [sem("s_sca0"), sem("s_sca1")]
        s_cin = [sem(f"s_cin{q}") for q in range(CBS)]
        s_cv = sem("s_cv")
        s_cp = sem("s_cp")
        s_cy = sem("s_cy")
        s_cn = sem("s_cn")
        s_out = [sem(f"s_out{q}") for q in range(CBS)]
        w1_v = w1.rearrange("e (c p) f -> p e c f", p=P)
        w3_v = w3.rearrange("e (c p) f -> p e c f", p=P)
        y_v = y_d[0:TOPK * T, :].rearrange("(k n p) d -> p n k d", p=P, n=NT)
        sx_v = sx_d.rearrange("(n p) d -> p n d", p=P)
        xn_v = x2_d.rearrange("(n p) d -> p n d", p=P)
        o_v = out.rearrange("b (i p) d -> p (b i) d", p=P)
        NH = SH * NT

        LEAD, TRAIL = 6, 4

        def shared(eng, half, between=None):
            def tile_(n, par):
                if between and isinstance(n, int):
                    between(n)
                for s in range(SH):
                    half(n, s, par)
            for n in range(LEAD):
                tile_(n, n % 2)
            with eng.Fori(0, (NT - LEAD - TRAIL) // 2) as i:
                for k in range(2):
                    tile_(2 * i + (LEAD + k), (LEAD + k) % 2)
            for n in range(NT - TRAIL, NT):
                tile_(n, n % 2)

        HEAD, STEP = 3, 4
        TAIL = 3 + (RT - HEAD - 3) % STEP
        assert (TAIL + HEAD + RT) % 2 == 0 and STEP % 2 == 0 and NT % 2 == 0

        def tiles(eng, body):
            for j in range(HEAD):
                body(j, j % 2)
            with eng.Fori(0, (RT - HEAD - TAIL) // STEP) as i:
                for k in range(STEP):
                    body(STEP * i + (HEAD + k), (HEAD + k) % 2)
            for j in range(RT - TAIL, RT):
                body(j, j % 2)

        UP, DOWN = [0, 1], [2]

        def parts(buf):
            if isinstance(buf, int):
                pick = lambda t: t[:, buf:buf + 1]
            else:
                pick = lambda t: t[:, bass.ds(buf, 1)]
            return [(pick(raw).rearrange("p o a n -> p (o a n)"),
                     pick(split)[:, :, 0].rearrange("p o a n -> p (o a n)"),
                     pick(split)[:, :, 1].rearrange("p o a n -> p (o a n)"))
                    for raw, split in ((w1_r, w1_s), (w3_r, w3_s), (w2_r, w2_s))]

        def if_first(eng, j, split, which):
            with eng.If(eng.value_load(first_i[0:1, bass.ds(j, 1)], min_val=0, max_val=1)):
                e = eng.value_load(need_i[0:1, bass.ds(j, 1)], min_val=1, max_val=E + SH - 1)
                split(e, 1 - eng.value_load(buf_i[0:1, bass.ds(j, 1)], min_val=0, max_val=1), which)

        def is_first(j):
            return isinstance(j, int) and j == 0

        def is_last(j, n):
            return isinstance(j, int) and j == n - 1

        block2 = ctx.enter_context(nc.Block())

        @block2.sync
        def _(sp):
            def load_x(n, par):
                sp.dma_start(xg[:, par, :], xn_v[:, bass.ds(n, 1)]).then_inc(s_xs[par], 16)

            def expert(e, par):
                sp.wait_ge(s_wlo, 2 * (e + 1))
                apart(sp)
                sp.wait_ge(s_w2lo, e + 1)
                apart(sp)
                sp.wait_ge(s_w, 64 * (e + SH))
                apart(sp)
                weights(sp, [(w1_r[:, par], w1_v[:, bass.ds(e, 1)]), (w3_r[:, par], w3_v[:, bass.ds(e, 1)]),
                             (w2_r[:, par, 0:NKF - 1, :], w2[bass.ds(e, 1), 0:W2K, :].rearrange("e (k p) d -> p (e k) d", p=P)),
                             (w2_r[0:F - W2K, par, NKF - 1, :], w2[bass.ds(e, 1), W2K:F, :].rearrange("e p d -> p (e d)"))])

            load_x(0, 0)
            load_x(1, 1)
            expert(0, 0)
            expert(1, 1)

            def stored(n, par):
                sp.wait_ge(s_ye, n + 1)
                apart(sp)
                sp.dma_start(sx_v[:, bass.ds(n, 1)], yg[:, par, :]).then_inc(s_ys[par], 16)

            with sp.Fori(0, NT // 2 - 1) as i:
                for par in range(2):
                    stored(2 * i + par, par)
                    load_x(2 * i + (par + 2), par)
            for par in range(2):
                stored(NT - 2 + par, par)
            with sp.Fori(1, E // 2) as e2:
                for par in range(2):
                    expert(2 * e2 + par, par)
            for par in range(2):
                sp.wait_ge(s_sca[par], 8 * RT)
                sp.wait_ge(s_ys[par], 8 * NT)

            def load(n, q):
                sp.dma_start(cb[q][:, 0:TOPK, :], y_v[:, bass.ds(n, 1)]).then_inc(s_cin[q], 16)
                sp.dma_start(cb[q][:, TOPK, :], sx_v[:, bass.ds(n, 1)]).then_inc(s_cin[q], 16)

            def store(n, q):
                sp.wait_ge(s_cy, n + 1)
                apart(sp)
                sp.dma_start(o_v[:, bass.ds(n, 1)], cb[q][:, 0, :]).then_inc(s_out[q], 16)

            def again(i, q):
                sp.wait_ge(s_out[q], 16 * i + 16)
                apart(sp)
                load(CBS * i + (q + CBS), q)

            for q in range(CBS):
                load(q, q)
            with sp.Fori(0, NT // CBS - 1) as i:
                for q in range(CBS):
                    store(CBS * i + q, q)
                    if q:
                        again(i, q - 1)
                again(i, CBS - 1)
            for q in range(CBS):
                store(NT - CBS + q, q)
            for q in range(CBS):
                sp.wait_ge(s_out[q], 16 * NT // CBS)

        @block2.gpsimd
        def _(pool):
            pool.wait_ge(s_slotld, 16)
            pool.wait_ge(s_rt, NPLACE)
            for n in range(NT):
                for k in range(TOPK):
                    pool.indirect_dma_start(slot_d, bass.IndirectOffsetOnAxis(ap=posk_i[:, n, k:k + 1], axis=0),
                                            tokf[:, n, k:k + 1], None).then_inc(s_slots, 16)
            pool.wait_ge(s_slots, 16 * NK)
            pool.dma_start(slot_T[:, :], slot_d.rearrange("(t p) a -> t (p a)", p=P)).then_inc(s_slotrd, 16)
            pool.wait_ge(s_tab, 1)

            def gather(j, par):
                pool.tensor_copy(six[:, par, :], src_i[:, bass.ds(j, 1)]).then_inc(s_six, 1)
                pool.wait_ge(s_six, j + 1)
                apart(pool)
                pool.indirect_dma_start(xg[:, par, :], None, x2_d,
                                        bass.IndirectOffsetOnAxis(ap=six[:, par, :], axis=0)).then_inc(s_gat[par], 16)

            def scatter(j, par):
                pool.wait_ge(s_ye, j + (NT + 1))
                pool.tensor_copy(dix[:, par, :], dst_i[:, bass.ds(j, 1)]).then_inc(s_dix, 1)
                pool.wait_ge(s_dix, j + 1)
                apart(pool)
                pool.indirect_dma_start(y_d, bass.IndirectOffsetOnAxis(ap=dix[:, par, :], axis=0),
                                        yg[:, par, :], None).then_inc(s_sca[par], 16)

            def one(j, par):
                if not isinstance(j, int) or j + 2 < RT:
                    pool.wait_ge(s_tx, j + (NT + 1))
                    gather(j + 2, par)
                if not is_first(j):
                    scatter(j - 1, 1 - par)

            for j in range(2):
                pool.wait_ge(s_ye, NT - 1 + j)
                gather(j, j)
            tiles(pool, one)
            scatter(RT - 1, (RT - 1) % 2)
            with pool.Fori(0, NT // CBS) as i:
                for h in range(CBS // 2):
                    pool.wait_ge(s_cv, CBS * i + (2 * h + 2))
                    pool.tensor_tensor(rs2[:, 2 * h:2 * h + 2], ve[:, 2 * h:2 * h + 2], halfn[:, 0:2], ALU.pow).then_inc(s_cp, 1)

        @block2.scalar
        def _(act):
            def split(e, buf, which):
                act.wait_ge(s_w, e * 64 + 64)
                apart(act)
                for n in which:
                    raw, hi, lo = parts(buf)[n]
                    act.copy(hi, raw).then_inc(s_whi, 1)

            def high_x(n, par):
                act.wait_ge(s_tx, n + 1)
                act.copy(xgT[:, par, 0, :], psTX[:, :]).then_inc(s_xhi, 1)

            def gate(h):
                act.wait_ge(s_up, h + 1)
                act.activation(silg[:, :], psUA[:, 0:F], ACT.Silu).then_inc(s_sil, 1)

            def half(n, s, par):
                if is_last(n, NT) and s == SH - 1:
                    act.wait_ge(s_up, NH - 1)
                    split(SH, 0, UP)
                gate(SH * n + s)
                if s == SH - 1:
                    if is_last(n, NT):
                        act.wait_ge(s_tab, 1)
                    high_x(n + 1, 1 - par)
                if is_last(n, NT) and s == SH - 1:
                    act.wait_ge(s_dn, NH - 1)
                    split(SH, 0, DOWN)

            def one(j, par):
                if_first(act, j, split, UP)
                gate(j + NH)
                if not is_last(j, RT):
                    high_x(j + (NT + 1), 1 - par)
                if not is_first(j):
                    evacuate(j - 1, 1 - par)
                if is_first(j):
                    act.wait_ge(s_dn, NH)
                if_first(act, j, split, DOWN)

            def evacuate(j, par):
                act.wait_ge(s_dn, j + (NH + 1))
                if not isinstance(j, int) or j >= 2:
                    act.wait_ge(s_sca[par], 8 * (j - par))
                else:
                    act.wait_ge(s_ys[par], 8 * NT)
                act.copy(yg[:, par, :], psY[par][:, :]).then_inc(s_ye, 1)

            act.wait_ge(s_zero, 2)
            for s in range(SH):
                split(s, s, UP + DOWN)
                if s == 0:
                    high_x(0, 0)
            shared(act, half)
            tiles(act, one)
            evacuate(RT - 1, (RT - 1) % 2)

            with act.Fori(0, NT // CBS) as i:
                for q in range(CBS):
                    act.wait_ge(s_cn, CBS * i + (q + 1))
                    act.activation(cb[q][:, 0, :], cb[q][:, TOPK, :], ACT.Identity, scale=rs2[:, q:q + 1],
                                   bias=nb[:, q:q + 1]).then_inc(s_cy, 1)

        @block2.tensor
        def _(pe):
            SPLIT = [(0, 0), (1, 0), (0, 1)]

            pe.matmul(psP[:, 0:NE], upper[:, :], chosen[:, :, :].rearrange("p n e -> p (n e)"), start=True, stop=True)
            pe.matmul(psQ[:, 0:NE], ones[:, :], chosen[:, :, :].rearrange("p n e -> p (n e)"), start=True,
                      stop=True).then_inc(s_slotT, 1)

            def transposed(par):
                for c in range(C):
                    mm = pe.transpose(psTX[:, c * P:(c + 1) * P], xg[:, par, c * P:(c + 1) * P], ident[:, :])
                mm.then_inc(s_tx, 1)

            def loaded(n, par):
                pe.wait_ge(s_xs[par], 8 * (n - par) + 16)
                transposed(par)

            def gathered(j, par):
                pe.wait_ge(s_gat[par], 8 * (j - par) + 16)
                transposed(par)

            def up(par, buf):
                for t, w in ((psUA, w1_s), (psUB, w3_s)):
                    for c in range(C):
                        for n, (a_, b_) in enumerate(SPLIT):
                            mm = pe.matmul(t[:, 0:F], xgT[:, par, a_, c * P:(c + 1) * P], w[:, buf, b_, c, :],
                                           start=(c == 0 and n == 0), stop=(c == C - 1 and n == len(SPLIT) - 1))
                mm.then_inc(s_up, 1)

            def down(par, buf, first=True, last_=True):
                for k, (k0, kn) in enumerate(KF):
                    for n, (a_, b_) in enumerate(SPLIT):
                        mm = pe.matmul(psY[par][:, :], hgT[0:kn, a_, k * P:(k + 1) * P], w2_s[0:kn, buf, b_, k, :],
                                       start=(first and k == 0 and n == 0),
                                       stop=(last_ and k == NKF - 1 and n == len(SPLIT) - 1), skip_group_check=True)
                mm.then_inc(s_dn, 1)

            def turned(h):
                pe.wait_ge(s_hm, h + 1)
                for k, (k0, kn) in enumerate(KF):
                    mm = pe.transpose(psTH[0:kn, k * P:(k + 1) * P], hg[:, k0:k0 + kn], ident[:, :])
                mm.then_inc(s_th, 1)

            def down_shared(n, s, par):
                pe.wait_ge(s_ht, SH * n + (s + 1))
                if s == 0 and (not isinstance(n, int) or n >= 2):
                    pe.wait_ge(s_ye, n - 1)
                if isinstance(n, int) and n == 0:
                    pe.wait_ge(s_w2lo, s + 1)
                down(par, s, s == 0, s == SH - 1)

            def half(n, s, par):
                if s == 0:
                    pe.wait_ge(s_xe, n + 1)
                if isinstance(n, int) and n == 0:
                    pe.wait_ge(s_wlo, 2 * (s + 1))
                if not (is_first(n) and s == 0):
                    pe.wait_ge(s_hm, SH * n + s)
                up(par, s)
                if s == SH - 1 and not is_last(n, NT):
                    loaded(n + 1, 1 - par)
                if s == SH - 1 and is_last(n, NT):
                    gathered(0, 0)
                if s:
                    down_shared(n, s - 1, par)
                elif not is_first(n):
                    down_shared(n - 1, SH - 1, 1 - par)
                turned(SH * n + s)

            def between(n):
                if n == NT - 2:
                    pe.wait_ge(s_slotrd, 16)
                    pe.wait_ge(s_rt, NPLACE + NTABLE)
                    pe.transpose(psP[:, 0:RT], slot_T[:, :], ident[0:RT, 0:RT]).then_inc(s_slotT, 1)

            def down_routed(j, par):
                pe.wait_ge(s_ht, j + (NH + 1))
                pe.wait_ge(s_ye, j + (NT - 1))
                apart(pe)
                need = pe.value_load(need_i[0:1, bass.ds(j, 1)], min_val=1, max_val=E + SH)
                pe.wait_ge(s_w2lo, need)
                apart(pe)
                buf = pe.value_load(buf_i[0:1, bass.ds(j, 1)], min_val=0, max_val=1)
                down(par, bass.ds(buf, 1))

            def one(j, par):
                need = pe.value_load(need_i[0:1, bass.ds(j, 1)], min_val=1, max_val=E + SH)
                pe.wait_ge(s_wlo, need * 2)
                apart(pe)
                pe.wait_ge(s_xe, j + (NT + 1))
                apart(pe)
                buf = pe.value_load(buf_i[0:1, bass.ds(j, 1)], min_val=0, max_val=1)
                up(par, bass.ds(buf, 1))
                if is_first(j):
                    down_shared(NT - 1, SH - 1, 1 - par)
                if not is_last(j, RT):
                    gathered(j + 1, 1 - par)
                if not is_first(j):
                    down_routed(j - 1, 1 - par)
                turned(j + NH)

            loaded(0, 0)
            shared(pe, half, between)
            tiles(pe, one)
            down_routed(RT - 1, (RT - 1) % 2)

        @block2.vector
        def _(dve):
            step = [0]

            def link(ins):
                ins.then_inc(s_rt, 1)
                step[0] += 1
                dve.wait_ge(s_rt, step[0])

            def split(e, buf, which):
                for n in which:
                    raw, hi, lo = parts(buf)[n]
                    dve.wait_ge(s_whi, e * 3 + (n + 1))
                    apart(dve)
                    dve.tensor_tensor(lo, raw, hi.bitcast(F32), ALU.subtract).then_inc(s_wlo if n in UP else s_w2lo, 1)

            def totals():
                dve.wait_ge(s_slotT, 1)
                link(dve.memset(offs[:, 0, :], 0.0))
                tot = psQ[:, 0:NE].rearrange("p (n e) -> p n e", e=E)
                for n in range(NT):
                    link(dve.tensor_tensor(offs[:, n + 1, :], offs[:, n, :], tot[:, n, :], ALU.add))

            def places():
                cnt = offs[:, NT, :].rearrange("p (e o) -> p e o", o=1)
                pv = wa[:, 0:E * NT].rearrange("p (e k) -> p e k", e=E)
                link(dve.tensor_tensor(pv, cnt.to_broadcast([P, E, NT]), k128[:, :, :], ALU.is_gt))
                link(dve.tensor_reduce(ntile[:, :], pv, AX.X, ALU.add))
                link(dve.tensor_scalar(ntile[:, :], ntile[:, :], 1.0, None, ALU.max))
                pe2 = wa[:, 0:E * E].rearrange("p (e k) -> p e k", e=E)
                link(dve.tensor_tensor(pe2, ntile[:, :].rearrange("p (o e) -> p o e", o=1).to_broadcast([P, E, E]),
                                       tri16[:, :, :], ALU.mult))
                link(dve.tensor_reduce(base[:, :], pe2, AX.X, ALU.add))
                link(dve.tensor_tensor(tend[:, :], base[:, :], ntile[:, :], ALU.add))
                link(dve.tensor_tensor(pos[:, :, :], psP[:, 0:NE].rearrange("p (n e) -> p n e", e=E), offs[:, 0:NT, :], ALU.add))
                link(dve.scalar_tensor_tensor(out=pos[:, :, :], in0=base[:, :].rearrange("p (o e) -> p o e", o=1).to_broadcast([P, NT, E]),
                                              scalar=float(P), in1=pos[:, :, :], op0=ALU.mult, op1=ALU.add))

            def slots():
                isk = as4(wa, NT, TOPK, E)
                tmp = as4(wb_, NT, TOPK, E)
                link(dve.tensor_tensor(isk, mid(rank[:, :, :], TOPK), front(krow[:, :, :], NT), ALU.is_equal))
                link(dve.tensor_tensor(tmp, isk, mid(pos[:, :, :], TOPK), ALU.mult))
                link(dve.tensor_reduce(posk[:, :, :], tmp, AX.X, ALU.add))
                link(dve.tensor_copy(posk_i[:, :, :], posk[:, :, :]))
                assert step[0] == NPLACE, step[0]

            def owners():
                pj = work[:, 0:RT * E].rearrange("p (j e) -> p j e", e=E)
                link(dve.tensor_tensor(pj, tend[:, :].rearrange("p (o e) -> p o e", o=1).to_broadcast([P, RT, E]),
                                       jrow[:, :, :].to_broadcast([P, RT, E]), ALU.is_le))
                link(dve.tensor_reduce(need_f[:, :], pj, AX.X, ALU.add))
                link(dve.tensor_scalar(need_f[:, :], need_f[:, :], float(E - 1), float(SH + 1), ALU.min, ALU.add))
                link(dve.tensor_copy(need_i[:, :], need_f[0:1, :]))
                link(dve.memset(first_f[:, :], 1.0))
                link(dve.tensor_tensor(first_f[:, 1:RT], need_f[:, 1:RT], need_f[:, 0:RT - 1], ALU.is_gt))
                link(dve.scalar_tensor_tensor(out=first_f[:, :], in0=need_f[:, :], scalar=float(E + SH), in1=first_f[:, :],
                                              op0=ALU.is_lt, op1=ALU.mult))
                link(dve.tensor_copy(first_i[:, :], first_f[0:1, :]))
                link(dve.tensor_scalar(need_f[:, :], need_f[:, :], -1.0, None, ALU.add))
                assert step[0] == NPLACE + NTABLE, step[0]
                link(dve.tensor_copy(buf_i[:, :], need_f[0:1, :]))
                link(dve.tensor_scalar(buf_i[:, :], buf_i[:, :], 1, None, ALU.bitwise_and))

            def sources():
                dve.wait_ge(s_slotT, 2)
                link(dve.tensor_copy(dst_i[:, :], psP[:, 0:RT]))
                dve.tensor_scalar(src_i[:, :], dst_i[:, :], T - 1, None, ALU.bitwise_and).then_inc(s_tab, 1)

            def between(n):
                stage = {1: totals, 2: places, 3: slots, 4: owners, NT - 1: sources}.get(n)
                if stage:
                    stage()

            def low_x(n, par):
                dve.wait_ge(s_xhi, n + 1)
                dve.tensor_tensor(xgT[:, par, 1, :], psTX[:, :], xgT[:, par, 0, :].bitcast(F32),
                                  ALU.subtract).then_inc(s_xe, 1)

            def gated(h):
                dve.wait_ge(s_sil, h + 1)
                dve.tensor_tensor(hg[:, :], silg[:, :], psUB[:, 0:F], ALU.mult).then_inc(s_hm, 1)

            def turned(h):
                dve.wait_ge(s_th, h + 1)
                dve.tensor_copy(hgT[:, 0, :], psTH[:, 0:NKF * P]).then_inc(s_hhi, 1)
                dve.wait_ge(s_hhi, h + 1)
                dve.tensor_tensor(hgT[:, 1, :], psTH[:, 0:NKF * P], hgT[:, 0, :].bitcast(F32),
                                  ALU.subtract).then_inc(s_ht, 1)

            def summed(n, par):
                dve.wait_ge(s_dn, SH * n + SH)
                if not isinstance(n, int) or n >= 2:
                    dve.wait_ge(s_ys[par], 8 * (n - par))
                dve.tensor_tensor(yg[:, par, :], xg[:, par, :], psY[par][:, :], ALU.add).then_inc(s_ye, 1)

            def half(n, s, par):
                if is_last(n, NT) and s == SH - 1:
                    split(SH, 0, UP)
                gated(SH * n + s)
                if s == SH - 1:
                    low_x(n + 1, 1 - par)
                if s == 0 and not is_first(n):
                    summed(n - 1, 1 - par)
                turned(SH * n + s)
                if is_last(n, NT) and s == SH - 1:
                    split(SH, 0, DOWN)

            def one(j, par):
                if_first(dve, j, split, UP)
                gated(j + NH)
                if is_first(j):
                    summed(NT - 1, 1 - par)
                if not is_last(j, RT):
                    low_x(j + (NT + 1), 1 - par)
                turned(j + NH)
                if_first(dve, j, split, DOWN)

            dve.memset(psTH[:, :], 0.0).then_inc(s_zero, 1)
            dve.memset(w2_r[F - W2K:P, :, NKF - 1, :], 0.0).then_inc(s_zero, 1)
            split(0, 0, UP + DOWN)
            low_x(0, 0)
            split(1, 1, UP + DOWN)
            shared(dve, half, between)
            tiles(dve, one)
            def combine(i, h):
                def done(k):
                    dve.wait_ge(s_cc, i * (CBS // 2 * NCC) + (h * NCC + k))
                qs = (2 * h, 2 * h + 1)
                for k in range(TOPK):
                    for m, q in enumerate(qs):
                        if k == 0:
                            dve.wait_ge(s_cin[q], i * 32 + 32)
                        else:
                            done(2 * k + m - 1)
                        acc = cb[q][:, TOPK, :]
                        w = cwk[:, bass.ds(CBS * i + q, 1), k:k + 1].rearrange("p a b -> p (a b)")
                        dve.scalar_tensor_tensor(out=acc, in0=cb[q][:, k, :], scalar=w, in1=acc,
                                                 op0=ALU.mult, op1=ALU.add).then_inc(s_cc, 1)
                for m, q in enumerate(qs):
                    done(2 * TOPK + m - 1)
                    dve.bn_stats(bn2[:, q, :], cb[q][:, TOPK, :]).then_inc(s_cc, 1)
                for m, q in enumerate(qs):
                    done(2 * TOPK + 1 + m)
                    apart(dve)
                    dve.bn_aggr(mv2[:, q, :], bn2[:, q, :]).then_inc(s_cc, 1)
                for m, q in enumerate(qs):
                    done(2 * TOPK + 3 + m)
                    dve.tensor_scalar(ve[:, q:q + 1], mv2[:, q, 1:2], LN_EPS, None, ALU.add).then_inc(s_cv, 1)

            def centred(i, h):
                for q in (2 * h, 2 * h + 1):
                    dve.wait_ge(s_cp, CBS // 2 * i + (h + 1))
                    dve.scalar_tensor_tensor(out=nb[:, q:q + 1], in0=mv2[:, q, 0:1], scalar=-1.0, in1=rs2[:, q:q + 1],
                                             op0=ALU.mult, op1=ALU.mult).then_inc(s_cn, 1)

            def turn(i, before):
                for h in range(CBS // 2):
                    combine(i, h)
                    if h or before is not None:
                        centred(*((i, h - 1) if h else (before, CBS // 2 - 1)))
            turn(0, None)
            with dve.Fori(1, NT // CBS) as i:
                turn(i, i - 1)
            centred(NT // CBS - 1, CBS // 2 - 1)


_INS = ["x", "fside_BxS2xS2_0", "ctx_1024", "L0_attn_Wqkv", "L0_attn_bqkv", "L0_attn_Wo", "L0_attn_bo", "L0_ffn_gate_w",
        "L0_ffn_expert_bias", "L0_ffn_w1", "L0_ffn_w2", "L0_ffn_w3", "L0_ffn_sw1", "L0_ffn_sw2", "L0_ffn_sw3"]
_OUTS = [((4, 512, 512), "float32")]


def kernel(**inputs):
    import numpy as _np
    import concourse.bacc as _bacc
    from concourse import mybir as _mybir
    from concourse.bass_utils import run_bass_kernel_spmd as _run

    nc = _bacc.Bacc("TRN2", target_bir_lowering=False, num_devices=1)
    arrays, args = {}, []
    for name in _INS:
        a = _np.ascontiguousarray(inputs[name])
        arrays[f"in_{name}_dram"] = a
        args.append(nc.dram_tensor(f"in_{name}_dram", a.shape, _mybir.dt.from_np(a.dtype), kind="ExternalInput").ap())
    for i, (shape, dtype) in enumerate(_OUTS):
        dt = _mybir.dt.from_np(_np.dtype(dtype))
        args.append(nc.dram_tensor(f"out_{i}_dram", shape, dt, kind="ExternalOutput").ap())
    decoder_layer(nc, *args)
    r = _run(nc, [arrays], core_ids=[0])
    got = tuple(r.results[0][f"out_{i}_dram"] for i in range(len(_OUTS)))
    return got[0]
```

```python
from contextlib import ExitStack

import concourse.bass as bass
from concourse import mybir

F32 = mybir.dt.float32
F32R = mybir.dt.float32r
BF16 = mybir.dt.bfloat16
I32 = mybir.dt.int32
U32 = mybir.dt.uint32
ALU = mybir.AluOpType
ACT = mybir.ActivationFunctionType
AX = mybir.AxisListType

P = 128
HEADS = 16
HD = 32
LN_EPS = 1e-5
Q_EPS = 1e-6
QMAX = 127.0
ROUND = 12582912.0
NEG = -1e30
BIG = 1e30
NR = 3
TOPK = 4


def decoder_layer(nc, x, fside, ctxw, Wqkv, bqkv, Wo, bo, gate_w, ebias, w1, w2, w3, sw1, sw2, sw3, out):
    B, S, D = x.shape
    C = D // P
    ST = S // P
    I2 = ctxw.shape[2]
    C2 = I2 // P
    E, _, F = w1.shape
    NT = B * ST
    T = B * S
    KF = [(k * P, min(P, F - k * P)) for k in range((F + P - 1) // P)]
    SH = sw1.shape[1] // F
    SCALE = float(HD) ** -0.5
    PW = ST * S - P * ST * (ST - 1) // 2
    RT = (TOPK * T + (P - 1) * E) // P
    RT += RT % 2
    assert D == 512 and S == 512 and HEADS * HD == D and I2 == 256 and sw1.shape[1] == SH * F

    x2_d = nc.dram_tensor("x2_d", [T, D], F32).ap()
    slot_d = nc.dram_tensor("slot_d", [RT * P, 1], F32).ap()
    YPAD = TOPK * T
    y_d = nc.dram_tensor("y_d", [YPAD + RT * P, D], F32).ap()
    sx_d = nc.dram_tensor("sx_d", [T, D], F32).ap()

    with ExitStack() as ctx:
        def sb(name, shape, dt=F32, stack=ctx):
            return stack.enter_context(nc.sbuf_tensor(name, shape, dt))

        def sem(name):
            return ctx.enter_context(nc.semaphore(name))

        ident = sb("ident", [P, P])
        identb = sb("identb", [P, P], BF16)
        ones = sb("ones", [P, P])
        mask_qk = sb("mask_qk", [P, P], BF16)
        mask_kq = sb("mask_kq", [P, P], BF16)
        onehot = sb("onehot", [P, HEADS, 32])
        sel = sb("sel", [HEADS, D])
        tri16 = sb("tri16", [P, E, E])
        tri4 = sb("tri4", [P, 4, 4])
        upper = sb("upper", [P, P])
        k128 = sb("k128", [P, E, NT])
        jrow = sb("jrow", [P, RT, 1])
        krow = sb("krow", [P, TOPK, E])
        halfp = sb("halfp", [P, 8])
        halfn = sb("halfn", [P, 8])
        tokf = sb("tokf", [P, NT, TOPK])
        padf = sb("padf", [RT, P])
        score = sb("score", [P, NT, E])
        rank = sb("rank", [P, NT, E])
        chosen = sb("chosen", [P, NT, E])
        cwk = sb("cwk", [P, NT, TOPK])
        UPN, DNN = C * F, len(KF) * D
        WN = 2 * UPN + DNN
        room = sb("room", [P, max(2 * WN, 4 * C * D + D)])
        assert WN <= 3 * C * D
        raw = room[:, 0:2 * WN].rearrange("p (a n) -> p a n", a=2)
        w1_r = raw[:, :, 0:UPN].rearrange("p a (c n) -> p a c n", c=C)
        w3_r = raw[:, :, UPN:2 * UPN].rearrange("p a (c n) -> p a c n", c=C)
        w2_r = raw[:, :, 2 * UPN:WN].rearrange("p a (c n) -> p a c n", c=len(KF))
        ebias_bc = sb("ebias_bc", [P, E])

        psR = [ctx.enter_context(nc.psum_tensor(f"psR{i}", [P, 512], F32)) for i in range(NR)]
        psA = ctx.enter_context(ExitStack())
        psST = psA.enter_context(nc.psum_tensor("psST", [P, 3 * 512], F32))
        psOT = psA.enter_context(nc.psum_tensor("psOT", [P, 512], F32))
        psDEN = psA.enter_context(nc.psum_tensor("psDEN", [P, 512], F32))

        s_const = sem("s_const")
        s_apart = sem("s_apart")
        s_pool_fill = sem("s_pool_fill")
        s_wfirst = sem("s_wfirst")
        s_wqk = sem("s_wqk")
        s_wv = sem("s_wv")
        s_wlast = sem("s_wlast")
        s_gw = sem("s_gw")
        s_gwT = sem("s_gwT")
        s_x = sem("s_x")
        s_xr = sem("s_xr")
        s_bw = sem("s_bw")
        s_rfull = sem("s_rfull")
        s_dfree = sem("s_dfree")
        s_afree = sem("s_afree")
        s_dve = sem("s_dve")
        s_qkhi = sem("s_qkhi")
        s_scr = sem("s_scr")
        s_stk = [sem(f"s_stk{i}") for i in range(2)]
        s_mrow = [sem(f"s_mrow{i}") for i in range(2)]
        s_st = sem("s_st")
        s_exp = sem("s_exp")
        s_pv = sem("s_pv")
        s_ot = sem("s_ot")
        s_rden = sem("s_rden")
        s_xrb = sem("s_xrb")
        s_qin = sem("s_qin")
        s_diag = sem("s_diag")
        s_quant = sem("s_quant")
        s_powin = sem("s_powin")
        s_pow = sem("s_pow")
        s_silu = sem("s_silu")
        s_x2 = sem("s_x2")
        s_x2st = sem("s_x2st")

        MERGED = 8

        def quant_steps(n, cn):
            return ([("wtr", n, c) for c in range(cn)] + [("xtr", n, c) for c in range(cn)] + [("s", n)]
                    + [("ws", n), ("wq", n), ("wb", n)] + [("wqt", n, c) for c in range(cn)]
                    + [("xs", n), ("xq", n)] + [("xqt", n, c) for c in range(cn)] + [("h", n, i) for i in range(ST)])

        def merge(*lists):
            return [x for items in lists for x in items]

        b_steps = [("ln1",)] + quant_steps(0, C) + [("a2",)] + quant_steps(1, C2) + [("ln2",)] + [
            ("x2t", c) for c in range(C)] + [("lg",), ("lgt",), ("route",)]
        B_KINDS = {x[0] for x in b_steps}
        rest = list(b_steps)

        def take(n):
            out_ = rest[:n]
            del rest[:n]
            return out_

        def until(*x):
            return take(rest.index(x) + 1)

        def heads(*hs):
            return merge(*([("scores", h)] + [("weigh", h - 1)] * (h > 0) for h in hs))

        def each(kind, *ns):
            return [(kind, n) for n in ns]

        SEQ = merge(
            until("ln1"), each("xt", *range(C)), each("qk", 0, 1), until("wtr", 0, C - 1), each("qk", 2, 3),
            until("s", 0), each("v", 0), until("ws", 0), each("v", 1), until("wq", 0), each("v", 2), until("wb", 0),
            each("max", 0, 1, 2, 3), until("wqt", 0, C - 1), each("rows", 0), each("v", 3), heads(0), until("xs", 0), heads(1), until("xq", 0), heads(2), until("xqt", 0, C - 1),
            each("max", 4, 5, 6, 7), until("h", 0, 1), each("rows", 1), heads(3), until("a2"), heads(4), each("qk", 4), until("xtr", 1, C2 - 1), each("qk", 5), until("s", 1),
            heads(5, 6), until("ws", 1), heads(7), until("wq", 1), each("qk", 6), until("wb", 1), each("max", 8, 9, 10, 11), until("wqt", 1, C2 - 1),
            each("rows", 2), each("qk", 7), heads(8), until("xq", 1), heads(9), until("h", 1, ST - 1), heads(10), until("ln2"), heads(11),
            each("max", 12, 13, 14, 15), until("x2t", C - 1), each("rows", 3), until("lgt"), heads(12), until("route"), heads(13),
            heads(14, 15), each("weigh", 15), each("bc", *range(C)), each("wo", *range(ST)))
        assert not rest
        ONE = {"xt", "qk", "v", "rows", "bc", "wo", "wtr", "xtr", "ws", "wb", "wqt", "xs", "xqt", "h", "x2t", "lg", "lgt"}
        TICKS = {"max": ST, **dict.fromkeys(ONE, 1)}
        CHAIN = {"rows": 1, "ln1": 11, "ln2": 12, "s": None, "ws": ST + 2, "wq": ST + 1, "xs": 3, "xq": ST + 1,
                 "route": 24}

        BY_ACT = {"xt", "wqt", "xqt", "x2t", "lg", "lgt"}

        def chain(x):
            return {0: 3 + 2 * C, 1: 3 + 2 * C2}[x[1]] if x[0] == "s" else CHAIN.get(x[0], 0)

        def apart(eng):
            eng.sem_inc(s_apart, 1)

        class Pass:

            def __init__(self, steps, start):
                self.steps, self.start, self.where, self.holder = steps, start, {}, []
                n = [0, 0, 0, 0]
                for x in steps:
                    self.where[x] = tuple(n)
                    used = TICKS.get(x[0], 0)
                    self.holder += [(x, m) for m in range(used)]
                    n[0] += used
                    n[2 if x[0] in BY_ACT else 1] += used
                    n[3] += chain(x)
                self.count = tuple(n)

            def end(self, turns=1):
                return tuple(s_ + turns * c_ for s_, c_ in zip(self.start, self.count))

        class At:

            def __init__(self, p, turn):
                self.p, self.turn = p, turn

            def value(self, which, local):
                p = self.p
                if self.turn is None:
                    return p.start[which] + local
                return self.turn * p.count[which] + (p.start[which] + local)

            def ticket(self, x):
                return self.value(0, self.p.where[x][0])

            def freed(self, x):
                return self.value(1, self.p.where[x][1])

            def ordered(self, x):
                return self.value(3, self.p.where[x][3])

            def let_go(self, eng, x, more=0):
                if x[0] in BY_ACT:
                    eng.wait_ge(s_afree, self.value(2, self.p.where[x][2] + more + 1))
                else:
                    eng.wait_ge(s_dfree, self.value(1, self.p.where[x][1] + more + 1))

            def bank(self, x, more=0):
                return psR[(self.p.where[x][0] + more) % NR][:, :]

            def take_bank(self, pe, x, more=0):
                n = self.p.where[x][0] + more
                if n >= NR:
                    self.let_go(pe, *self.p.holder[n - NR])
                elif n == 0 and self.p.start[0]:
                    pe.wait_ge(s_dfree, self.value(1, 0))
                    apart(pe)
                    pe.wait_ge(s_afree, self.value(2, 0))
                return self.bank(x, more)

        A_ONLY = [x for x in SEQ if x[0] not in B_KINDS]
        first_pass = Pass(A_ONLY, (0, 0, 0, 0))
        both_pass = Pass(SEQ, first_pass.end())
        halves = [("half", n, s) for n in range(MERGED) for s in range(SH)]
        SHARED_AFTER = {
            ("ln1",): [("split", 0)], ("wtr", 0, C - 1): [("lead",)], ("s", 0): 1, ("ws", 0): 1, ("wb", 0): 1,
            ("xs", 0): 1, ("xq", 0): 1, ("h", 0, ST - 1): 1, ("s", 1): 1, ("ws", 1): 1, ("wb", 1): 1,
            ("xs", 1): 1, ("xq", 1): 1, ("h", 1, ST - 1): 1, ("ln2",): 2, ("lgt",): 1, ("route",): 1}
        ending = [("ready",)]
        for x_ in b_steps:
            ending.append(x_)
            extra = SHARED_AFTER.get(x_, 0)
            if isinstance(extra, int):
                extra, halves = halves[:extra], halves[extra:]
            ending += ([("split", 1)] if x_ == ("s", 0) else []) + extra
        assert not halves, halves
        last_pass = Pass(ending, both_pass.end(B - 1))

        def passes(eng, walk):
            walk(first_pass.steps, 0, None, At(first_pass, None))
            with eng.Fori(1, B) as i:
                walk(both_pass.steps, i, i - 1, At(both_pass, i - 1))
            walk(last_pass.steps, None, B - 1, At(last_pass, None))

        breg = sb("breg", [P, ST * D + ST * I2 + ST * D])
        wf = breg[:, 0:ST * D].rearrange("p (i d) -> p i d", i=ST)
        h1 = breg[:, ST * D:2 * ST * D].rearrange("p (i d) -> p i d", i=ST)
        wc = breg[:, 2 * ST * D:].rearrange("p (i d) -> p i d", i=ST)
        gwT = sb("gwT", [P, C, E])
        xr = sb("xr", [P, ST, D])
        x1 = sb("x1", [P, ST, D])
        dg = sb("dg", [P, 2, D])
        xs = sb("xs", [P, ST, D])
        xq = sb("xq", [P, ST, D], BF16)
        xqT = sb("xqT", [P, C, S], BF16)
        wqT = sb("wqT", [P, C, S], BF16)
        wsc_bc = sb("wsc_bc", [P, D])
        x2T = xs
        small = sb("small", [P, 16])
        biased = sb("biased", [P, ST, E])
        gmax = sb("gmax", [P, ST, 4])
        gpair = sb("gpair", [P, ST * 16])
        gpair2 = sb("gpair2", [P, ST * 16])
        grank = sb("grank", [P, ST, 4])
        cwt = sb("cwt", [P, ST, E])
        wsum = sb("wsum", [P, ST])
        epair = xs[:, 0:2, :].rearrange("p a n -> p (a n)")
        epair2 = xs[:, 2:4, :].rearrange("p a n -> p (a n)")
        amw, amx, ram, sm, rsm, wsc, rws, xsc, rxs = (sb(n, [P, 4]) for n in
                                                      ("amw", "amx", "ram", "sm", "rsm", "wsc", "rws", "xsc", "rxs"))
        bn = sb("bn", [P, ST, 6])
        mv = sb("mv", [P, ST, 2])
        gate_half = h1[:, :, 0:I2]
        gw = h1[0:E, 0, :]
        lgT = h1[0:E, 1, :]

        stA = ctx.enter_context(ExitStack())

        def sa(name, shape, dt=F32):
            return sb(name, shape, dt, stA)

        wqkv = room[:, 0:3 * C * D].rearrange("p (c n) -> p c n", c=C)
        wo_s = room[:, 3 * C * D:4 * C * D].rearrange("p (c n) -> p c n", c=C)
        bv_bc = room[:, 4 * C * D:4 * C * D + D]
        bqk = sa("bqk", [P, 2 * C])
        bo_bc = sa("bo_bc", [P, D])
        xt = sa("xt", [P, ST, D])
        xT = sa("xT", [P, C, S])
        v_s = sa("v_s", [P, ST, D])
        qhl = sa("qhl", [P, 4, 2, S], F32R)
        qst = sa("qst", [P, 2, 4, S], F32R)
        kst = sa("kst", [P, 2, 4, S], F32R)
        pT = sa("pT", [P, 2, PW])
        nm = sa("nm", [P, HEADS, ST])
        nmh = sa("nmh", [4 * ST, 2, P], F32R)
        nml = sa("nml", [4 * ST, 2, P], F32R)
        rden = sa("rden", [HEADS, S])
        otu = sa("otu", [P, C, S])

        scr_d = nc.dram_tensor("scr_d", [2 * C, 2, P, S], F32).ap()
        x_v = x.rearrange("b (i p) d -> p b i d", p=P)
        f_v = fside.rearrange("b (i p) d -> p b i d", p=P)
        c_v = ctxw.rearrange("b (i p) d -> p b i d", p=P)
        x2_v = x2_d.rearrange("(b i p) d -> p b i d", p=P, i=ST)
        wqkv_v = Wqkv.rearrange("(c p) n -> p c n", p=P)
        KOFF = [0, S, 2 * S, 2 * S - P]

        def mid(t, k):
            return t.rearrange("p a (o b) -> p a o b", o=1).to_broadcast([P, t.shape[1], k, t.shape[2]])

        def last(t, k):
            return t.rearrange("p a (b o) -> p a b o", o=1).to_broadcast([P, t.shape[1], t.shape[2], k])

        def front(t, n):
            return t.rearrange("p (o a) b -> p o a b", o=1).to_broadcast([P, n, t.shape[1], t.shape[2]])

        def as4(t, n, a, b):
            return t[:, 0:n * a * b].rearrange("p (n a b) -> p n a b", a=a, b=b)

        def bias_row(b, lo):
            return b[lo:lo + D].rearrange("(a n) -> a n", a=1).to_broadcast([P, D])

        s_w = sem("s_w")
        s_slotld = sem("s_slotld")
        sw1_v = sw1.rearrange("(c p) (s f) -> p s c f", p=P, f=F)
        sw3_v = sw3.rearrange("(c p) (s f) -> p s c f", p=P, f=F)
        W2K = (len(KF) - 1) * P

        def weights(sp, parts_):
            for dst, src_ in parts_:
                sp.dma_start(dst, src_).then_inc(s_w, 16)


        stA.close()
        psA.close()
        stR = ctx.enter_context(ExitStack())

        def se(name, shape, dt=F32):
            return sb(name, shape, dt, stR)

        NE = NT * E
        NK = NT * TOPK
        NKF = len(KF)
        xg = se("xg", [P, 2, D])
        xgT = se("xgT", [P, 2, 2, D], F32R)
        silg = se("silg", [P, F])
        hg = se("hg", [P, F])
        hgT = se("hgT", [P, 2, NKF * P], F32R)
        yg = se("yg", [P, 2, D])
        slot_T = se("slot_T", [RT, P])
        src_i = se("src_i", [P, RT + 1], I32)
        dst_i = se("dst_i", [P, RT], I32)
        six = se("six", [P, 2, 1], I32)
        dix = se("dix", [P, 2, 1], I32)
        need_i = se("need_i", [1, RT], I32)
        buf_i = se("buf_i", [1, RT], I32)
        first_i = se("first_i", [1, RT], I32)
        NCB = TOPK + 1
        work = breg
        CBS = 8
        WK = NT * TOPK * E
        wa, wb_ = work[:, 0:WK], work[:, WK:2 * WK]
        assert 2 * NCB * D <= 2 * ST * D + ST * I2 and 2 * WK <= 2 * ST * D and RT * E <= 2 * WK
        bn2 = se("bn2", [P, CBS, 6])
        mv2 = se("mv2", [P, CBS, 2])
        ve, rs2, nb = (se(n, [P, CBS]) for n in ("ve", "rs2", "nb"))
        pos = se("pos", [P, NT, E])
        offs = se("offs", [P, NT + 1, E])
        ntile = se("ntile", [P, E])
        base = se("base", [P, E])
        tend = se("tend", [P, E])
        posk = se("posk", [P, NT, TOPK])
        posk_i = se("posk_i", [P, NT, TOPK], I32)
        need_f = se("need_f", [P, RT])
        run_f = se("run_f", [P, 8])
        run_i = se("run_i", [1, 8], I32)
        runs_f = se("runs_f", [P, 1])
        fin_f = se("fin_f", [P, 2])
        fin_i = se("fin_i", [1, 2], I32)
        first_f = se("first_f", [P, RT])

        stW = ctx.enter_context(ExitStack())
        w1_s, w3_s = (sb(n, [P, 2, 2, C, F], F32R, stW) for n in ("w1_s", "w3_s"))
        w2_s = sb("w2_s", [P, 2, 2, NKF, D], F32R, stW)
        stW.close()
        work2 = se("work2", [P, (CBS - 2) * NCB * D])
        cb = [t.rearrange("p (a k d) -> p a k d", a=n, k=NCB)[:, i] for t, n in ((work, 2), (work2, CBS - 2)) for i in range(n)]

        psE = ctx.enter_context(ExitStack())
        psTX, psUA, psUB, psTH, psY0 = (
            psE.enter_context(nc.psum_tensor(n, [P, 512], F32)) for n in ("psTX", "psUA", "psUB", "psTH", "psY0"))
        psP, psQ, psY1 = psR
        psY = [psY0, psY1]

        s_rt = sem("s_rt")
        s_slots = sem("s_slots")
        s_slotT = sem("s_slotT")
        s_slotrd = sem("s_slotrd")
        s_tab = sem("s_tab")
        s_xs = [sem("s_xs0"), sem("s_xs1")]
        s_ys = [sem("s_ys0"), sem("s_ys1")]
        s_gat = [sem("s_gat0"), sem("s_gat1")]
        s_six = sem("s_six")
        s_dix = sem("s_dix")
        s_cc = sem("s_cc")
        NPLACE, NTABLE = 29, 9
        NCC = 2 * (TOPK + 2)
        assert NT % CBS == 0
        s_tx = sem("s_tx")
        s_xhi = sem("s_xhi")
        s_xe = sem("s_xe")
        s_ye = sem("s_ye")
        s_up = sem("s_up")
        s_sil = sem("s_sil")
        s_hm = sem("s_hm")
        s_th = sem("s_th")
        s_hhi = sem("s_hhi")
        s_ht = sem("s_ht")
        s_dn = sem("s_dn")
        s_whi = sem("s_whi")
        s_wlo = sem("s_wlo")
        s_w2lo = sem("s_w2lo")
        s_zero = sem("s_zero")
        s_keep = sem("s_keep")
        s_sca = [sem("s_sca0"), sem("s_sca1")]
        s_cin = [sem(f"s_cin{q}") for q in range(CBS)]
        s_cv = sem("s_cv")
        s_cp = sem("s_cp")
        s_cy = sem("s_cy")
        s_cn = sem("s_cn")
        s_out = [sem(f"s_out{q}") for q in range(CBS)]
        w1_v = w1.rearrange("e (c p) f -> p e c f", p=P)
        w3_v = w3.rearrange("e (c p) f -> p e c f", p=P)
        y_v = y_d[0:TOPK * T, :].rearrange("(k n p) d -> p n k d", p=P, n=NT)
        sx_v = sx_d.rearrange("(n p) d -> p n d", p=P)
        xn_v = x2_d.rearrange("(n p) d -> p n d", p=P)
        o_v = out.rearrange("b (i p) d -> p (b i) d", p=P)
        NH = SH * NT

        LEAD, TRAIL = MERGED + 2, 2
        assert (NT - LEAD - TRAIL) % 2 == 0 and MERGED % 2 == 0 and MERGED < (B - 1) * ST

        def shared(eng, half, between=None):
            def tile_(n, par):
                for s in range(SH):
                    if between and isinstance(n, int):
                        between(n, s)
                    half(n, s, par)
            for n in range(MERGED, LEAD):
                tile_(n, n % 2)
            with eng.Fori(0, (NT - LEAD - TRAIL) // 2) as i:
                for k in range(2):
                    tile_(2 * i + (LEAD + k), (LEAD + k) % 2)
            for n in range(NT - TRAIL, NT):
                tile_(n, n % 2)

        MUST = TOPK * T // P
        HEAD, STEP, GROUP = 3, 10, 4
        LOOPS = (MUST - HEAD) // STEP
        GSTART = HEAD + LOOPS * STEP
        NG = (RT - GSTART + GROUP - 1) // GROUP
        assert (TOPK * T + (P - 1) * E) // P < RT and GSTART <= MUST
        assert GSTART % 2 and STEP % 2 == 0 and GROUP % 2 == 0 and NT % 2 == 0 and GSTART + (NG - 1) * GROUP == RT - 1

        def runs(eng, g):
            return eng.If(eng.value_load(run_i[0:1, bass.ds(g, 1)], min_val=0, max_val=1))

        def tiles(eng, body):
            for j in range(HEAD):
                body(j, j % 2)
            with eng.Fori(0, LOOPS) as i:
                for k in range(STEP):
                    body(STEP * i + (HEAD + k), (HEAD + k) % 2)
            with eng.Fori(0, NG - 1) as g:
                with runs(eng, g):
                    for k in range(GROUP):
                        body(GROUP * g + (GSTART + k), (GSTART + k) % 2)
            with runs(eng, NG - 1):
                body(RT - 1, (RT - 1) % 2)

        UP, DOWN = [0, 1], [2]

        def parts(buf):
            if isinstance(buf, int):
                pick = lambda t: t[:, buf:buf + 1]
            else:
                pick = lambda t: t[:, bass.ds(buf, 1)]
            return [(pick(raw).rearrange("p o a n -> p (o a n)"),
                     pick(split)[:, :, 0].rearrange("p o a n -> p (o a n)"),
                     pick(split)[:, :, 1].rearrange("p o a n -> p (o a n)"))
                    for raw, split in ((w1_r, w1_s), (w3_r, w3_s), (w2_r, w2_s))]

        def if_first(eng, j, split, which):
            with eng.If(eng.value_load(first_i[0:1, bass.ds(j, 1)], min_val=0, max_val=1)):
                e = eng.value_load(need_i[0:1, bass.ds(j, 1)], min_val=1, max_val=E + SH - 1)
                split(e, 1 - eng.value_load(buf_i[0:1, bass.ds(j, 1)], min_val=0, max_val=1), which)

        def is_first(j):
            return isinstance(j, int) and j == 0

        def is_last(j, n):
            return isinstance(j, int) and j == n - 1

        def attention_over(eng):
            eng.wait_ge(s_dfree, last_pass.start[1])
            eng.wait_ge(s_x, 16 * (B + 1))

        block = ctx.enter_context(nc.Block())

        @block.sync
        def _(sp):
            def load_x(n, par):
                sp.dma_start(xg[:, par, :], xn_v[:, bass.ds(n, 1)]).then_inc(s_xs[par], 16)

            def expert(e, par):
                sp.wait_ge(s_wlo, 2 * (e + 1))
                apart(sp)
                sp.wait_ge(s_w2lo, e + 1)
                apart(sp)
                sp.wait_ge(s_w, 64 * (e + SH))
                apart(sp)
                weights(sp, [(w1_r[:, par], w1_v[:, bass.ds(e, 1)]), (w3_r[:, par], w3_v[:, bass.ds(e, 1)]),
                             (w2_r[:, par, 0:NKF - 1, :], w2[bass.ds(e, 1), 0:W2K, :].rearrange("e (k p) d -> p (e k) d", p=P)),
                             (w2_r[0:F - W2K, par, NKF - 1, :], w2[bass.ds(e, 1), W2K:F, :].rearrange("e p d -> p (e d)"))])

            def shared_expert(s):
                rows = sw2[s * F:(s + 1) * F, :]
                weights(sp, [(w1_r[:, s], sw1_v[:, s]), (w3_r[:, s], sw3_v[:, s]),
                             (w2_r[:, s, 0:NKF - 1, :], rows[0:W2K, :].rearrange("(k p) d -> p k d", p=P)),
                             (w2_r[0:F - W2K, s, NKF - 1, :], rows[W2K:F, :])])

            def stored(n, par):
                sp.wait_ge(s_ye, n + 1)
                apart(sp)
                sp.dma_start(sx_v[:, bass.ds(n, 1)], yg[:, par, :]).then_inc(s_ys[par], 16)

            def half(n, s, par):
                if s:
                    return
                if not is_first(n):
                    stored(n - 1, 1 - par)
                if not is_last(n, NT):
                    load_x(n + 1, 1 - par)
                if isinstance(n, int) and 2 <= n < 4:
                    expert(n - 2, par)

            def between(n, s):
                if (n, s) == (MERGED, 0):
                    sp.wait_ge(s_x2st, 16 * B)

            sp.dma_start(gw[:, :], gate_w).then_inc(s_wfirst, 16)
            with nc.allow_non_contiguous_dma(reason="a bias by rows, once"):
                sp.dma_start(bqk[:, :], bqkv[0:2 * D].rearrange("(c p) -> p c", p=P)).then_inc(s_wfirst, 16)
            sp.dma_start(xt[:, :, :], x_v[:, 0]).then_inc(s_x, 16)
            sp.dma_start(wqkv[:, :, 0:D], wqkv_v[:, :, 0:D]).then_inc(s_wqk, 16)
            sp.dma_start(wqkv[:, :, D:2 * D], wqkv_v[:, :, D:2 * D]).then_inc(s_wqk, 16)
            sp.dma_start(wqkv[:, :, 2 * D:3 * D], wqkv_v[:, :, 2 * D:3 * D]).then_inc(s_wv, 16)
            sp.dma_start(bv_bc[:, :], bias_row(bqkv, 2 * D)).then_inc(s_wv, 16)
            sp.dma_start(bo_bc[:, :], bias_row(bo, 0)).then_inc(s_wlast, 16)
            sp.dma_start(wo_s[:, :, :], Wo.rearrange("(c p) n -> p c n", p=P)).then_inc(s_wlast, 16)
            sp.dma_start(ebias_bc[:, :], ebias.rearrange("(a n) -> a n", a=1).to_broadcast([P, E])).then_inc(s_wlast, 16)

            def walk(steps, a, b, at):
                if b is not None:
                    sp.dma_start(wf[:, :, :], f_v[:, bass.ds(b, 1)]).then_inc(s_bw, 16)
                    sp.dma_start(wc[:, :, :], c_v[:, bass.ds(b, 1)]).then_inc(s_bw, 16)
                if a is not None:
                    if b is not None:
                        sp.wait_ge(s_qin, 2 * b + 1)
                        apart(sp)
                    sp.dma_start(xr[:, :, :], x_v[:, bass.ds(a, 1)]).then_inc(s_xr, 16)
                if a is None:
                    sp.wait_ge(s_const, 14)
                    sp.dma_start(slot_d.rearrange("(t p) a -> t (p a)", p=P), padf[:, :]).then_inc(s_slotld, 16)
                    At(both_pass, B - 2).let_go(sp, ("qk", 2 * C - 1))
                    shared_expert(0)
                for x in steps:
                    if x == ("xt", C - 1):
                        at.let_go(sp, x)
                        apart(sp)
                        nxt = (a + 1) % B
                        sp.dma_start(xt[:, :, :], x_v[:, bass.ds(nxt, 1)]).then_inc(s_x, 16)
                    elif x[0] == "qk" and x[1] % 2:
                        g = x[1] // 2
                        i = g % 2
                        at.let_go(sp, x)
                        for t in (2 * g, 2 * g + 1):
                            sp.dma_start(scr_d[t].rearrange("v p s -> p v s"), qhl[:, t % 4].bitcast(F32)).then_inc(s_scr, 16)
                        sp.wait_ge(s_scr, a * (32 * C) + 32 * (g + 1))
                        apart(sp)
                        if g >= 2:
                            sp.wait_ge(s_st, a * HEADS + 4 * (g - 1))
                            apart(sp)
                        for t, stack, first, second in ((2 * g, qst, (0, 1), 0), (2 * g + 1, kst, (0, 0), 1)):
                            src = scr_d[t].rearrange("v (j r) s -> v r j s", r=HD)
                            for k, v in enumerate((*first, second)):
                                sp.dma_start(stack[HD * k:HD * (k + 1), i].bitcast(F32), src[v]).then_inc(s_stk[i], 16)
                    elif x[0] == "rows":
                        i = x[1] % 2
                        at.let_go(sp, x)
                        sp.dma_start(qst[96:97, i].bitcast(F32), nmh[:, i, :].bitcast(F32)).then_inc(s_mrow[i], 16)
                        sp.dma_start(qst[97:98, i].bitcast(F32), nml[:, i, :].bitcast(F32)).then_inc(s_mrow[i], 16)
                    elif x == ("ready",):
                        attention_over(sp)
                        sp.wait_ge(s_x2st, 16 * (B - 1))
                        load_x(0, 0)
                    elif x == ("split", 0):
                        sp.wait_ge(s_w, 64)
                        shared_expert(1)
                    elif x[0] == "half":
                        half(x[1], x[2], x[1] % 2)
                    elif x[0] == "ln2":
                        sp.wait_ge(s_x2, b + 1)
                        apart(sp)
                        sp.dma_start(x2_v[:, bass.ds(b, 1)], x1[:, :, :]).then_inc(s_x2st, 16)
            passes(sp, walk)

            shared(sp, half, between)
            stored(NT - 1, (NT - 1) % 2)
            with sp.Fori(1, E // 2) as e2:
                for par in range(2):
                    expert(2 * e2 + par, par)
            for par in range(2):
                fin = sp.value_load(fin_i[0:1, par:par + 1], min_val=8 * (GSTART - 1), max_val=8 * RT)
                sp.wait_ge(s_sca[par], fin)
                apart(sp)
                sp.wait_ge(s_ys[par], 8 * NT)
                apart(sp)

            def load(n, q):
                sp.dma_start(cb[q][:, 0:TOPK, :], y_v[:, bass.ds(n, 1)]).then_inc(s_cin[q], 16)
                sp.dma_start(cb[q][:, TOPK, :], sx_v[:, bass.ds(n, 1)]).then_inc(s_cin[q], 16)

            def store(n, q):
                sp.wait_ge(s_cy, n + 1)
                apart(sp)
                sp.dma_start(o_v[:, bass.ds(n, 1)], cb[q][:, 0, :]).then_inc(s_out[q], 16)

            def again(i, q):
                sp.wait_ge(s_out[q], 16 * i + 16)
                apart(sp)
                load(CBS * i + (q + CBS), q)

            for q in range(CBS):
                load(q, q)
            with sp.Fori(0, NT // CBS - 1) as i:
                for q in range(CBS):
                    store(CBS * i + q, q)
                    if q:
                        again(i, q - 1)
                again(i, CBS - 1)
            for q in range(CBS):
                store(NT - CBS + q, q)
            for q in range(CBS):
                sp.wait_ge(s_out[q], 16 * NT // CBS)

        @block.gpsimd
        def _(pool):
            def split(e):
                for n, (raw_, hi, lo) in enumerate(parts(e)):
                    pool.wait_ge(s_whi, e * 3 + (n + 1))
                    pool.tensor_tensor(lo, raw_, hi.bitcast(F32), ALU.subtract).then_inc(s_wlo if n in UP else s_w2lo, 1)

            n = [0]

            def fill(t, v):
                pool.memset(t, v).then_inc(s_pool_fill, 1)
                n[0] += 1

            def cut(t, pattern, base, mult, op, v):
                pool.affine_select(out=t, in_=t, compare_op=op, fill=v, base=base, pattern=pattern,
                                   channel_multiplier=mult).then_inc(s_const, 1)
            fill(ident[:, :], 0.0)
            fill(identb[:, :], 0.0)
            fill(ones[:, :], 1.0)
            fill(mask_qk[:, :], 0.0)
            fill(mask_kq[:, :], 0.0)
            fill(onehot[:, :, :], 0.0)
            fill(sel[:, :], 0.0)
            fill(tri16[:, :, :], 1.0)
            fill(tri4[:, :, :], 1.0)
            fill(upper[:, :], 1.0)
            fill(halfp[:, :], 0.5)
            fill(halfn[:, :], -0.5)
            pool.wait_ge(s_pool_fill, n[0])
            cut(ident[:, :], [[-1, P]], 0, 1, ALU.not_equal, 1.0)
            cut(identb[:, :], [[-1, P]], 0, 1, ALU.not_equal, 1.0)
            cut(mask_qk[:, :], [[-1, P]], 0, 1, ALU.is_ge, NEG)
            cut(mask_kq[:, :], [[1, P]], 0, -1, ALU.is_ge, NEG)
            cut(onehot[:, :, :], [[1, HEADS], [-1, 32]], 0, 0, ALU.not_equal, 1.0)
            cut(sel[:, :].rearrange("h (g r) -> h g r", r=HD), [[1, HEADS], [0, HD]], 0, -1, ALU.not_equal, 1.0)
            cut(tri16[:, :, :], [[1, E], [-1, E]], -1, 0, ALU.is_ge, 0.0)
            cut(tri4[:, :, :], [[1, 4], [-1, 4]], -1, 0, ALU.is_ge, 0.0)
            cut(upper[:, :], [[1, P]], -1, -1, ALU.is_ge, 0.0)
            for t, pat, base, mult in ((k128, [[0, E], [P, NT]], 0, 0), (jrow, [[1, RT], [0, 1]], 0, 0),
                                       (krow, [[1, TOPK], [0, E]], 0, 0), (tokf, [[P, NT], [T, TOPK]], 0, 1)):
                pool.iota(t[:, :, :], pat, base=base, channel_multiplier=mult,
                          allow_small_or_imprecise_dtypes=True).then_inc(s_const, 1)
            pool.iota(padf[:, :], [[1, P]], base=TOPK * T, channel_multiplier=P,
                      allow_small_or_imprecise_dtypes=True).then_inc(s_const, 1)
            asked = [0]

            def power(b, width, half):
                pool.wait_ge(s_powin, 4 * b + asked[0] % 4 + 1)
                pool.tensor_tensor(small[:, 8:8 + width], small[:, 0:width], half[:, 0:width], ALU.pow).then_inc(s_pow, 1)
                asked[0] += 1

            def walk(steps, a, b, at):
                for x in steps:
                    if x[0] == "split":
                        split(x[1])
                    elif x[0] in ("ln1", "ln2"):
                        power(b, ST, halfn)
                    elif x[0] == "s":
                        power(b, C2 if x[1] else C, halfp)
                    elif x == ("rows", 1):
                        if b is None:
                            pool.wait_ge(s_wlast, 48)
                        pool.wait_ge(s_xr, 16 * (a + 1))
                        for i in range(ST):
                            pool.tensor_tensor(xr[:, i, :], xr[:, i, :], bo_bc[:, :], ALU.add).then_inc(s_xrb, 1)
            passes(pool, walk)

            pool.wait_ge(s_slotld, 16)
            pool.wait_ge(s_rt, NPLACE)
            for n in range(NT):
                for k in range(TOPK):
                    pool.indirect_dma_start(slot_d, bass.IndirectOffsetOnAxis(ap=posk_i[:, n, k:k + 1], axis=0),
                                            tokf[:, n, k:k + 1], None).then_inc(s_slots, 16)
            pool.wait_ge(s_slots, 16 * NK)
            pool.dma_start(slot_T[:, :], slot_d.rearrange("(t p) a -> t (p a)", p=P)).then_inc(s_slotrd, 16)
            pool.wait_ge(s_tab, 1)

            def gather(j, par):
                pool.tensor_copy(six[:, par, :], src_i[:, bass.ds(j, 1)]).then_inc(s_six, 1)
                pool.wait_ge(s_six, j + 1)
                apart(pool)
                pool.indirect_dma_start(xg[:, par, :], None, x2_d,
                                        bass.IndirectOffsetOnAxis(ap=six[:, par, :], axis=0)).then_inc(s_gat[par], 16)

            def scatter(j, par):
                pool.wait_ge(s_ye, j + (NT + 1))
                pool.tensor_copy(dix[:, par, :], dst_i[:, bass.ds(j, 1)]).then_inc(s_dix, 1)
                pool.wait_ge(s_dix, j + 1)
                apart(pool)
                pool.indirect_dma_start(y_d, bass.IndirectOffsetOnAxis(ap=dix[:, par, :], axis=0),
                                        yg[:, par, :], None).then_inc(s_sca[par], 16)

            def one(j, par):
                if not isinstance(j, int) or j + 2 < RT:
                    pool.wait_ge(s_tx, j + (NT + 1))
                    gather(j + 2, par)
                if not is_first(j):
                    scatter(j - 1, 1 - par)

            pool.wait_ge(s_ye, NT - 1)
            gather(0, 0)
            pool.wait_ge(s_keep, 1)
            gather(1, 1)
            tiles(pool, one)
            with pool.Fori(0, NT // CBS) as i:
                for h in range(CBS // 2):
                    pool.wait_ge(s_cv, CBS * i + (2 * h + 2))
                    pool.tensor_tensor(rs2[:, 2 * h:2 * h + 2], ve[:, 2 * h:2 * h + 2], halfn[:, 0:2], ALU.pow).then_inc(s_cp, 1)

        @block.scalar
        def _(act):
            def split(e, buf, which):
                act.wait_ge(s_w, e * 64 + 64)
                apart(act)
                for n in which:
                    raw, hi, lo = parts(buf)[n]
                    act.copy(hi, raw).then_inc(s_whi, 1)

            def high_x(n, par):
                act.wait_ge(s_tx, n + 1)
                act.copy(xgT[:, par, 0, :], psTX[:, :]).then_inc(s_xhi, 1)

            def gate(h):
                act.wait_ge(s_up, h + 1)
                act.activation(silg[:, :], psUA[:, 0:F], ACT.Silu).then_inc(s_sil, 1)

            def half(n, s, par):
                if is_last(n, NT) and s == SH - 1:
                    act.wait_ge(s_up, NH - 1)
                    split(SH, 0, UP)
                gate(SH * n + s)
                if is_last(n, NT) and s == 0:
                    act.wait_ge(s_ys[par], 8 * (n - par))
                    act.copy(yg[:, par, :], xg[:, par, :]).then_inc(s_keep, 1)
                if s == SH - 1:
                    if is_last(n, NT):
                        act.wait_ge(s_tab, 1)
                    high_x(n + 1, 1 - par)
                if is_last(n, NT) and s == SH - 1:
                    act.wait_ge(s_dn, NH - 1)
                    split(SH, 0, DOWN)

            def one(j, par):
                if_first(act, j, split, UP)
                gate(j + NH)
                if not is_last(j, RT):
                    high_x(j + (NT + 1), 1 - par)
                if not is_first(j):
                    evacuate(j - 1, 1 - par)
                if is_first(j):
                    act.wait_ge(s_dn, NH)
                if_first(act, j, split, DOWN)

            def evacuate(j, par):
                act.wait_ge(s_dn, j + (NH + 1))
                if not isinstance(j, int) or j >= 2:
                    act.wait_ge(s_sca[par], 8 * (j - par))
                else:
                    act.wait_ge(s_ys[par], 8 * NT)
                act.copy(yg[:, par, :], psY[par][:, :]).then_inc(s_ye, 1)

            act.wait_ge(s_wfirst, 32)

            def walk(steps, a, b, at):
                for x in steps:
                    if x[0] in BY_ACT:
                        act.wait_ge(s_rfull, at.ticket(x) + 1)
                        t, c = at.bank(x), x[-1]
                        if x[0] == "xt":
                            act.copy(xT[:, c, :], t).then_inc(s_afree, 1)
                        elif x[0] in ("wqt", "xqt"):
                            act.copy((wqT if x[0] == "wqt" else xqT)[:, c, :], t.bitcast(BF16)[:, 0:S]).then_inc(s_afree, 1)
                        elif x[0] == "x2t":
                            act.copy(x2T[:, c, :], t).then_inc(s_afree, 1)
                        elif x[0] == "lg":
                            act.copy(lgT[:, :], t[0:E, :]).then_inc(s_afree, 1)
                        else:
                            act.activation(score[:, bass.ds(b * ST, ST), :].rearrange("p n e -> p (n e)"), t[:, 0:ST * E],
                                           ACT.Sigmoid).then_inc(s_afree, 1)
                    elif x[0] == "qk":
                        n = x[1]
                        m = n // 2 + C * (n % 2)
                        act.wait_ge(s_rfull, at.ticket(x) + 1)
                        if n >= 4:
                            act.wait_ge(s_scr, a * (32 * C) + 32 * (n // 2 - 1))
                        act.activation(qhl[:, n % 4, 0, :], at.bank(x), ACT.Identity,
                                       bias=bqk[:, m:m + 1]).then_inc(s_qkhi, 1)
                    elif x[0] == "scores":
                        h = x[1]
                        act.wait_ge(s_st, a * HEADS + h + 1)
                        if h >= 2:
                            act.wait_ge(s_pv, a * HEADS + h - 1)
                        act.activation(pT[:, h % 2, :], psST[:, 0:PW], ACT.Exp, scale=SCALE).then_inc(s_exp, 1)
                    elif x[0] == "weigh" and x[1] % 4 == 3:
                        act.wait_ge(s_pv, a * HEADS + x[1] + 1)
                        act.copy(otu[:, x[1] // 4, :], psOT[:, :]).then_inc(s_ot, 1)
                    elif x == ("ready",):
                        attention_over(act)
                        act.wait_ge(s_zero, 2)
                    elif x[0] == "split":
                        split(x[1], x[1], UP + DOWN)
                    elif x == ("lead",):
                        high_x(0, 0)
                    elif x[0] == "half":
                        half(x[1], x[2], x[1] % 2)
                    elif x[0] == "a2":
                        at.let_go(act, ("h", 0, ST - 1))
                        act.activation(gate_half, gate_half, ACT.Silu).then_inc(s_silu, 1)
            passes(act, walk)

            shared(act, half)
            tiles(act, one)

            with act.Fori(0, NT // CBS) as i:
                for q in range(CBS):
                    act.wait_ge(s_cn, CBS * i + (q + 1))
                    act.activation(cb[q][:, 0, :], cb[q][:, TOPK, :], ACT.Identity, scale=rs2[:, q:q + 1],
                                   bias=nb[:, q:q + 1]).then_inc(s_cy, 1)

        @block.tensor
        def _(pe):
            SPLIT = [(0, 0), (1, 0), (0, 1)]

            def counts():
                pe.wait_ge(s_dve, last_pass.end()[3])
                pe.wait_ge(s_afree, last_pass.end()[2])
                pe.matmul(psP[:, 0:NE], upper[:, :], chosen[:, :, :].rearrange("p n e -> p (n e)"), start=True, stop=True)
                pe.matmul(psQ[:, 0:NE], ones[:, :], chosen[:, :, :].rearrange("p n e -> p (n e)"), start=True,
                          stop=True).then_inc(s_slotT, 1)

            def transposed(par):
                for c in range(C):
                    mm = pe.transpose(psTX[:, c * P:(c + 1) * P], xg[:, par, c * P:(c + 1) * P], ident[:, :])
                mm.then_inc(s_tx, 1)

            def loaded(n, par):
                pe.wait_ge(s_xs[par], 8 * (n - par) + 16)
                transposed(par)

            def gathered(j, par):
                pe.wait_ge(s_gat[par], 8 * (j - par) + 16)
                transposed(par)

            def up(par, buf):
                for t, w in ((psUA, w1_s), (psUB, w3_s)):
                    for c in range(C):
                        for n, (a_, b_) in enumerate(SPLIT):
                            mm = pe.matmul(t[:, 0:F], xgT[:, par, a_, c * P:(c + 1) * P], w[:, buf, b_, c, :],
                                           start=(c == 0 and n == 0), stop=(c == C - 1 and n == len(SPLIT) - 1))
                mm.then_inc(s_up, 1)

            def down(psy, buf, first=True, last_=True):
                for k, (k0, kn) in enumerate(KF):
                    for n, (a_, b_) in enumerate(SPLIT):
                        mm = pe.matmul(psy[:, :], hgT[0:kn, a_, k * P:(k + 1) * P], w2_s[0:kn, buf, b_, k, :],
                                       start=(first and k == 0 and n == 0),
                                       stop=(last_ and k == NKF - 1 and n == len(SPLIT) - 1), skip_group_check=True)
                mm.then_inc(s_dn, 1)

            def turned(h):
                pe.wait_ge(s_hm, h + 1)
                for k, (k0, kn) in enumerate(KF):
                    mm = pe.transpose(psTH[0:kn, k * P:(k + 1) * P], hg[:, k0:k0 + kn], ident[:, :])
                mm.then_inc(s_th, 1)

            def down_shared(n, s, par):
                pe.wait_ge(s_ht, SH * n + (s + 1))
                if s == 0 and not is_first(n):
                    pe.wait_ge(s_ye, n)
                if isinstance(n, int) and n == 0:
                    pe.wait_ge(s_w2lo, s + 1)
                down(psY[0], s, s == 0, s == SH - 1)

            def half(n, s, par):
                if s == 0:
                    pe.wait_ge(s_xe, n + 1)
                if isinstance(n, int) and n == 0:
                    pe.wait_ge(s_wlo, 2 * (s + 1))
                if not (is_first(n) and s == 0):
                    pe.wait_ge(s_hm, SH * n + s)
                up(par, s)
                if s == SH - 1 and not is_last(n, NT):
                    loaded(n + 1, 1 - par)
                if s == SH - 1 and is_last(n, NT):
                    gathered(0, 0)
                if s:
                    down_shared(n, s - 1, par)
                elif not is_first(n):
                    down_shared(n - 1, SH - 1, 1 - par)
                turned(SH * n + s)

            def between(n, s):
                if (n, s) == (MERGED, 1):
                    counts()
                if (n, s) == (NT - 1, 0):
                    pe.wait_ge(s_slotrd, 16)
                    pe.wait_ge(s_rt, NPLACE + NTABLE)
                    pe.transpose(psP[:, 0:RT], slot_T[:, :], ident[0:RT, 0:RT]).then_inc(s_slotT, 1)

            def registers(j):
                return (pe.value_load(need_i[0:1, bass.ds(j, 1)], min_val=1, max_val=E + SH),
                        pe.value_load(buf_i[0:1, bass.ds(j, 1)], min_val=0, max_val=1))

            def down_routed(j, par, regs):
                pe.wait_ge(s_ht, j + (NH + 1))
                pe.wait_ge(s_ye, NT if is_first(j) else j + (NT - 1))
                apart(pe)
                pe.wait_ge(s_w2lo, regs[0])
                down(psY[par], bass.ds(regs[1], 1))

            def one(j, par, before, regs, ahead=True):
                pe.wait_ge(s_wlo, regs[0] * 2)
                pe.wait_ge(s_xe, j + (NT + 1))
                up(par, bass.ds(regs[1], 1))
                if not is_last(j, RT):
                    gathered(j + 1, 1 - par)
                if is_first(j):
                    down_shared(NT - 1, SH - 1, 1 - par)
                after = registers(j + 1) if ahead else None
                if not is_first(j):
                    down_routed(j - 1, 1 - par, before)
                turned(j + NH)
                return after

            def routed():
                def span(start, par, n):
                    before, regs = registers(start - 1), registers(start)
                    for k in range(n):
                        before, regs = regs, one(start + k, (par + k) % 2, before, regs, k < n - 1)

                before, regs = None, registers(0)
                for j in range(HEAD):
                    before, regs = regs, one(j, j % 2, before, regs, j < HEAD - 1)
                with pe.Fori(0, LOOPS) as i:
                    span(STEP * i + HEAD, HEAD, STEP)
                with pe.Fori(0, NG - 1) as g:
                    with runs(pe, g):
                        span(GROUP * g + GSTART, GSTART, GROUP)
                with runs(pe, NG - 1):
                    one(RT - 1, (RT - 1) % 2, registers(RT - 2), registers(RT - 1), False)

            def product(out_, pairs):
                for n, (l, r) in enumerate(pairs):
                    mm = pe.matmul(out_, l, r, start=(n == 0), stop=(n == len(pairs) - 1))
                return mm

            pe.wait_ge(s_const, 14)
            pe.wait_ge(s_wfirst, 32)
            for c in range(C):
                mm = pe.transpose(psOT[:, c * E:(c + 1) * E], gw[:, c * P:(c + 1) * P], ident[0:E, 0:E])
            mm.then_inc(s_gw, 1)
            pe.wait_ge(s_gwT, 3)

            def walk(steps, a, b, at):
                def transposes(t, src, c, idn=ident):
                    for i in range(ST):
                        mm = pe.transpose(t[:, i * P:(i + 1) * P], src[:, i, c * P:(c + 1) * P], idn[:, :])
                    return mm

                group = {}
                for x in steps:
                    if x == ("ready",):
                        pe.wait_ge(s_zero, 2)
                    elif x == ("lead",):
                        loaded(0, 0)
                    elif x[0] == "half":
                        half(x[1], x[2], x[1] % 2)
                    if x[0] in ("ready", "lead", "half", "split"):
                        continue
                    kind, n = x[0], (x[1] if len(x) > 1 else None)
                    c = x[2] if len(x) > 2 else None
                    if b is None and x in (("qk", 0), ("v", 0), ("wo", 0)):
                        pe.wait_ge(*{"qk": (s_wqk, 32), "v": (s_wv, 32), "wo": (s_wlast, 48)}[kind])
                    if x == ("xt", 0):
                        pe.wait_ge(s_x, 16 * (a + 1))
                    elif x in (("qk", 0), ("h", 0, 0), ("h", 1, 0), ("wo", 0), ("lg",), ("lgt",)):
                        at.let_go(pe, {"qk": ("xt", C - 1), "h": ("xqt", n, (C2 if n else C) - 1), "wo": ("bc", C - 1),
                                       "lg": ("x2t", C - 1), "lgt": ("lg",)}[kind])
                        apart(pe)
                    elif x == ("wtr", 0, 0):
                        pe.wait_ge(s_bw, 32 * b + 32)
                    elif kind == "xtr" and c == 0:
                        pe.wait_ge(s_qin, 2 * b + n + 1)
                    elif kind in ("ws", "wb"):
                        pe.wait_ge(s_diag, 4 * b + 2 * n + 1 + (kind == "wb"))
                    elif kind in ("wqt", "xqt") and c == 0:
                        pe.wait_ge(s_quant, 4 * b + 2 * n + 1 + (kind == "xqt"))
                    elif x == ("x2t", 0):
                        pe.wait_ge(s_x2, b + 1)
                    elif kind == "max" and n % 4 == 0:
                        pe.wait_ge(s_stk[n // 4 % 2], 96 * (2 * a + n // 8 + 1))
                    elif kind == "scores" and n % 4 == 0:
                        pe.wait_ge(s_mrow[n // 4 % 2], 32 * (2 * a + n // 8 + 1))
                    elif x == ("bc", 0):
                        pe.wait_ge(s_rden, a + 1)
                    elif kind == "rows":
                        at.let_go(pe, ("max", 4 * n + 3), ST - 1)
                        apart(pe)
                    if kind in ONE:
                        t = at.take_bank(pe, x)
                    if kind in ("rows", "lgt"):
                        apart(pe)
                    if kind == "xt":
                        mm = transposes(t, xt, n)
                    elif kind == "qk":
                        m = n // 2 + C * (n % 2)
                        mm = product(t, [(wqkv[:, k, m * P:(m + 1) * P], xT[:, k, :]) for k in range(C)])
                    elif kind == "v":
                        mm = product(t, [(xT[:, k, n * P:(n + 1) * P], wqkv[:, k, 2 * D:3 * D]) for k in range(C)])
                    elif kind == "max":
                        i, j = n // 4 % 2, n % 4
                        for q in range(ST):
                            t = at.take_bank(pe, x, q)
                            w = max(2, q + 1) * P
                            pe.matmul(t[:, 0:w], qst[0:96, i, j, q * P:(q + 1) * P], kst[0:96, i, j, 0:w],
                                      start=True, stop=False)
                            pe.matmul(t[:, q * P:(q + 1) * P], identb[:, :], mask_qk[:, :], start=False,
                                      stop=True).then_inc(s_rfull, 1)
                    elif kind == "rows":
                        mm = pe.transpose(t[0:4 * ST, 0:P], nm[:, 4 * n:4 * n + 4, :].rearrange("p h q -> p (h q)"),
                                          ident[:, :])
                    elif kind == "scores":
                        i, j = n // 4 % 2, n % 4
                        if n:
                            pe.wait_ge(s_exp, a * HEADS + n)
                        for kb in (0, 3, 1, 2):
                            o, w = (KOFF[kb], S - kb * P) if kb < 3 else (KOFF[3] - P, 2 * P)
                            pe.matmul(psST[:, o:o + w], kst[0:98, i, j, kb * P:(kb + 1) * P], qst[0:98, i, j, S - w:S],
                                      start=True, stop=False)
                            mm = pe.matmul(psST[:, KOFF[kb]:KOFF[kb] + P], identb[:, :], mask_kq[:, :], start=False,
                                           stop=True)
                        mm.then_inc(s_st, 1)
                    elif kind == "weigh":
                        g, j = divmod(n, 4)
                        pe.wait_ge(s_exp, a * HEADS + n + 1)
                        if j == 0 and g:
                            pe.wait_ge(s_ot, a * C + g)
                        if n == 0:
                            at.let_go(pe, ("v", ST - 1))
                        for kb in range(ST):
                            p = pT[:, n % 2, KOFF[kb]:KOFF[kb] + S - kb * P]
                            pe.matmul(psOT[HD * j:HD * (j + 1), kb * P:S], v_s[:, kb, n * HD:(n + 1) * HD], p,
                                      start=(kb == 0), stop=(kb == ST - 1), skip_group_check=True)
                            mm = pe.matmul(psDEN[0:32, kb * P:S], onehot[:, n, :], p, start=(n == 0 and kb == 0),
                                           stop=(n == HEADS - 1 and kb == ST - 1), skip_group_check=True)
                        mm.then_inc(s_pv, 1)
                    elif kind == "bc":
                        mm = product(t, [(sel[:, n * P:(n + 1) * P], rden[:, :])])
                    elif kind == "wo":
                        mm = product(t, [(otu[:, k, n * P:(n + 1) * P], wo_s[:, k, :]) for k in range(C)])
                    elif kind == "wtr":
                        mm = transposes(t, wc if n else wf, c)
                    elif kind == "xtr":
                        mm = transposes(t, h1 if n else x1, c)
                    elif kind in ("ws", "xs"):
                        w = I2 if n else D
                        mm = product(t[:, 0:w], [(ones[:, :], dg[:, int(kind == "xs"), 0:w])])
                    elif kind == "wb":
                        mm = product(t, [(ones[:, :], dg[:, 0, :])])
                    elif kind in ("wqt", "xqt"):
                        mm = transposes(t.bitcast(BF16)[:, 0:S], xq, c, identb)
                    elif kind == "h":
                        mm = product(t, [(xqT[:, k, c * P:(c + 1) * P], wqT[:, k, :]) for k in range(C2 if n else C)])
                    elif kind == "x2t":
                        mm = transposes(t, x1, n)
                    elif kind == "lg":
                        mm = product(t[0:E, :], [(gwT[:, k, :], x2T[:, k, :]) for k in range(C)])
                    elif kind == "lgt":
                        for i in range(ST):
                            mm = pe.transpose(t[:, i * E:(i + 1) * E], lgT[:, i * P:(i + 1) * P], ident[0:E, 0:E])
                    if kind in ONE:
                        mm.then_inc(s_rfull, 1)
            passes(pe, walk)

            shared(pe, half, between)
            routed()

        @block.vector
        def _(dve):
            step = [0]

            def link(ins):
                ins.then_inc(s_rt, 1)
                step[0] += 1
                dve.wait_ge(s_rt, step[0])

            def split(e, buf, which):
                for n in which:
                    raw, hi, lo = parts(buf)[n]
                    dve.wait_ge(s_whi, e * 3 + (n + 1))
                    apart(dve)
                    dve.tensor_tensor(lo, raw, hi.bitcast(F32), ALU.subtract).then_inc(s_wlo if n in UP else s_w2lo, 1)

            def totals():
                dve.wait_ge(s_slotT, 1)
                link(dve.memset(offs[:, 0, :], 0.0))
                tot = psQ[:, 0:NE].rearrange("p (n e) -> p n e", e=E)
                for n in range(NT):
                    link(dve.tensor_tensor(offs[:, n + 1, :], offs[:, n, :], tot[:, n, :], ALU.add))

            def places():
                cnt = offs[:, NT, :].rearrange("p (e o) -> p e o", o=1)
                pv = wa[:, 0:E * NT].rearrange("p (e k) -> p e k", e=E)
                link(dve.tensor_tensor(pv, cnt.to_broadcast([P, E, NT]), k128[:, :, :], ALU.is_gt))
                link(dve.tensor_reduce(ntile[:, :], pv, AX.X, ALU.add))
                link(dve.tensor_scalar(ntile[:, :], ntile[:, :], 1.0, None, ALU.max))
                pe2 = wa[:, 0:E * E].rearrange("p (e k) -> p e k", e=E)
                link(dve.tensor_tensor(pe2, ntile[:, :].rearrange("p (o e) -> p o e", o=1).to_broadcast([P, E, E]),
                                       tri16[:, :, :], ALU.mult))
                link(dve.tensor_reduce(base[:, :], pe2, AX.X, ALU.add))
                link(dve.tensor_tensor(tend[:, :], base[:, :], ntile[:, :], ALU.add))
                link(dve.tensor_tensor(pos[:, :, :], psP[:, 0:NE].rearrange("p (n e) -> p n e", e=E), offs[:, 0:NT, :], ALU.add))
                link(dve.scalar_tensor_tensor(out=pos[:, :, :], in0=base[:, :].rearrange("p (o e) -> p o e", o=1).to_broadcast([P, NT, E]),
                                              scalar=float(P), in1=pos[:, :, :], op0=ALU.mult, op1=ALU.add))

            def slots():
                isk = as4(wa, NT, TOPK, E)
                tmp = as4(wb_, NT, TOPK, E)
                link(dve.tensor_tensor(isk, mid(rank[:, :, :], TOPK), front(krow[:, :, :], NT), ALU.is_equal))
                link(dve.tensor_tensor(tmp, isk, mid(pos[:, :, :], TOPK), ALU.mult))
                link(dve.tensor_reduce(posk[:, :, :], tmp, AX.X, ALU.add))
                link(dve.tensor_copy(posk_i[:, :, :], posk[:, :, :]))
                assert step[0] == NPLACE, step[0]

            def owners():
                pj = work[:, 0:RT * E].rearrange("p (j e) -> p j e", e=E)
                link(dve.tensor_tensor(pj, tend[:, :].rearrange("p (o e) -> p o e", o=1).to_broadcast([P, RT, E]),
                                       jrow[:, :, :].to_broadcast([P, RT, E]), ALU.is_le))
                link(dve.tensor_reduce(need_f[:, :], pj, AX.X, ALU.add))
                link(dve.tensor_scalar(need_f[:, :], need_f[:, :], float(E - 1), float(SH + 1), ALU.min, ALU.add))
                link(dve.tensor_copy(need_i[:, :], need_f[0:1, :]))
                link(dve.memset(first_f[:, :], 1.0))
                link(dve.tensor_tensor(first_f[:, 1:RT], need_f[:, 1:RT], need_f[:, 0:RT - 1], ALU.is_gt))
                link(dve.scalar_tensor_tensor(out=first_f[:, :], in0=need_f[:, :], scalar=float(E + SH), in1=first_f[:, :],
                                              op0=ALU.is_lt, op1=ALU.mult))
                link(dve.tensor_copy(first_i[:, :], first_f[0:1, :]))
                link(dve.tensor_scalar(need_f[:, :], need_f[:, :], -1.0, None, ALU.add))
                assert step[0] == NPLACE + NTABLE, step[0]
                link(dve.tensor_copy(buf_i[:, :], need_f[0:1, :]))
                link(dve.tensor_scalar(buf_i[:, :], buf_i[:, :], 1, None, ALU.bitwise_and))
                link(dve.tensor_tensor(run_f[:, 0:NG], jrow[:, GSTART:RT:GROUP, 0], tend[:, E - 1:E].to_broadcast([P, NG]),
                                       ALU.is_le))
                link(dve.tensor_copy(run_i[:, 0:NG], run_f[0:1, 0:NG]))
                link(dve.tensor_reduce(runs_f[:, :], run_f[:, 0:NG - 1], AX.X, ALU.add))
                link(dve.tensor_scalar(fin_f[:, 1:2], runs_f[:, :], float(8 * GROUP), float(8 * (GSTART - 1)), ALU.mult, ALU.add))
                link(dve.scalar_tensor_tensor(out=fin_f[:, 0:1], in0=run_f[:, NG - 1:NG], scalar=16.0, in1=fin_f[:, 1:2],
                                              op0=ALU.mult, op1=ALU.add))
                link(dve.tensor_copy(fin_i[:, :], fin_f[0:1, :]))
                link(dve.memset(src_i[:, RT:RT + 1], 0))

            def sources():
                dve.wait_ge(s_slotT, 2)
                link(dve.tensor_copy(dst_i[:, :], psP[:, 0:RT]))
                dve.tensor_scalar(src_i[:, 0:RT], dst_i[:, :], T - 1, None, ALU.bitwise_and).then_inc(s_tab, 1)

            def between(n, s):
                stage = {(MERGED, 1): totals, (MERGED + 1, 0): places, (MERGED + 1, 1): slots, (NT - 2, 0): owners,
                         (NT - 1, 0): sources}.get((n, s))
                if stage:
                    stage()

            def low_x(n, par):
                dve.wait_ge(s_xhi, n + 1)
                dve.tensor_tensor(xgT[:, par, 1, :], psTX[:, :], xgT[:, par, 0, :].bitcast(F32),
                                  ALU.subtract).then_inc(s_xe, 1)

            def gated(h):
                dve.wait_ge(s_sil, h + 1)
                dve.tensor_tensor(hg[:, :], silg[:, :], psUB[:, 0:F], ALU.mult).then_inc(s_hm, 1)

            def turned(h):
                dve.wait_ge(s_th, h + 1)
                dve.tensor_copy(hgT[:, 0, :], psTH[:, 0:NKF * P]).then_inc(s_hhi, 1)
                dve.wait_ge(s_hhi, h + 1)
                dve.tensor_tensor(hgT[:, 1, :], psTH[:, 0:NKF * P], hgT[:, 0, :].bitcast(F32),
                                  ALU.subtract).then_inc(s_ht, 1)

            def summed(n, par):
                dve.wait_ge(s_dn, SH * n + SH)
                if is_last(n, NT):
                    dve.wait_ge(s_keep, 1)
                elif not isinstance(n, int) or n >= 2:
                    dve.wait_ge(s_ys[par], 8 * (n - par))
                x_ = yg if is_last(n, NT) else xg
                dve.tensor_tensor(yg[:, par, :], x_[:, par, :], psY[0][:, :], ALU.add).then_inc(s_ye, 1)

            def half(n, s, par):
                if is_last(n, NT) and s == SH - 1:
                    split(SH, 0, UP)
                gated(SH * n + s)
                if s == SH - 1:
                    low_x(n + 1, 1 - par)
                if s == 0 and not is_first(n):
                    summed(n - 1, 1 - par)
                turned(SH * n + s)
                if is_last(n, NT) and s == SH - 1:
                    split(SH, 0, DOWN)

            def one(j, par):
                if_first(dve, j, split, UP)
                gated(j + NH)
                if not is_last(j, RT):
                    low_x(j + (NT + 1), 1 - par)
                if is_first(j):
                    summed(NT - 1, 1 - par)
                turned(j + NH)
                if_first(dve, j, split, DOWN)

            for i in range(2):
                dve.memset(kst[96:98, i].bitcast(F32), 1.0).then_inc(s_gwT, 1)
            dve.wait_ge(s_wfirst, 32)
            dve.wait_ge(s_const, 14)
            dve.wait_ge(s_gw, 1)
            dve.tensor_copy(gwT[:, :, :], psOT[:, 0:C * E].rearrange("p (c e) -> p c e", c=C)).then_inc(s_gwT, 1)

            def walk(steps, a, b, at):
                k = [0]
                asked = [0]
                x = None

                def made(ins):
                    ins.then_inc(s_dve, 1)
                    k[0] += 1

                def after():
                    dve.wait_ge(s_dve, at.ordered(x) + k[0])

                def done(ins):
                    ins.then_inc(s_dfree, 1)

                def power():
                    asked[0] += 1
                    dve.wait_ge(s_pow, 4 * b + asked[0])

                def normalise(r, signal):
                    for i in range(ST):
                        made(dve.bn_stats(bn[:, i, :], r[:, i, :]))
                    after()
                    apart(dve)
                    for i in range(ST):
                        made(dve.bn_aggr(mv[:, i, :], bn[:, i, :]))
                    after()
                    dve.tensor_scalar(small[:, 0:ST], mv[:, :, 1], LN_EPS, None, ALU.add).then_inc(s_powin, 1)
                    power()
                    for i in range(ST):
                        ins = dve.tensor_scalar(x1[:, i, :], r[:, i, :], mv[:, i, 0:1], small[:, 8 + i:9 + i],
                                                ALU.subtract, ALU.mult)
                        if i < ST - 1:
                            made(ins)
                    ins.then_inc(signal, 1)

                def scaled(dst, src, t, m, sc, rc):
                    w = dst.shape[2]
                    done(dve.tensor_tensor(dst, src, t[:, 0:w].rearrange("p (a n) -> p a n", a=1).to_broadcast([P, ST, w]),
                                           ALU.mult))
                    dve.wait_ge(s_dfree, at.freed(x) + 1)
                    made(dve.tensor_reduce(m[:, :], dst, AX.X, ALU.max, apply_absolute_value=True))
                    after()
                    made(dve.tensor_scalar(sc[:, :], m[:, :], Q_EPS, 1.0 / QMAX, ALU.max, ALU.mult))
                    after()
                    return dve.reciprocal(rc[:, :], sc[:, :])

                def quantised(v, q, rc):
                    for i in range(ST):
                        made(dve.tensor_scalar(v[:, i, :], v[:, i, :], rc[:, i:i + 1], QMAX, ALU.mult, ALU.min))
                    after()
                    made(dve.tensor_scalar(v, v, -QMAX, ROUND, ALU.max, ALU.add))
                    after()
                    dve.tensor_scalar(q, v, -ROUND, None, ALU.add).then_inc(s_quant, 1)

                def link(ins):
                    made(ins)
                    after()

                def ranks(out_, val, tri, m, t1, t2):
                    link(dve.tensor_tensor(as4(t1, ST, m, m), mid(val, m), last(val, m), ALU.is_equal))
                    link(dve.tensor_tensor(as4(t1, ST, m, m), as4(t1, ST, m, m), front(tri, ST), ALU.mult))
                    link(dve.tensor_tensor(as4(t2, ST, m, m), mid(val, m), last(val, m), ALU.is_gt))
                    link(dve.tensor_tensor(as4(t1, ST, m, m), as4(t1, ST, m, m), as4(t2, ST, m, m), ALU.add))
                    link(dve.tensor_reduce(out_, as4(t1, ST, m, m), AX.X, ALU.add))

                def route(score_, rank_, chosen_, cwk_):
                    link(dve.tensor_tensor(biased[:, :, :], score_,
                                           ebias_bc[:, :].rearrange("p (o e) -> p o e", o=1).to_broadcast([P, ST, E]), ALU.add))
                    grouped = biased[:, :, :].rearrange("p n (g r) -> p (n g) r", g=4)
                    link(dve.tensor_reduce(gmax[:, :, :].rearrange("p n g -> p (n g)"), grouped, AX.X, ALU.max))
                    ranks(grank[:, :, :], gmax[:, :, :], tri4[:, :, :], 4, gpair, gpair2)
                    link(dve.tensor_scalar(grank[:, :, :], grank[:, :, :], 2.0, None, ALU.is_lt))
                    spread = grank[:, :, :].rearrange("p n (g o) -> p (n g) o", o=1).to_broadcast([P, ST * 4, 4])
                    link(dve.tensor_tensor(grouped, grouped, spread, ALU.mult))
                    link(dve.tensor_scalar(grank[:, :, :], grank[:, :, :], BIG, -BIG, ALU.mult, ALU.add))
                    link(dve.tensor_tensor(grouped, grouped, spread, ALU.add))
                    ranks(rank_, biased[:, :, :], tri16[:, :, :], E, epair, epair2)
                    link(dve.tensor_scalar(chosen_, rank_, float(TOPK), None, ALU.is_lt))
                    link(dve.tensor_tensor(cwt[:, :, :], chosen_, score_, ALU.mult))
                    link(dve.tensor_reduce(wsum[:, :], cwt[:, :, :], AX.X, ALU.add))
                    link(dve.reciprocal(wsum[:, :], wsum[:, :]))
                    link(dve.tensor_tensor(cwt[:, :, :], cwt[:, :, :],
                                           wsum[:, :].rearrange("p (n o) -> p n o", o=1).to_broadcast([P, ST, E]), ALU.mult))
                    link(dve.tensor_tensor(as4(epair, ST, TOPK, E), mid(rank_, TOPK), front(krow[:, :, :], ST), ALU.is_equal))
                    link(dve.tensor_tensor(as4(epair, ST, TOPK, E), as4(epair, ST, TOPK, E), mid(cwt[:, :, :], TOPK), ALU.mult))
                    link(dve.tensor_reduce(cwk_, as4(epair, ST, TOPK, E), AX.X, ALU.add))

                for x in steps:
                    kind, n = x[0], (x[1] if len(x) > 1 else None)
                    c = x[2] if len(x) > 2 else None
                    k[0] = 0
                    w, cn = (I2, C2) if n else (D, C)
                    if kind == "ready":
                        attention_over(dve)
                        dve.memset(psTH[:, :], 0.0).then_inc(s_zero, 1)
                        dve.memset(w2_r[F - W2K:P, :, NKF - 1, :], 0.0).then_inc(s_zero, 1)
                    elif kind == "lead":
                        low_x(0, 0)
                    elif kind == "half":
                        half(x[1], x[2], x[1] % 2)
                    if kind in BY_ACT or kind in ("ready", "split", "lead", "half"):
                        continue
                    if kind in ONE:
                        dve.wait_ge(s_rfull, at.ticket(x) + 1)
                        t = at.bank(x)
                    if kind == "qk":
                        m = n // 2 + C * (n % 2)
                        dve.wait_ge(s_qkhi, a * 2 * C + n + 1)
                        done(dve.scalar_tensor_tensor(out=qhl[:, n % 4, 1, :], in0=t, scalar=bqk[:, m:m + 1],
                                                      in1=qhl[:, n % 4, 0, :].bitcast(F32), op0=ALU.add, op1=ALU.subtract))
                    elif kind == "v":
                        if b is None and n == 0:
                            dve.wait_ge(s_wv, 32)
                        done(dve.tensor_tensor(v_s[:, n, :], t, bv_bc[:, :], ALU.add))
                    elif kind == "max":
                        for q in range(ST):
                            dve.wait_ge(s_rfull, at.ticket(x) + (q + 1))
                            done(dve.tensor_reduce(nm[:, n, q:q + 1], at.bank(x, q)[:, 0:(q + 1) * P], AX.X, ALU.max,
                                                   negate=True))
                    elif kind == "rows":
                        made(dve.tensor_copy(nmh[:, n % 2, :], t[0:4 * ST, 0:P]))
                        after()
                        done(dve.tensor_tensor(nml[:, n % 2, :], t[0:4 * ST, 0:P], nmh[:, n % 2, :].bitcast(F32),
                                               ALU.subtract))
                    elif kind == "weigh" and n == HEADS - 1:
                        dve.wait_ge(s_pv, a * HEADS + HEADS)
                        dve.reciprocal(rden[:, :], psDEN[0:HEADS, :]).then_inc(s_rden, 1)
                    elif kind == "bc":
                        dve.wait_ge(s_ot, a * C + C)
                        done(dve.tensor_tensor(otu[:, n, :], otu[:, n, :], t, ALU.mult))
                    elif kind == "wo":
                        dve.wait_ge(s_xrb, ST * (a + 1))
                        done(dve.tensor_tensor(xr[:, n, :], xr[:, n, :], t, ALU.add))
                    elif kind == "ln1":
                        dve.wait_ge(s_dfree, at.freed(x))
                        normalise(xr, s_qin)
                    elif kind in ("wtr", "xtr"):
                        am = amw if kind == "wtr" else amx
                        done(dve.tensor_reduce(am[:, c:c + 1], t, AX.X, ALU.max, apply_absolute_value=True))
                    elif kind == "s":
                        dve.wait_ge(s_dfree, at.freed(x))
                        made(dve.tensor_scalar(amw[:, 0:cn], amw[:, 0:cn], Q_EPS, None, ALU.max))
                        after()
                        made(dve.reciprocal(ram[:, 0:cn], amw[:, 0:cn]))
                        after()
                        dve.scalar_tensor_tensor(out=small[:, 0:cn], in0=amx[:, 0:cn], scalar=Q_EPS, in1=ram[:, 0:cn],
                                                 op0=ALU.max, op1=ALU.mult).then_inc(s_powin, 1)
                        dve.wait_ge(s_pow, 4 * b + n + 2)
                        made(dve.tensor_scalar(sm[:, 0:cn], small[:, 8:8 + cn], Q_EPS, None, ALU.max))
                        after()
                        made(dve.reciprocal(rsm[:, 0:cn], sm[:, 0:cn]))
                        after()
                        for i, f in enumerate((sm, rsm)):
                            for m in range(cn):
                                ins = dve.tensor_scalar(dg[:, i, m * P:(m + 1) * P], ident[:, :], f[:, m:m + 1], None,
                                                        ALU.mult)
                                if i == 0 or m < cn - 1:
                                    made(ins)
                        ins.then_inc(s_diag, 1)
                    elif kind == "ws":
                        made(scaled(xs[:, :, 0:w], wc[:, :, :] if n else wf[:, :, :], t, amw, wsc, rws))
                        for i in range(ST):
                            ins = dve.tensor_scalar(dg[:, 0, i * P:(i + 1) * P], ident[:, :], wsc[:, i:i + 1], None,
                                                    ALU.mult)
                            if i < ST - 1:
                                made(ins)
                        ins.then_inc(s_diag, 1)
                    elif kind == "wq":
                        dve.wait_ge(s_dve, at.ordered(x))
                        quantised(xs[:, :, 0:w], xq[:, :, 0:w], rws)
                    elif kind == "wb":
                        done(dve.tensor_copy(wsc_bc[:, :], t))
                    elif kind == "xs":
                        made(scaled(xs[:, :, 0:w], gate_half if n else x1[:, :, :], t, amx, xsc, rxs))
                    elif kind == "xq":
                        dve.wait_ge(s_dve, at.ordered(x))
                        apart(dve)
                        dve.wait_ge(s_rfull, at.ticket(("wqt", n, cn - 1)) + 1)
                        apart(dve)
                        quantised(xs[:, :, 0:w], xq[:, :, 0:w], rxs)
                    elif kind == "h":
                        done(dve.scalar_tensor_tensor(out=h1[:, c, :], in0=t, scalar=xsc[:, c:c + 1], in1=wsc_bc[:, :],
                                                      op0=ALU.mult, op1=ALU.mult))
                    elif kind == "a2":
                        dve.wait_ge(s_silu, b + 1)
                        dve.tensor_tensor(gate_half, gate_half, h1[:, :, I2:D], ALU.mult).then_inc(s_qin, 1)
                        dve.wait_ge(s_qin, 2 * b + 2)
                    elif kind == "ln2":
                        dve.wait_ge(s_dfree, at.freed(x))
                        made(dve.tensor_tensor(h1[:, :, :], h1[:, :, :], x1[:, :, :], ALU.add))
                        after()
                        asked[0] = 3
                        normalise(h1, s_x2)
                    elif kind == "route":
                        at.let_go(dve, ("lgt",))
                        apart(dve)
                        dve.wait_ge(s_x2st, 16 * b + 16)
                        apart(dve)
                        rows = bass.ds(b * ST, ST)
                        dve.wait_ge(s_wlast, 48)
                        route(score[:, rows, :], rank[:, rows, :], chosen[:, rows, :], cwk[:, rows, :])
                    want = chain(x)
                    assert k[0] == want, (x, k[0], want)
            passes(dve, walk)

            shared(dve, half, between)
            tiles(dve, one)
            def combine(i, h):
                def done(k):
                    dve.wait_ge(s_cc, i * (CBS // 2 * NCC) + (h * NCC + k))
                qs = (2 * h, 2 * h + 1)
                for k in range(TOPK):
                    for m, q in enumerate(qs):
                        if k == 0:
                            dve.wait_ge(s_cin[q], i * 32 + 32)
                        else:
                            done(2 * k + m - 1)
                        acc = cb[q][:, TOPK, :]
                        w = cwk[:, bass.ds(CBS * i + q, 1), k:k + 1].rearrange("p a b -> p (a b)")
                        dve.scalar_tensor_tensor(out=acc, in0=cb[q][:, k, :], scalar=w, in1=acc,
                                                 op0=ALU.mult, op1=ALU.add).then_inc(s_cc, 1)
                for m, q in enumerate(qs):
                    done(2 * TOPK + m - 1)
                    dve.bn_stats(bn2[:, q, :], cb[q][:, TOPK, :]).then_inc(s_cc, 1)
                for m, q in enumerate(qs):
                    done(2 * TOPK + 1 + m)
                    apart(dve)
                    dve.bn_aggr(mv2[:, q, :], bn2[:, q, :]).then_inc(s_cc, 1)
                for m, q in enumerate(qs):
                    done(2 * TOPK + 3 + m)
                    dve.tensor_scalar(ve[:, q:q + 1], mv2[:, q, 1:2], LN_EPS, None, ALU.add).then_inc(s_cv, 1)

            def centred(i, h):
                for q in (2 * h, 2 * h + 1):
                    dve.wait_ge(s_cp, CBS // 2 * i + (h + 1))
                    dve.scalar_tensor_tensor(out=nb[:, q:q + 1], in0=mv2[:, q, 0:1], scalar=-1.0, in1=rs2[:, q:q + 1],
                                             op0=ALU.mult, op1=ALU.mult).then_inc(s_cn, 1)

            def turn(i, before):
                for h in range(CBS // 2):
                    combine(i, h)
                    if h or before is not None:
                        centred(*((i, h - 1) if h else (before, CBS // 2 - 1)))
            turn(0, None)
            with dve.Fori(1, NT // CBS) as i:
                turn(i, i - 1)
            centred(NT // CBS - 1, CBS // 2 - 1)


_INS = ["x", "fside_BxS2xS2_0", "ctx_1024", "L0_attn_Wqkv", "L0_attn_bqkv", "L0_attn_Wo", "L0_attn_bo", "L0_ffn_gate_w",
        "L0_ffn_expert_bias", "L0_ffn_w1", "L0_ffn_w2", "L0_ffn_w3", "L0_ffn_sw1", "L0_ffn_sw2", "L0_ffn_sw3"]
_OUTS = [((4, 512, 512), "float32")]


def kernel(**inputs):
    import numpy as _np
    import concourse.bacc as _bacc
    from concourse import mybir as _mybir
    from concourse.bass_utils import run_bass_kernel_spmd as _run

    nc = _bacc.Bacc("TRN2", target_bir_lowering=False, num_devices=1)
    arrays, args = {}, []
    for name in _INS:
        a = _np.ascontiguousarray(inputs[name])
        arrays[f"in_{name}_dram"] = a
        args.append(nc.dram_tensor(f"in_{name}_dram", a.shape, _mybir.dt.from_np(a.dtype), kind="ExternalInput").ap())
    for i, (shape, dtype) in enumerate(_OUTS):
        dt = _mybir.dt.from_np(_np.dtype(dtype))
        args.append(nc.dram_tensor(f"out_{i}_dram", shape, dt, kind="ExternalOutput").ap())
    decoder_layer(nc, *args)
    r = _run(nc, [arrays], core_ids=[0])
    got = tuple(r.results[0][f"out_{i}_dram"] for i in range(len(_OUTS)))
    return got[0]
```
